# Optimizing a Trainium2 kernel written in Bass

```python
import numpy as np
import jax
import jax.numpy as jnp

def _softmax(x, axis=-1):
    return jax.nn.softmax(x, axis=axis)

def _gelu(x):
    return jax.nn.gelu(x, approximate=True)

def _silu(x):
    return jax.nn.silu(x)

def _sigmoid(x):
    return jax.nn.sigmoid(x)

def _layernorm(x, axis=-1, eps=1e-05):
    m = jnp.mean(x, axis=axis, keepdims=True)
    v = jnp.var(x, axis=axis, keepdims=True)
    return (x - m) / jnp.sqrt(v + eps)

def _scatter_add(tgt, idx, src, axis=0):
    return tgt.at[idx].add(src)

def _segment_sum(src, seg, n):
    return jax.ops.segment_sum(src, seg, n)
kernel_name = 'mk_decoder_preln_d4_seqx_r8_42da43'

def setup_inputs(seed: int=0):
    np.random.seed(seed)
    _w = jnp.asarray

    def _rec_inputs():
        import jax
        import jax.numpy as jnp
        _rk = jax.random.key(seed)
        x = -0.0002928 + 1 * jax.random.normal(jax.random.fold_in(_rk, 1), (128, 64, 128), jnp.float32)
        _lenS = 64 - jax.random.randint(jax.random.fold_in(_rk, 7), (128,), 0, max(1, 64 // 4) + 1, jnp.int32)
        _lenS2 = 64 - jax.random.randint(jax.random.fold_in(_rk, 8), (128,), 0, max(1, 64 // 4) + 1, jnp.int32)
        _ctx_1024P = jax.random.normal(jax.random.fold_in(_rk, 11), (128, 16, 128), jnp.float32)
        _ctx_1024c = jax.random.dirichlet(jax.random.fold_in(_rk, 511), 0.3 * jnp.ones((16,), jnp.float32), (128, 64))
        _ctx_1024t = jnp.einsum('bsk,bkd->bsd', _ctx_1024c, _ctx_1024P)
        _ctx_1024t = _ctx_1024t * jax.lax.rsqrt(jnp.mean(jnp.square(_ctx_1024t)) + 1e-12) * 0.953939
        ctx_1024 = -1.39393e-06 + 0.999914 * (_ctx_1024t + 0.3 * jax.random.normal(jax.random.fold_in(_rk, 611), (128, 64, 128), jnp.float32))
        _validS = jnp.arange(64)[None, :] < _lenS[:, None]
        _validS2 = jnp.arange(64)[None, :] < _lenS2[:, None]
        _causal = jnp.tril(jnp.ones((64, 64), dtype=bool))
        mask_Bx1xSxS2_bf0 = jnp.logical_not(jnp.ones((128, 1, 64, 64), dtype=bool))
        return (x, ctx_1024, mask_Bx1xSxS2_bf0)
    x, ctx_1024, mask_Bx1xSxS2_bf0 = _rec_inputs()

    def _L0_attn_setup():
        import jax, jax.numpy as jnp
        import numpy as np
        DIM = 128
        HEADS = 16
        HEAD_DIM = DIM // HEADS
        RANK = 16
        LORA_ALPHA = 1
        SCALING = LORA_ALPHA / RANK
        SCALE = HEAD_DIM ** (-0.5)
        B, N = (8, 128)

        def _lora_linear(x, W, A, Blo, bias=None):
            y = x @ W.T + x @ A.T @ Blo.T * SCALING
            if bias is not None:
                y = y + bias
            return y

        def _split_heads(t, b, n):
            return t.reshape(b, n, HEADS, HEAD_DIM).transpose(0, 2, 1, 3)
        key = jax.random.key(seed)
        ks = jax.random.split(key, 15)
        s = 1.0 / np.sqrt(DIM)
        inp = {'x': jax.random.normal(ks[0], (B, N, DIM), jnp.float32), 'Wq': jax.random.normal(ks[1], (DIM, DIM), jnp.float32) * s, 'Wk': jax.random.normal(ks[2], (DIM, DIM), jnp.float32) * s, 'Wv': jax.random.normal(ks[3], (DIM, DIM), jnp.float32) * s, 'Wo': jax.random.normal(ks[4], (DIM, DIM), jnp.float32) * s, 'bo': jnp.zeros((DIM,), jnp.float32), 'Aq': jax.random.normal(ks[5], (RANK, DIM), jnp.float32) * s, 'Bq': jax.random.normal(ks[6], (DIM, RANK), jnp.float32) * s, 'Ak': jax.random.normal(ks[7], (RANK, DIM), jnp.float32) * s, 'Bk': jax.random.normal(ks[8], (DIM, RANK), jnp.float32) * s, 'Av': jax.random.normal(ks[9], (RANK, DIM), jnp.float32) * s, 'Bv': jax.random.normal(ks[10], (DIM, RANK), jnp.float32) * s, 'Ao': jax.random.normal(ks[11], (RANK, DIM), jnp.float32) * s, 'Bo': jax.random.normal(ks[12], (DIM, RANK), jnp.float32) * s}
        return inp
    _L0_attn_all = _L0_attn_setup()
    _L0_attn_in = {k: v for k, v in _L0_attn_all.items() if k in ('Wq', 'Wk', 'Wv', 'Wo', 'bo', 'Aq', 'Bq', 'Ak', 'Bk', 'Av', 'Bv', 'Ao', 'Bo')}
    del _L0_attn_all

    def _L0_xattn_setup():
        import jax, jax.numpy as jnp
        import numpy as np
        D_MODEL = 128
        NUM_HEADS = 16
        HEAD_DIM = D_MODEL // NUM_HEADS
        key = jax.random.key(seed)
        ks = jax.random.split(key, 11)
        B, S = (2, 256)
        inp = {'query': jax.random.normal(ks[0], (B, S, D_MODEL), jnp.float32), 'key': jax.random.normal(ks[1], (B, S, D_MODEL), jnp.float32), 'value': jax.random.normal(ks[2], (B, S, D_MODEL), jnp.float32), 'mask': 1, 'w_q': jax.random.normal(ks[3], (D_MODEL, D_MODEL), jnp.float32) / np.sqrt(D_MODEL), 'b_q': jax.random.normal(ks[4], (D_MODEL,), jnp.float32) * 0.02, 'w_k': jax.random.normal(ks[5], (D_MODEL, D_MODEL), jnp.float32) / np.sqrt(D_MODEL), 'b_k': jax.random.normal(ks[6], (D_MODEL,), jnp.float32) * 0.02, 'w_v': jax.random.normal(ks[7], (D_MODEL, D_MODEL), jnp.float32) / np.sqrt(D_MODEL), 'b_v': jax.random.normal(ks[8], (D_MODEL,), jnp.float32) * 0.02, 'w_o': jax.random.normal(ks[9], (D_MODEL, D_MODEL), jnp.float32) / np.sqrt(D_MODEL), 'b_o': jax.random.normal(ks[10], (D_MODEL,), jnp.float32) * 0.02}
        return inp
    _L0_xattn_all = _L0_xattn_setup()
    _L0_xattn_in = {k: v for k, v in _L0_xattn_all.items() if k in ('w_q', 'b_q', 'w_k', 'b_k', 'w_v', 'b_v', 'w_o', 'b_o')}
    del _L0_xattn_all

    def _L0_ffn_setup():
        import jax, jax.numpy as jnp
        import numpy as np
        E, K, NG, TG = (64, 8, 8, 4)
        CAP = 128
        SCALE = 2.5

        def _route(x_flat, gate_weight, e_bias):
            T = x_flat.shape[0]
            logits = x_flat.astype(jnp.float32) @ gate_weight.astype(jnp.float32).T
            scores = jax.nn.sigmoid(logits)
            sfc = scores + e_bias[None, :]
            group_scores = jax.lax.top_k(sfc.reshape(T, NG, E // NG), 2)[0].sum(-1)
            _, gidx = jax.lax.top_k(group_scores, TG)
            gmask = jnp.zeros((T, NG), jnp.float32).at[jnp.arange(T)[:, None], gidx].set(1.0)
            smask = jnp.repeat(gmask, E // NG, axis=1)
            tmp = jnp.where(smask > 0, sfc, 0.0)
            _, topk_idx = jax.lax.top_k(tmp, K)
            topk_w = jnp.take_along_axis(scores, topk_idx, axis=1)
            topk_w = topk_w / (topk_w.sum(-1, keepdims=True) + 1e-20)
            return (topk_idx, topk_w * SCALE)

        def _moe_forward(hidden_states, gate_weight, e_bias, w1, w2, w3, shared_gate, shared_up, shared_down):
            B, S, H = hidden_states.shape
            T = B * S
            x = hidden_states.reshape(T, H)
            topk_idx, topk_w = _route(x, gate_weight, e_bias)
            Sk = T * K
            flat_e = topk_idx.reshape(-1)
            order = jnp.argsort(flat_e)
            sorted_e = flat_e[order]
            counts = jax.ops.segment_sum(jnp.ones((Sk,), jnp.int32), flat_e, num_segments=E)
            offsets = jnp.cumsum(counts) - counts
            pos = jnp.arange(Sk) - offsets[sorted_e]
            tok_sorted = x[order // K]
            xe = jnp.zeros((E, CAP, H), x.dtype).at[sorted_e, pos].set(tok_sorted, mode='drop')
            h = jax.nn.silu(jnp.einsum('ech,efh->ecf', xe, w1)) * jnp.einsum('ech,efh->ecf', xe, w3)
            ye = jnp.einsum('ecf,ehf->ech', h, w2)
            pos_c = jnp.minimum(pos, CAP - 1)
            vals = ye[sorted_e, pos_c]
            vals = jnp.where((pos < CAP)[:, None], vals, 0.0)
            flat_w = topk_w.reshape(-1)[order].astype(vals.dtype)
            flat_t = (jnp.arange(Sk) // K)[order]
            out = jax.ops.segment_sum(vals * flat_w[:, None], flat_t, num_segments=T)
            shared = jax.nn.silu(x @ shared_gate.T) * (x @ shared_up.T) @ shared_down.T
            return (out + shared).reshape(B, S, H)
        key = jax.random.key(seed)
        ks = jax.random.split(key, 9)
        B, S, H, F = (1, 256, 128, 64)
        bound = 1.0 / 32.0
        return {'hidden_states': jax.random.normal(ks[0], (B, S, H), jnp.float32), 'gate_weight': jax.random.uniform(ks[1], (E, H), jnp.float32, -bound, bound), 'e_bias': jnp.zeros((E,), jnp.float32), 'w1': jax.random.normal(ks[2], (E, F, H), jnp.float32) * 0.02, 'w2': jax.random.normal(ks[3], (E, H, F), jnp.float32) * 0.02, 'w3': jax.random.normal(ks[4], (E, F, H), jnp.float32) * 0.02, 'shared_gate': jax.random.normal(ks[5], (2 * F, H), jnp.float32) * 0.02, 'shared_up': jax.random.normal(ks[6], (2 * F, H), jnp.float32) * 0.02, 'shared_down': jax.random.normal(ks[7], (H, 2 * F), jnp.float32) * 0.02}
    _L0_ffn_all = _L0_ffn_setup()
    _L0_ffn_in = {k: v for k, v in _L0_ffn_all.items() if k in ('gate_weight', 'e_bias', 'w1', 'w2', 'w3', 'shared_gate', 'shared_up', 'shared_down')}
    del _L0_ffn_all

    def _L1_attn_setup():
        import jax, jax.numpy as jnp
        import numpy as np
        N_HEADS = 16
        MAX_LEN = 128
        key = jax.random.key(seed)
        ks = jax.random.split(key, 6)
        B, T, C = (4, 128, 128)
        scale = 0.02
        return {'x': jax.random.normal(ks[0], (B, T, C), dtype=jnp.float32), 'qkv_w': jax.random.normal(ks[1], (3 * C, C), dtype=jnp.float32) * scale, 'qkv_b': jax.random.normal(ks[2], (3 * C,), dtype=jnp.float32) * scale, 'proj_w': jax.random.normal(ks[3], (C, C), dtype=jnp.float32) * scale, 'proj_b': jax.random.normal(ks[4], (C,), dtype=jnp.float32) * scale, 'rel_pos_emb': jax.random.normal(ks[5], (2 * MAX_LEN - 1, C), dtype=jnp.float32) * scale}
    _L1_attn_all = _L1_attn_setup()
    _L1_attn_in = {k: v for k, v in _L1_attn_all.items() if k in ('qkv_w', 'qkv_b', 'proj_w', 'proj_b', 'rel_pos_emb')}
    del _L1_attn_all

    def _L1_xattn_setup():
        import jax, jax.numpy as jnp
        import numpy as np
        NUM_HEADS = 16
        D_MODEL = 128
        LN_EPS = 1e-05
        key = jax.random.key(seed)
        ks = jax.random.split(key, 10)
        B, S, D = (2, 256, D_MODEL)
        s = 1.0 / np.sqrt(D)
        return {'encoded': jax.random.normal(ks[0], (B, S, D), jnp.float32), 'decoded': jax.random.normal(ks[1], (B, S, D), jnp.float32), 'Wq': jax.random.normal(ks[2], (D, D), jnp.float32) * s, 'bq': jax.random.normal(ks[3], (D,), jnp.float32) * s, 'Wk': jax.random.normal(ks[4], (D, D), jnp.float32) * s, 'bk': jax.random.normal(ks[5], (D,), jnp.float32) * s, 'Wv': jax.random.normal(ks[6], (D, D), jnp.float32) * s, 'bv': jax.random.normal(ks[7], (D,), jnp.float32) * s, 'gamma': jnp.ones((D,), jnp.float32), 'beta': jnp.zeros((D,), jnp.float32)}
    _L1_xattn_all = _L1_xattn_setup()
    _L1_xattn_in = {k: v for k, v in _L1_xattn_all.items() if k in ('Wq', 'bq', 'Wk', 'bk', 'Wv', 'bv', 'gamma', 'beta')}
    del _L1_xattn_all

    def _L1_ffn_setup():
        import jax, jax.numpy as jnp
        import numpy as np
        HIDDEN = 128
        INNER = 512

        def _weight_quant(w):
            scale = 1.0 / jnp.clip(jnp.mean(jnp.abs(w)), 1e-05)
            wq = jnp.clip(jnp.round(w * scale), -1.0, 1.0) / scale
            return w + jax.lax.stop_gradient(wq - w)

        def _act_quant(x):
            scale = 127.0 / jnp.clip(jnp.max(jnp.abs(x), axis=-1, keepdims=True), 1e-05)
            xq = jnp.clip(jnp.round(x * scale), -128.0, 127.0) / scale
            return x + jax.lax.stop_gradient(xq - x)

        def _bitlinear(x, w):
            return jnp.einsum('bsi,oi->bso', _act_quant(x), _weight_quant(w))
        key = jax.random.key(seed)
        k0, k1, k2, k3 = jax.random.split(key, 4)
        x = jax.random.normal(k0, (4, 256, HIDDEN), dtype=jnp.float32)
        w_gate = jax.random.normal(k1, (INNER, HIDDEN), dtype=jnp.float32) / np.sqrt(HIDDEN)
        w_up = jax.random.normal(k2, (INNER, HIDDEN), dtype=jnp.float32) / np.sqrt(HIDDEN)
        w_down = jax.random.normal(k3, (HIDDEN, INNER), dtype=jnp.float32) / np.sqrt(INNER)
        return {'x': x, 'w_gate': w_gate, 'w_up': w_up, 'w_down': w_down}
    _L1_ffn_all = _L1_ffn_setup()
    _L1_ffn_in = {k: v for k, v in _L1_ffn_all.items() if k in ('w_gate', 'w_up', 'w_down')}
    del _L1_ffn_all

    def _L2_attn_setup():
        import jax, jax.numpy as jnp
        import numpy as np
        B, S, DIN, DIM = (1, 512, 128, 128)
        NH, NKV = (16, 4)
        HD = DIM // NH
        GS = NH // NKV
        key = jax.random.key(seed)
        ks = jax.random.split(key, 5)

        def w(k, shape, fan_in):
            return jax.random.normal(k, shape, jnp.float32) * fan_in ** (-0.5)
        return {'x': jax.random.normal(ks[0], (B, S, DIN), jnp.float32), 'wq': w(ks[1], (DIM, DIN), DIN), 'wk': w(ks[2], (NKV * HD, DIN), DIN), 'wv': w(ks[3], (NKV * HD, DIN), DIN), 'wo': w(ks[4], (DIM, DIM), DIM)}
    _L2_attn_all = _L2_attn_setup()
    _L2_attn_in = {k: v for k, v in _L2_attn_all.items() if k in ('wq', 'wk', 'wv', 'wo')}
    del _L2_attn_all

    def _L2_xattn_setup():
        import jax, jax.numpy as jnp
        import numpy as np
        DIM = 128
        HEADS = 16
        HEAD_DIM = DIM // HEADS
        SCALE = HEAD_DIM ** (-0.5)
        key = jax.random.key(seed)
        ks = jax.random.split(key, 7)
        b, n = (2, 256)
        x1 = jax.random.normal(ks[0], (b, n, DIM), dtype=jnp.float32)
        x2 = jax.random.normal(ks[1], (b, n, DIM), dtype=jnp.float32)
        s = DIM ** (-0.5)
        wq = jax.random.normal(ks[2], (DIM, DIM), dtype=jnp.float32) * s
        wk = jax.random.normal(ks[3], (DIM, DIM), dtype=jnp.float32) * s
        wv = jax.random.normal(ks[4], (DIM, DIM), dtype=jnp.float32) * s
        wo = jax.random.normal(ks[5], (DIM, DIM), dtype=jnp.float32) * s
        bo = jax.random.normal(ks[6], (DIM,), dtype=jnp.float32) * 0.01
        return {'x1': x1, 'x2': x2, 'wq': wq, 'wk': wk, 'wv': wv, 'wo': wo, 'bo': bo}
    _L2_xattn_all = _L2_xattn_setup()
    _L2_xattn_in = {k: v for k, v in _L2_xattn_all.items() if k in ('wq', 'wk', 'wv', 'wo', 'bo')}
    del _L2_xattn_all

    def _L2_ffn_setup():
        import jax, jax.numpy as jnp
        import numpy as np
        import math
        E = 16
        TOP_K = 2
        D = 128
        F = 512
        SH = 256
        key = jax.random.key(seed)
        ks = jax.random.split(key, 10)
        s = lambda k, shape, fan: jax.random.normal(k, shape, jnp.float32) / np.sqrt(fan)
        return {'x': jax.random.normal(ks[0], (32, 32, D), jnp.float32), 'gate_w': s(ks[1], (E, D), D), 'up_w': s(ks[2], (E, F, D), D), 'up_b': s(ks[3], (E, F), D), 'gw': s(ks[4], (E, F, D), D), 'gb': s(ks[5], (E, F), D), 'down_w': s(ks[6], (E, D, F), F), 'down_b': s(ks[7], (E, D), F), 'sh_gate_w': s(ks[8], (SH, D), D), 'sh_up_w': s(ks[9], (SH, D), D), 'sh_down_w': s(jax.random.fold_in(key, 11), (D, SH), SH)}
    _L2_ffn_all = _L2_ffn_setup()
    _L2_ffn_in = {k: v for k, v in _L2_ffn_all.items() if k in ('gate_w', 'up_w', 'up_b', 'gw', 'gb', 'down_w', 'down_b', 'sh_gate_w', 'sh_up_w', 'sh_down_w')}
    del _L2_ffn_all

    def _L3_attn_setup():
        import jax, jax.numpy as jnp
        import numpy as np
        EMBED_DIM = 128
        NUM_HEADS = 16
        HEAD_DIM = EMBED_DIM // NUM_HEADS
        SCALING = HEAD_DIM ** (-0.5)
        B, T = (2, 256)
        key = jax.random.key(seed)
        ks = jax.random.split(key, 8)
        s = 0.02
        return {'hidden_states': jax.random.normal(ks[0], (B, T, EMBED_DIM), jnp.float32), 'Wq': jax.random.normal(ks[1], (EMBED_DIM, EMBED_DIM), jnp.float32) * s, 'bq': jax.random.normal(ks[2], (EMBED_DIM,), jnp.float32) * s, 'Wk': jax.random.normal(ks[3], (HEAD_DIM, EMBED_DIM), jnp.float32) * s, 'Wv': jax.random.normal(ks[4], (HEAD_DIM, EMBED_DIM), jnp.float32) * s, 'bv': jax.random.normal(ks[5], (HEAD_DIM,), jnp.float32) * s, 'Wo': jax.random.normal(ks[6], (EMBED_DIM, EMBED_DIM), jnp.float32) * s, 'bo': jax.random.normal(ks[7], (EMBED_DIM,), jnp.float32) * s}
    _L3_attn_all = _L3_attn_setup()
    _L3_attn_in = {k: v for k, v in _L3_attn_all.items() if k in ('Wq', 'bq', 'Wk', 'Wv', 'bv', 'Wo', 'bo')}
    del _L3_attn_all

    def _L3_xattn_setup():
        import jax, jax.numpy as jnp
        import numpy as np
        B, S, D, H = (2, 256, 128, 16)
        HD = D // H
        LN_EPS = 1e-05

        def _linear(x, w, b):
            return jnp.einsum('bsd,od->bso', x, w) + b

        def _split_heads(x):
            b, s, _ = x.shape
            return x.reshape(b, s, H, HD).transpose(0, 2, 1, 3)
        key = jax.random.key(seed)
        ks = jax.random.split(key, 14)
        w = 0.02
        return {'q': jax.random.normal(ks[0], (B, S, D), jnp.float32), 'k': jax.random.normal(ks[1], (B, S, D), jnp.float32), 'v': jax.random.normal(ks[2], (B, S, D), jnp.float32), 'mask': jnp.zeros((B, 1, S, S), dtype=bool), 'training': 0, 'wq_w': jax.random.normal(ks[3], (D, D), jnp.float32) * w, 'wq_b': jnp.zeros((D,), jnp.float32), 'wk_w': jax.random.normal(ks[4], (D, D), jnp.float32) * w, 'wk_b': jnp.zeros((D,), jnp.float32), 'wv_w': jax.random.normal(ks[5], (D, D), jnp.float32) * w, 'wv_b': jnp.zeros((D,), jnp.float32), 'wo_w': jax.random.normal(ks[6], (D, D), jnp.float32) * w, 'wo_b': jnp.zeros((D,), jnp.float32), 'ln_g': jnp.ones((D,), jnp.float32), 'ln_b': jnp.zeros((D,), jnp.float32)}
    _L3_xattn_all = _L3_xattn_setup()
    _L3_xattn_in = {k: v for k, v in _L3_xattn_all.items() if k in ('wq_w', 'wq_b', 'wk_w', 'wk_b', 'wv_w', 'wv_b', 'wo_w', 'wo_b', 'ln_g', 'ln_b')}
    del _L3_xattn_all

    def _L3_ffn_setup():
        import jax, jax.numpy as jnp
        import numpy as np
        D_MODEL = 128
        N_HEADS = 16
        N_EXPERTS = 8
        TOP_K = 2
        EXPERT_HIDDEN = D_MODEL * 4 // N_EXPERTS

        def layer_norm(x, g, b, eps=1e-05):
            mu = jnp.mean(x, axis=-1, keepdims=True)
            var = jnp.var(x, axis=-1, keepdims=True)
            return (x - mu) * jax.lax.rsqrt(var + eps) * g + b
        key = jax.random.key(seed)
        ks = jax.random.split(key, 12)
        s = 1.0 / np.sqrt(D_MODEL)
        return {'x': jax.random.normal(ks[0], (2, 256, D_MODEL), dtype=jnp.float32), 'Wq': jax.random.normal(ks[1], (D_MODEL, D_MODEL), dtype=jnp.float32) * s, 'Wk': jax.random.normal(ks[2], (D_MODEL, D_MODEL), dtype=jnp.float32) * s, 'Wv': jax.random.normal(ks[3], (D_MODEL, D_MODEL), dtype=jnp.float32) * s, 'Wo': jax.random.normal(ks[4], (D_MODEL, D_MODEL), dtype=jnp.float32) * s, 'g1': jnp.ones((D_MODEL,), jnp.float32), 'b1': jnp.zeros((D_MODEL,), jnp.float32), 'g2': jnp.ones((D_MODEL,), jnp.float32), 'b2': jnp.zeros((D_MODEL,), jnp.float32), 'Wg': jax.random.normal(ks[5], (D_MODEL, N_EXPERTS), dtype=jnp.float32) * s, 'W1': jax.random.normal(ks[6], (N_EXPERTS, D_MODEL, EXPERT_HIDDEN), dtype=jnp.float32) * s, 'W2': jax.random.normal(ks[7], (N_EXPERTS, EXPERT_HIDDEN, D_MODEL), dtype=jnp.float32) * (1.0 / np.sqrt(EXPERT_HIDDEN))}
    _L3_ffn_all = _L3_ffn_setup()
    _L3_ffn_in = {k: v for k, v in _L3_ffn_all.items() if k in ('Wq', 'Wk', 'Wv', 'Wo', 'g1', 'b1', 'g2', 'b2', 'Wg', 'W1', 'W2')}
    del _L3_ffn_all
    return {'x': x, 'ctx_1024': ctx_1024, 'mask_Bx1xSxS2_bf0': mask_Bx1xSxS2_bf0, 'L0_attn_Wq': _L0_attn_in['Wq'], 'L0_attn_Wk': _L0_attn_in['Wk'], 'L0_attn_Wv': _L0_attn_in['Wv'], 'L0_attn_Wo': _L0_attn_in['Wo'], 'L0_attn_bo': _L0_attn_in['bo'], 'L0_attn_Aq': _L0_attn_in['Aq'], 'L0_attn_Bq': _L0_attn_in['Bq'], 'L0_attn_Ak': _L0_attn_in['Ak'], 'L0_attn_Bk': _L0_attn_in['Bk'], 'L0_attn_Av': _L0_attn_in['Av'], 'L0_attn_Bv': _L0_attn_in['Bv'], 'L0_attn_Ao': _L0_attn_in['Ao'], 'L0_attn_Bo': _L0_attn_in['Bo'], 'L0_xattn_w_q': _L0_xattn_in['w_q'], 'L0_xattn_b_q': _L0_xattn_in['b_q'], 'L0_xattn_w_k': _L0_xattn_in['w_k'], 'L0_xattn_b_k': _L0_xattn_in['b_k'], 'L0_xattn_w_v': _L0_xattn_in['w_v'], 'L0_xattn_b_v': _L0_xattn_in['b_v'], 'L0_xattn_w_o': _L0_xattn_in['w_o'], 'L0_xattn_b_o': _L0_xattn_in['b_o'], 'L0_ffn_gate_weight': _L0_ffn_in['gate_weight'], 'L0_ffn_e_bias': _L0_ffn_in['e_bias'], 'L0_ffn_w1': _L0_ffn_in['w1'], 'L0_ffn_w2': _L0_ffn_in['w2'], 'L0_ffn_w3': _L0_ffn_in['w3'], 'L0_ffn_shared_gate': _L0_ffn_in['shared_gate'], 'L0_ffn_shared_up': _L0_ffn_in['shared_up'], 'L0_ffn_shared_down': _L0_ffn_in['shared_down'], 'L1_attn_qkv_w': _L1_attn_in['qkv_w'], 'L1_attn_qkv_b': _L1_attn_in['qkv_b'], 'L1_attn_proj_w': _L1_attn_in['proj_w'], 'L1_attn_proj_b': _L1_attn_in['proj_b'], 'L1_attn_rel_pos_emb': _L1_attn_in['rel_pos_emb'], 'L1_xattn_Wq': _L1_xattn_in['Wq'], 'L1_xattn_bq': _L1_xattn_in['bq'], 'L1_xattn_Wk': _L1_xattn_in['Wk'], 'L1_xattn_bk': _L1_xattn_in['bk'], 'L1_xattn_Wv': _L1_xattn_in['Wv'], 'L1_xattn_bv': _L1_xattn_in['bv'], 'L1_xattn_gamma': _L1_xattn_in['gamma'], 'L1_xattn_beta': _L1_xattn_in['beta'], 'L1_ffn_w_gate': _L1_ffn_in['w_gate'], 'L1_ffn_w_up': _L1_ffn_in['w_up'], 'L1_ffn_w_down': _L1_ffn_in['w_down'], 'L2_attn_wq': _L2_attn_in['wq'], 'L2_attn_wk': _L2_attn_in['wk'], 'L2_attn_wv': _L2_attn_in['wv'], 'L2_attn_wo': _L2_attn_in['wo'], 'L2_xattn_wq': _L2_xattn_in['wq'], 'L2_xattn_wk': _L2_xattn_in['wk'], 'L2_xattn_wv': _L2_xattn_in['wv'], 'L2_xattn_wo': _L2_xattn_in['wo'], 'L2_xattn_bo': _L2_xattn_in['bo'], 'L2_ffn_gate_w': _L2_ffn_in['gate_w'], 'L2_ffn_up_w': _L2_ffn_in['up_w'], 'L2_ffn_up_b': _L2_ffn_in['up_b'], 'L2_ffn_gw': _L2_ffn_in['gw'], 'L2_ffn_gb': _L2_ffn_in['gb'], 'L2_ffn_down_w': _L2_ffn_in['down_w'], 'L2_ffn_down_b': _L2_ffn_in['down_b'], 'L2_ffn_sh_gate_w': _L2_ffn_in['sh_gate_w'], 'L2_ffn_sh_up_w': _L2_ffn_in['sh_up_w'], 'L2_ffn_sh_down_w': _L2_ffn_in['sh_down_w'], 'L3_attn_Wq': _L3_attn_in['Wq'], 'L3_attn_bq': _L3_attn_in['bq'], 'L3_attn_Wk': _L3_attn_in['Wk'], 'L3_attn_Wv': _L3_attn_in['Wv'], 'L3_attn_bv': _L3_attn_in['bv'], 'L3_attn_Wo': _L3_attn_in['Wo'], 'L3_attn_bo': _L3_attn_in['bo'], 'L3_xattn_wq_w': _L3_xattn_in['wq_w'], 'L3_xattn_wq_b': _L3_xattn_in['wq_b'], 'L3_xattn_wk_w': _L3_xattn_in['wk_w'], 'L3_xattn_wk_b': _L3_xattn_in['wk_b'], 'L3_xattn_wv_w': _L3_xattn_in['wv_w'], 'L3_xattn_wv_b': _L3_xattn_in['wv_b'], 'L3_xattn_wo_w': _L3_xattn_in['wo_w'], 'L3_xattn_wo_b': _L3_xattn_in['wo_b'], 'L3_xattn_ln_g': _L3_xattn_in['ln_g'], 'L3_xattn_ln_b': _L3_xattn_in['ln_b'], 'L3_ffn_Wq': _L3_ffn_in['Wq'], 'L3_ffn_Wk': _L3_ffn_in['Wk'], 'L3_ffn_Wv': _L3_ffn_in['Wv'], 'L3_ffn_Wo': _L3_ffn_in['Wo'], 'L3_ffn_g1': _L3_ffn_in['g1'], 'L3_ffn_b1': _L3_ffn_in['b1'], 'L3_ffn_g2': _L3_ffn_in['g2'], 'L3_ffn_b2': _L3_ffn_in['b2'], 'L3_ffn_Wg': _L3_ffn_in['Wg'], 'L3_ffn_W1': _L3_ffn_in['W1'], 'L3_ffn_W2': _L3_ffn_in['W2']}

def reference(x, ctx_1024, mask_Bx1xSxS2_bf0, L0_attn_Wq, L0_attn_Wk, L0_attn_Wv, L0_attn_Wo, L0_attn_bo, L0_attn_Aq, L0_attn_Bq, L0_attn_Ak, L0_attn_Bk, L0_attn_Av, L0_attn_Bv, L0_attn_Ao, L0_attn_Bo, L0_xattn_w_q, L0_xattn_b_q, L0_xattn_w_k, L0_xattn_b_k, L0_xattn_w_v, L0_xattn_b_v, L0_xattn_w_o, L0_xattn_b_o, L0_ffn_gate_weight, L0_ffn_e_bias, L0_ffn_w1, L0_ffn_w2, L0_ffn_w3, L0_ffn_shared_gate, L0_ffn_shared_up, L0_ffn_shared_down, L1_attn_qkv_w, L1_attn_qkv_b, L1_attn_proj_w, L1_attn_proj_b, L1_attn_rel_pos_emb, L1_xattn_Wq, L1_xattn_bq, L1_xattn_Wk, L1_xattn_bk, L1_xattn_Wv, L1_xattn_bv, L1_xattn_gamma, L1_xattn_beta, L1_ffn_w_gate, L1_ffn_w_up, L1_ffn_w_down, L2_attn_wq, L2_attn_wk, L2_attn_wv, L2_attn_wo, L2_xattn_wq, L2_xattn_wk, L2_xattn_wv, L2_xattn_wo, L2_xattn_bo, L2_ffn_gate_w, L2_ffn_up_w, L2_ffn_up_b, L2_ffn_gw, L2_ffn_gb, L2_ffn_down_w, L2_ffn_down_b, L2_ffn_sh_gate_w, L2_ffn_sh_up_w, L2_ffn_sh_down_w, L3_attn_Wq, L3_attn_bq, L3_attn_Wk, L3_attn_Wv, L3_attn_bv, L3_attn_Wo, L3_attn_bo, L3_xattn_wq_w, L3_xattn_wq_b, L3_xattn_wk_w, L3_xattn_wk_b, L3_xattn_wv_w, L3_xattn_wv_b, L3_xattn_wo_w, L3_xattn_wo_b, L3_xattn_ln_g, L3_xattn_ln_b, L3_ffn_Wq, L3_ffn_Wk, L3_ffn_Wv, L3_ffn_Wo, L3_ffn_g1, L3_ffn_b1, L3_ffn_g2, L3_ffn_b2, L3_ffn_Wg, L3_ffn_W1, L3_ffn_W2):
    import jax
    import jax.numpy as jnp

    def _L0_attn_ref(x, Wq, Wk, Wv, Wo, bo, Aq, Bq, Ak, Bk, Av, Bv, Ao, Bo):
        import jax, jax.numpy as jnp
        import numpy as np
        DIM = 128
        HEADS = 16
        HEAD_DIM = DIM // HEADS
        RANK = 16
        LORA_ALPHA = 1
        SCALING = LORA_ALPHA / RANK
        SCALE = HEAD_DIM ** (-0.5)
        B, N = (8, 128)

        def _lora_linear(x, W, A, Blo, bias=None):
            y = x @ W.T + x @ A.T @ Blo.T * SCALING
            if bias is not None:
                y = y + bias
            return y

        def _split_heads(t, b, n):
            return t.reshape(b, n, HEADS, HEAD_DIM).transpose(0, 2, 1, 3)
        b, n, c = x.shape
        q = _split_heads(_lora_linear(x, Wq, Aq, Bq), b, n)
        k = _split_heads(_lora_linear(x, Wk, Ak, Bk), b, n)
        v = _split_heads(_lora_linear(x, Wv, Av, Bv), b, n)
        attn = jnp.einsum('bhnd,bhmd->bhnm', q, k) * SCALE
        attn = jax.nn.softmax(attn, axis=-1)
        out = jnp.einsum('bhnm,bhmd->bhnd', attn, v)
        out = out.transpose(0, 2, 1, 3).reshape(b, n, c)
        return _lora_linear(out, Wo, Ao, Bo, bias=bo)

    def _L0_xattn_ref(query, key, value, mask, w_q, b_q, w_k, b_k, w_v, b_v, w_o, b_o):
        import jax, jax.numpy as jnp
        import numpy as np
        D_MODEL = 128
        NUM_HEADS = 16
        HEAD_DIM = D_MODEL // NUM_HEADS
        B, S, _ = query.shape
        H, Dh = (NUM_HEADS, HEAD_DIM)
        q = (query @ w_q + b_q).reshape(B, S, H, Dh).transpose(0, 2, 1, 3)
        k = (key @ w_k + b_k).reshape(B, S, H, Dh).transpose(0, 2, 1, 3)
        v = (value @ w_v + b_v).reshape(B, S, H, Dh).transpose(0, 2, 1, 3)
        scale = 1.0 / jnp.sqrt(jnp.asarray(Dh, q.dtype))
        scores = jnp.einsum('bhqd,bhkd->bhqk', q, k) * scale
        if mask:
            causal = jnp.tril(jnp.ones((S, S), dtype=bool))
            scores = jnp.where(causal, scores, jnp.asarray(-1000000000.0, scores.dtype))
        attn = jax.nn.softmax(scores, axis=-1)
        x = jnp.einsum('bhqk,bhkd->bhqd', attn, v)
        x = x.transpose(0, 2, 1, 3).reshape(B, S, H * Dh)
        return x @ w_o + b_o

    def _L0_ffn_ref(hidden_states, gate_weight, e_bias, w1, w2, w3, shared_gate, shared_up, shared_down):
        import jax, jax.numpy as jnp
        import numpy as np
        E, K, NG, TG = (64, 8, 8, 4)
        CAP = 128
        SCALE = 2.5

        def _route(x_flat, gate_weight, e_bias):
            T = x_flat.shape[0]
            logits = x_flat.astype(jnp.float32) @ gate_weight.astype(jnp.float32).T
            scores = jax.nn.sigmoid(logits)
            sfc = scores + e_bias[None, :]
            group_scores = jax.lax.top_k(sfc.reshape(T, NG, E // NG), 2)[0].sum(-1)
            _, gidx = jax.lax.top_k(group_scores, TG)
            gmask = jnp.zeros((T, NG), jnp.float32).at[jnp.arange(T)[:, None], gidx].set(1.0)
            smask = jnp.repeat(gmask, E // NG, axis=1)
            tmp = jnp.where(smask > 0, sfc, 0.0)
            _, topk_idx = jax.lax.top_k(tmp, K)
            topk_w = jnp.take_along_axis(scores, topk_idx, axis=1)
            topk_w = topk_w / (topk_w.sum(-1, keepdims=True) + 1e-20)
            return (topk_idx, topk_w * SCALE)

        def _moe_forward(hidden_states, gate_weight, e_bias, w1, w2, w3, shared_gate, shared_up, shared_down):
            B, S, H = hidden_states.shape
            T = B * S
            x = hidden_states.reshape(T, H)
            topk_idx, topk_w = _route(x, gate_weight, e_bias)
            Sk = T * K
            flat_e = topk_idx.reshape(-1)
            order = jnp.argsort(flat_e)
            sorted_e = flat_e[order]
            counts = jax.ops.segment_sum(jnp.ones((Sk,), jnp.int32), flat_e, num_segments=E)
            offsets = jnp.cumsum(counts) - counts
            pos = jnp.arange(Sk) - offsets[sorted_e]
            tok_sorted = x[order // K]
            xe = jnp.zeros((E, CAP, H), x.dtype).at[sorted_e, pos].set(tok_sorted, mode='drop')
            h = jax.nn.silu(jnp.einsum('ech,efh->ecf', xe, w1)) * jnp.einsum('ech,efh->ecf', xe, w3)
            ye = jnp.einsum('ecf,ehf->ech', h, w2)
            pos_c = jnp.minimum(pos, CAP - 1)
            vals = ye[sorted_e, pos_c]
            vals = jnp.where((pos < CAP)[:, None], vals, 0.0)
            flat_w = topk_w.reshape(-1)[order].astype(vals.dtype)
            flat_t = (jnp.arange(Sk) // K)[order]
            out = jax.ops.segment_sum(vals * flat_w[:, None], flat_t, num_segments=T)
            shared = jax.nn.silu(x @ shared_gate.T) * (x @ shared_up.T) @ shared_down.T
            return (out + shared).reshape(B, S, H)
        return _moe_forward(hidden_states, gate_weight, e_bias, w1, w2, w3, shared_gate, shared_up, shared_down)

    def _L1_attn_ref(x, qkv_w, qkv_b, proj_w, proj_b, rel_pos_emb):
        import jax, jax.numpy as jnp
        import numpy as np
        N_HEADS = 16
        MAX_LEN = 128
        B, T, C = x.shape
        H = N_HEADS
        D = C // H
        qkv = (x @ qkv_w.T + qkv_b).reshape(B, T, 3, H, D)
        qkv = jnp.transpose(qkv, (2, 0, 3, 1, 4))
        q, k, v = (qkv[0], qkv[1], qkv[2])
        att = jnp.einsum('bhtd,bhsd->bhts', q, k) / np.sqrt(D).astype(np.float32)
        table = rel_pos_emb.reshape(2 * MAX_LEN - 1, H, D).sum(axis=-1)
        pos = jnp.arange(T)
        rel_idx = pos[:, None] - pos[None, :] + (MAX_LEN - 1)
        bias = jnp.transpose(table[rel_idx], (2, 0, 1))
        att = att + bias[None]
        causal = pos[None, :] > pos[:, None]
        att = jnp.where(causal[None, None], -jnp.inf, att)
        att = jax.nn.softmax(att, axis=-1)
        out = jnp.einsum('bhts,bhsd->bhtd', att, v)
        out = jnp.transpose(out, (0, 2, 1, 3)).reshape(B, T, C)
        return out @ proj_w.T + proj_b

    def _L1_xattn_ref(encoded, decoded, Wq, bq, Wk, bk, Wv, bv, gamma, beta):
        import jax, jax.numpy as jnp
        import numpy as np
        NUM_HEADS = 16
        D_MODEL = 128
        LN_EPS = 1e-05
        B, Sq, D = decoded.shape
        H = NUM_HEADS
        dh = D // H
        q = decoded @ Wq.T + bq
        k = encoded @ Wk.T + bk
        v = encoded @ Wv.T + bv
        q = q.reshape(B, Sq, H, dh).transpose(0, 2, 1, 3)
        k = k.reshape(B, -1, H, dh).transpose(0, 2, 1, 3)
        v = v.reshape(B, -1, H, dh).transpose(0, 2, 1, 3)
        qk = jnp.einsum('bhqd,bhkd->bhqk', q, k)
        qk = jnp.where(jnp.isnan(qk), -jnp.inf, qk)
        attn = jax.nn.softmax(qk, axis=-1)
        attn = jnp.where(jnp.isnan(attn), 0.0, attn)
        v = jnp.where(jnp.isnan(v), 0.0, v)
        z = jnp.einsum('bhqk,bhkd->bhqd', attn, v)
        z = z.reshape(B, Sq, D)
        x = z + decoded
        mu = jnp.mean(x, axis=-1, keepdims=True)
        var = jnp.var(x, axis=-1, keepdims=True)
        return (x - mu) * jax.lax.rsqrt(var + LN_EPS) * gamma + beta

    def _L1_ffn_ref(x, w_gate, w_up, w_down):
        import jax, jax.numpy as jnp
        import numpy as np
        HIDDEN = 128
        INNER = 512

        def _weight_quant(w):
            scale = 1.0 / jnp.clip(jnp.mean(jnp.abs(w)), 1e-05)
            wq = jnp.clip(jnp.round(w * scale), -1.0, 1.0) / scale
            return w + jax.lax.stop_gradient(wq - w)

        def _act_quant(x):
            scale = 127.0 / jnp.clip(jnp.max(jnp.abs(x), axis=-1, keepdims=True), 1e-05)
            xq = jnp.clip(jnp.round(x * scale), -128.0, 127.0) / scale
            return x + jax.lax.stop_gradient(xq - x)

        def _bitlinear(x, w):
            return jnp.einsum('bsi,oi->bso', _act_quant(x), _weight_quant(w))
        gate = jax.nn.silu(_bitlinear(x, w_gate))
        up = _bitlinear(x, w_up)
        return _bitlinear(gate * up, w_down)

    def _L2_attn_ref(x, wq, wk, wv, wo):
        import jax, jax.numpy as jnp
        import numpy as np
        B, S, DIN, DIM = (1, 512, 128, 128)
        NH, NKV = (16, 4)
        HD = DIM // NH
        GS = NH // NKV
        b, s, _ = x.shape
        q = (x @ wq.T).reshape(b, s, NKV, GS, HD)
        k = (x @ wk.T).reshape(b, s, NKV, HD)
        v = (x @ wv.T).reshape(b, s, NKV, HD)
        scale = jnp.asarray(HD ** 0.5, x.dtype)
        att = jnp.einsum('bsgmd,btgd->bgmst', q, k) / scale
        causal = jnp.triu(jnp.ones((s, s), bool), 1)
        att = jnp.where(causal, -jnp.inf, att)
        att = jax.nn.softmax(att, axis=-1)
        ctx = jnp.einsum('bgmst,btgd->bsgmd', att, v).reshape(b, s, DIM)
        return ctx @ wo.T

    def _L2_xattn_ref(x1, x2, wq, wk, wv, wo, bo):
        import jax, jax.numpy as jnp
        import numpy as np
        DIM = 128
        HEADS = 16
        HEAD_DIM = DIM // HEADS
        SCALE = HEAD_DIM ** (-0.5)
        b, n, _ = x1.shape
        m = x2.shape[1]
        q = (x1 @ wq.T).reshape(b, n, HEADS, HEAD_DIM).transpose(0, 2, 1, 3)
        k = (x2 @ wk.T).reshape(b, m, HEADS, HEAD_DIM).transpose(0, 2, 1, 3)
        v = (x2 @ wv.T).reshape(b, m, HEADS, HEAD_DIM).transpose(0, 2, 1, 3)
        dots = jnp.einsum('bhnd,bhmd->bhnm', q, k) * SCALE
        attn = jax.nn.softmax(dots, axis=-1)
        out = jnp.einsum('bhnm,bhmd->bhnd', attn, v)
        out = out.transpose(0, 2, 1, 3).reshape(b, n, DIM)
        return out @ wo.T + bo

    def _L2_ffn_ref(x, gate_w, up_w, up_b, gw, gb, down_w, down_b, sh_gate_w, sh_up_w, sh_down_w):
        import jax, jax.numpy as jnp
        import numpy as np
        import math
        E = 16
        TOP_K = 2
        D = 128
        F = 512
        SH = 256
        B, S, Dm = x.shape
        h = x.reshape(-1, Dm)
        T = h.shape[0]
        scores = jax.nn.sigmoid(h @ gate_w.T)
        cap = math.ceil(T / E * TOP_K)
        topk_score, topk_ids = jax.lax.top_k(scores.T, cap)
        xin = h[topk_ids]
        up = jnp.einsum('ecd,efd->ecf', xin, up_w) + up_b[:, None, :]
        g = jnp.einsum('ecd,efd->ecf', xin, gw) + gb[:, None, :]
        eo = jax.nn.silu(g) * up
        eo = jnp.einsum('ecf,edf->ecd', eo, down_w) + down_b[:, None, :]
        flat = (eo * topk_score[..., None]).reshape(-1, Dm)
        out = jnp.zeros_like(h).at[topk_ids.reshape(-1)].add(flat)
        out = out.reshape(B, S, Dm)
        shared = jax.nn.silu(jnp.einsum('bsd,fd->bsf', x, sh_gate_w)) * jnp.einsum('bsd,fd->bsf', x, sh_up_w)
        shared = jnp.einsum('bsf,df->bsd', shared, sh_down_w)
        return out + shared

    def _L3_attn_ref(hidden_states, Wq, bq, Wk, Wv, bv, Wo, bo):
        import jax, jax.numpy as jnp
        import numpy as np
        EMBED_DIM = 128
        NUM_HEADS = 16
        HEAD_DIM = EMBED_DIM // NUM_HEADS
        SCALING = HEAD_DIM ** (-0.5)
        B, T = (2, 256)
        bsz, tgt_len, _ = hidden_states.shape
        q = (hidden_states @ Wq.T + bq) * SCALING
        k = hidden_states @ Wk.T
        v = hidden_states @ Wv.T + bv
        q = q.reshape(bsz, tgt_len, NUM_HEADS, HEAD_DIM)
        scores = jnp.einsum('bthd,bsd->bhts', q, k)
        probs = jax.nn.softmax(scores, axis=-1)
        ctx = jnp.einsum('bhts,bsd->bthd', probs, v)
        ctx = ctx.reshape(bsz, tgt_len, EMBED_DIM)
        return ctx @ Wo.T + bo

    def _L3_xattn_ref(q, k, v, mask, training, wq_w, wq_b, wk_w, wk_b, wv_w, wv_b, wo_w, wo_b, ln_g, ln_b):
        import jax, jax.numpy as jnp
        import numpy as np
        B, S, D, H = (2, 256, 128, 16)
        HD = D // H
        LN_EPS = 1e-05

        def _linear(x, w, b):
            return jnp.einsum('bsd,od->bso', x, w) + b

        def _split_heads(x):
            b, s, _ = x.shape
            return x.reshape(b, s, H, HD).transpose(0, 2, 1, 3)
        residual = q
        Q = _split_heads(_linear(q, wq_w, wq_b))
        K = _split_heads(_linear(k, wk_w, wk_b))
        V = _split_heads(_linear(v, wv_w, wv_b))
        dk = jnp.sqrt(jnp.asarray(HD, jnp.float16)).astype(jnp.float32) + 1e-08
        score = jnp.einsum('bhqd,bhkd->bhqk', Q, K) / dk
        attn = jnp.where(mask, -jnp.inf, score)
        ctx = jnp.einsum('bhqk,bhkd->bhqd', attn, V)
        b, _, s, _ = ctx.shape
        ctx = ctx.transpose(0, 2, 1, 3).reshape(b, s, D)
        o = _linear(ctx, wo_w, wo_b)
        x = residual + o
        mu = jnp.mean(x, axis=-1, keepdims=True)
        var = jnp.mean(jnp.square(x - mu), axis=-1, keepdims=True)
        return ln_g * (x - mu) * jax.lax.rsqrt(var + LN_EPS) + ln_b

    def _L3_ffn_ref(x, Wq, Wk, Wv, Wo, g1, b1, g2, b2, Wg, W1, W2):
        import jax, jax.numpy as jnp
        import numpy as np
        D_MODEL = 128
        N_HEADS = 16
        N_EXPERTS = 8
        TOP_K = 2
        EXPERT_HIDDEN = D_MODEL * 4 // N_EXPERTS

        def layer_norm(x, g, b, eps=1e-05):
            mu = jnp.mean(x, axis=-1, keepdims=True)
            var = jnp.var(x, axis=-1, keepdims=True)
            return (x - mu) * jax.lax.rsqrt(var + eps) * g + b
        B, S, D = x.shape
        H, dk = (N_HEADS, D // N_HEADS)
        xn = layer_norm(x, g1, b1)
        q = (xn @ Wq).reshape(B, S, H, dk).transpose(0, 2, 1, 3)
        k = (xn @ Wk).reshape(B, S, H, dk).transpose(0, 2, 1, 3)
        v = (xn @ Wv).reshape(B, S, H, dk).transpose(0, 2, 1, 3)
        scores = jnp.einsum('bhqd,bhkd->bhqk', q, k) / np.sqrt(dk)
        attn = jax.nn.softmax(scores, axis=-1)
        o = jnp.einsum('bhqk,bhkd->bhqd', attn, v)
        o = o.transpose(0, 2, 1, 3).reshape(B, S, D) @ Wo
        x = x + o
        xn2 = layer_norm(x, g2, b2)
        xf = xn2.reshape(B * S, D)
        gate = xf @ Wg
        topv, topi = jax.lax.top_k(gate, TOP_K)
        probs = jax.nn.softmax(topv, axis=-1)
        cw = jnp.sum(jax.nn.one_hot(topi, N_EXPERTS, dtype=xf.dtype) * probs[..., None], axis=1)
        h = jax.nn.relu(jnp.einsum('td,edh->teh', xf, W1))
        y = jnp.einsum('teh,ehd->ted', h, W2)
        moe = jnp.einsum('ted,te->td', y, cw).reshape(B, S, D)
        return x + moe
    x = x + _L0_attn_ref(_layernorm(x, axis=-1), L0_attn_Wq, L0_attn_Wk, L0_attn_Wv, L0_attn_Wo, L0_attn_bo, L0_attn_Aq, L0_attn_Bq, L0_attn_Ak, L0_attn_Bk, L0_attn_Av, L0_attn_Bv, L0_attn_Ao, L0_attn_Bo)
    x = x + _L0_xattn_ref(_layernorm(x, axis=-1), ctx_1024, ctx_1024, 1, L0_xattn_w_q, L0_xattn_b_q, L0_xattn_w_k, L0_xattn_b_k, L0_xattn_w_v, L0_xattn_b_v, L0_xattn_w_o, L0_xattn_b_o)
    x = x + _L0_ffn_ref(_layernorm(x, axis=-1), L0_ffn_gate_weight, L0_ffn_e_bias, L0_ffn_w1, L0_ffn_w2, L0_ffn_w3, L0_ffn_shared_gate, L0_ffn_shared_up, L0_ffn_shared_down)
    x = x + _L1_attn_ref(_layernorm(x, axis=-1), L1_attn_qkv_w, L1_attn_qkv_b, L1_attn_proj_w, L1_attn_proj_b, L1_attn_rel_pos_emb)
    x = x + _L1_xattn_ref(ctx_1024, _layernorm(x, axis=-1), L1_xattn_Wq, L1_xattn_bq, L1_xattn_Wk, L1_xattn_bk, L1_xattn_Wv, L1_xattn_bv, L1_xattn_gamma, L1_xattn_beta)
    x = x + _L1_ffn_ref(_layernorm(x, axis=-1), L1_ffn_w_gate, L1_ffn_w_up, L1_ffn_w_down)
    x = x + _L2_attn_ref(_layernorm(x, axis=-1), L2_attn_wq, L2_attn_wk, L2_attn_wv, L2_attn_wo)
    x = x + _L2_xattn_ref(_layernorm(x, axis=-1), ctx_1024, L2_xattn_wq, L2_xattn_wk, L2_xattn_wv, L2_xattn_wo, L2_xattn_bo)
    x = x + _L2_ffn_ref(_layernorm(x, axis=-1), L2_ffn_gate_w, L2_ffn_up_w, L2_ffn_up_b, L2_ffn_gw, L2_ffn_gb, L2_ffn_down_w, L2_ffn_down_b, L2_ffn_sh_gate_w, L2_ffn_sh_up_w, L2_ffn_sh_down_w)
    x = x + _L3_attn_ref(_layernorm(x, axis=-1), L3_attn_Wq, L3_attn_bq, L3_attn_Wk, L3_attn_Wv, L3_attn_bv, L3_attn_Wo, L3_attn_bo)
    x = x + _L3_xattn_ref(_layernorm(x, axis=-1), ctx_1024, ctx_1024, mask_Bx1xSxS2_bf0, 0, L3_xattn_wq_w, L3_xattn_wq_b, L3_xattn_wk_w, L3_xattn_wk_b, L3_xattn_wv_w, L3_xattn_wv_b, L3_xattn_wo_w, L3_xattn_wo_b, L3_xattn_ln_g, L3_xattn_ln_b)
    x = x + _L3_ffn_ref(_layernorm(x, axis=-1), L3_ffn_Wq, L3_ffn_Wk, L3_ffn_Wv, L3_ffn_Wo, L3_ffn_g1, L3_ffn_b1, L3_ffn_g2, L3_ffn_b2, L3_ffn_Wg, L3_ffn_W1, L3_ffn_W2)
    return x

_drawn_inputs = setup_inputs


def setup_inputs(seed=0):
    import zlib

    import numpy as np

    out = dict(_drawn_inputs(seed))
    spreads = {'L0_attn_bo': (0.0, 0.1),
     'L0_ffn_e_bias': (0.0, 0.678),
     'L1_xattn_gamma': (1.0, 0.2),
     'L1_xattn_beta': (0.0, 0.1),
     'L3_xattn_wq_b': (0.0, 0.47),
     'L3_xattn_wk_b': (0.0, 0.376),
     'L3_xattn_wv_b': (0.0, 0.395),
     'L3_xattn_wo_b': (0.0, 0.288),
     'L3_xattn_ln_g': (1.0, 0.2),
     'L3_xattn_ln_b': (0.0, 0.1),
     'L3_ffn_g1': (1.0, 0.2),
     'L3_ffn_b1': (0.0, 0.1),
     'L3_ffn_g2': (1.0, 0.2),
     'L3_ffn_b2': (0.0, 0.1)}
    factors = {'L0_attn_Aq': 3.289,
     'L0_attn_Bq': 3.202,
     'L0_attn_Ak': 3.167,
     'L0_attn_Bk': 3.276,
     'L0_attn_Av': 3.123,
     'L0_attn_Bv': 3.12,
     'L0_attn_Ao': 3.048,
     'L0_attn_Bo': 3.06,
     'L0_xattn_b_q': 2.863,
     'L0_xattn_b_k': 64.0,
     'L0_ffn_gate_weight': 7.07,
     'L0_ffn_w1': 6.202,
     'L0_ffn_w2': 6.507,
     'L0_ffn_w3': 6.345,
     'L0_ffn_shared_gate': 2.739,
     'L0_ffn_shared_up': 2.735,
     'L0_ffn_shared_down': 2.97,
     'L1_attn_qkv_b': 3.638,
     'L1_attn_rel_pos_emb': 22.511,
     'L1_xattn_bk': 64.0,
     'L2_xattn_bo': 5.455,
     'L3_attn_Wq': 8.0,
     'L3_attn_bq': 8.0,
     'L3_attn_Wk': 8.0,
     'L3_attn_Wv': 3.923,
     'L3_attn_bv': 8.0,
     'L3_attn_Wo': 3.931,
     'L3_attn_bo': 4.557}
    for name, (base, spread) in spreads.items():
        noise = np.random.default_rng([zlib.crc32(name.encode()), seed]).standard_normal(out[name].shape)
        drawn = base * np.exp(spread * noise) if base else spread * noise
        out[name] = jnp.asarray(drawn.astype(out[name].dtype))
    for name, factor in factors.items():
        out[name] = (out[name] * factor).astype(out[name].dtype)
    return out
```

```python
from contextlib import ExitStack, contextmanager

import numpy as np

import concourse.bass as bass
from concourse import mybir

F32 = mybir.dt.float32
U8 = mybir.dt.uint8
U32 = mybir.dt.uint32
I32 = mybir.dt.int32
BF16 = mybir.dt.bfloat16
ALU = mybir.AluOpType
ACT = mybir.ActivationFunctionType
AX = mybir.AxisListType

P = 128
D = 128
S = 64
B = 128
T = B * S
TILES = T // P
HEADS = 16
HD = D // HEADS
GROUPS = 4
GH = HEADS // GROUPS
VW = 2 * (HD + 1)
EPS = 1e-5
MASKED = -1e9
LOWEST = -3e38

ATTENTIONS = ["L0_attn", "L0_xattn", "L1_attn", "L1_xattn", "L2_attn", "L2_xattn", "L3_attn", "L3_xattn", "L3_ffn"]
NA = len(ATTENTIONS)
CROSS = {"L0_xattn", "L1_xattn", "L2_xattn", "L3_xattn"}
SCALES = {a: HD ** -0.5 for a in ATTENTIONS}
SCALES["L1_xattn"] = 1.0
SCALES["L3_xattn"] = 1.0 / (float(np.float32(np.sqrt(np.float16(HD)))) + 1e-8)
OUT_BIAS = {"L0_attn", "L0_xattn", "L1_attn", "L2_xattn", "L3_attn", "L3_xattn"}
POST_NORM = {"L1_xattn": 0, "L3_xattn": 1}
BIASED = {"L0_xattn", "L1_attn", "L1_xattn", "L2_attn", "L3_xattn"}

C_ID, C_HEAD, C_CAUSAL, C_FUTURE, C_UPPER = 0, 128, 132, 196, 260
C_SLOT = 388
C_EIGHT = 397
C_CHUNK = 405
C_EARLIER = 533
C_TOKEN0 = 661
C_END = 725
ROUTE_SCALE = 2.5



def lasting_semaphores(k, new):
    k.loaded = new("loaded")
    k.made = new("made")
    k.stats_done = new("stats_done")
    k.mv_done = new("mv_done")
    k.var_done = new("var_done")
    k.rstd_done = new("rstd_done")
    k.xn_done = new("xn_done")
    k.held_done = new("held_done")
    k.xT_psum = new("xT_psum")
    k.xT_done = new("xT_done")
    k.qk_psum = new("qk_psum")
    k.q_done = new("q_done")
    k.k_done = new("k_done")
    k.v_done = new("v_done")
    k.s_psum = new("s_psum")
    k.max_done = new("max_done")
    k.sub_done = new("sub_done")
    k.exp_done = new("exp_done")
    k.pT_psum = new("pT_psum")
    k.pT_done = new("pT_done")
    k.o_psum = new("o_psum")
    k.inv_done = new("inv_done")
    k.on_done = new("on_done")
    k.bias_done = new("bias_done")
    k.oT_psum = new("oT_psum")
    k.oT_done = new("oT_done")
    k.y_psum = new("y_psum")
    k.res_done = new("res_done")
    k.lora_psum = new("lora_psum")
    k.f_stats = new("f_stats")
    k.f_mv = new("f_mv")
    k.f_var = new("f_var")
    k.f_rstd = new("f_rstd")
    k.f_xn = new("f_xn")
    k.f_xT_psum = new("f_xT_psum")
    k.f_xT = new("f_xT")
    k.biased_done = new("biased_done")
    k.maskadd_done = new("maskadd_done")
    k.post_sum = new("post_sum")
    k.post_stats_done = new("post_stats_done")
    k.post_mv_done = new("post_mv_done")
    k.post_var_done = new("post_var_done")
    k.post_rstd_done = new("post_rstd_done")
    k.post_scaled = new("post_scaled")
    k.post_gained = new("post_gained")
    k.post_shifted = new("post_shifted")
    k.post_done = new("post_done")
    k.z_stored = [new("z_stored0"), new("z_stored1")]
    k.z_loaded = [new("z_loaded0"), new("z_loaded1")]
    k.lora_done = new("lora_done")
    k.stored = new("stored")
    k.ctx_loaded = [new("ctx0"), new("ctx1")]
    k.guarded = new("guarded")
    k.sum_done = new("sum_done")
    k.v_guard = new("v_guard")
    k.src_done = new("src_done")


def relative_bias_semaphores(k, new):
    k.rel_in = new("rel_in")
    k.rel_T = new("rel_T")
    k.rel_out = new("rel_out")
    k.rel_rows = new("rel_rows")
    k.rel_sum = new("rel_sum")
    k.rel_masked = new("rel_masked")
    k.rel_psum = new("rel_psum")


def bitlinear_semaphores(k, new):
    k.bw_chain = new("bw_chain")
    k.bw_sum = new("bw_sum")
    k.bw_psum = new("bw_psum")
    k.b_up = new("b_up")
    k.b_silu = new("b_silu")
    k.b_hchain = new("b_hchain")
    k.b_hT_psum = new("b_hT_psum")
    k.b_hq_done = new("b_hq_done")
    k.b_qchain = new("b_qchain")
    k.b_xT_psum = new("b_xT_psum")
    k.b_xq_done = new("b_xq_done")
    k.b_scaled = new("b_scaled")
    k.b_down = new("b_down")
    k.b_hscaled = new("b_hscaled")
    k.b_res = new("b_res")
    k.b_gate = new("b_gate")
    k.b_xT = new("b_xT")
    k.b_hT = new("b_hT")
    k.bit_loaded = new("bit_loaded")


def dense_moe_semaphores(k, new):
    k.m_chain = new("m_chain")
    k.m_gate = new("m_gate")
    k.m_neg_done = new("m_neg_done")
    k.m_exp = new("m_exp")
    k.m_hidden = new("m_hidden")
    k.m_hT_psum = new("m_hT_psum")
    k.m_h_done = new("m_h_done")
    k.m_held = new("m_held")
    k.m_down = new("m_down")
    k.m_res = new("m_res")
    k.m_hT = new("m_hT")


def routed_semaphores(k, new):
    k.x_out_ready = [new("x_out0"), new("x_out1")]
    k.w_out_ready = [new("w_out0"), new("w_out1")]
    k.score_ready = new("score_ready")
    k.sig_ready = new("sig_ready")
    k.down_ready = new("down_ready")
    k.gated_ready = new("gated_ready")
    k.up_ready = new("up_ready")
    k.hidden_ready = new("hidden_ready")
    k.res_ready = new("res_ready")
    k.gate_ready = new("gate_ready")
    k.logit_ready = new("logit_ready")
    k.spill_ready = new("spill_ready")
    k.zero_ready = new("zero_ready")
    k.ends_ready = new("ends_ready")
    k.slotchain_ready = new("slotchain_ready")
    k.index_ready = new("index_ready")
    k.within_ready = new("within_ready")
    k.rows_ready = [new("rows0"), new("rows1")]
    k.tokenchain_ready = new("tokenchain_ready")
    k.reload_ready = new("reload_ready")
    k.pause_find = new("pause_find")
    k.pause_gather = new("pause_gather")
    k.pause_add = new("pause_add")


def small_experts_semaphores(k, new):
    k.r_chain = new("r_chain")
    k.r_cum = new("r_cum")
    k.r_cum_psum = new("r_cum_psum")
    k.e_y = new("e_y")
    k.e_index = new("e_index")
    k.e_xT_psum = new("e_xT_psum")
    k.e_col = new("e_col")
    k.e_scaled = new("e_scaled")
    k.e_added = new("e_added")
    k.e_sindex = new("e_sindex")
    k.e_sig = new("e_sig")
    k.e_gated = new("e_gated")
    k.e_h3 = new("e_h3")
    k.e_hid = new("e_hid")
    k.e_xT = new("e_xT")
    k.e_h1 = new("e_h1")
    k.e_w_ready = [new("e_w0"), new("e_w1")]
    k.e_x_ready = [new("e_x0"), new("e_x1")]


def large_experts_semaphores(k, new):
    k.r_scoreT = new("r_scoreT")
    k.r_logitT = new("r_logitT")
    k.c_io = new("c_io")
    k.c_zero = new("c_zero")
    k.c_chain = new("c_chain")
    k.c_psum = new("c_psum")
    k.c_chain2 = new("c_chain2")
    k.c_total = new("c_total")
    k.g_biased = new("g_biased")
    k.g_index = new("g_index")
    k.g_xT_psum = new("g_xT_psum")
    k.g_col = new("g_col")
    k.g_scaled = new("g_scaled")
    k.g_added = new("g_added")
    k.g_sindex = new("g_sindex")
    k.g_y = new("g_y")
    k.g_silu = new("g_silu")
    k.g_up = new("g_up")
    k.g_hid = new("g_hid")
    k.g_xT = new("g_xT")
    k.g_gate = new("g_gate")
    k.g_w_ready = [new("g_w0"), new("g_w1")]
    k.g_x_ready = [new("g_x0"), new("g_x1")]


class Kernel:
    pass


SUM_BACK = {"L1_xattn": 5, "L3_xattn": 4}


@contextmanager
def phase(k, *makers):
    handles = []
    k.phases += 1

    def new(name):
        handles.append(k.nc.alloc_semaphore(name=f"{name}_phase{k.phases}"))
        return handles[-1]
    for semaphores in makers:
        semaphores(k, new)
    yield
    k.nc.clear_and_free_semaphores(handles)
    k.nc.all_engine_barrier()


def depth_of(name):
    return SUM_BACK[name] + 2 if name in POST_NORM else 5


def tile_pipeline(eng, step, depth, count=TILES, unroll=2):
    lead = -(-depth // unroll) * unroll
    for it in range(lead):
        step(it, it % unroll, count)
    with eng.Fori(lead // unroll, count // unroll) as group:
        for u in range(unroll):
            step(unroll * group + u, u, None)
    for it in range(count, count + depth - 1):
        step(it, it % unroll, count)


def ends_free(it, par):
    return it - par + 2


def active(it, back, ends):
    return ends is None or 0 <= it - back < ends


def positive(value):
    return not isinstance(value, int) or value > 0



def attention_loads(k, sp, name, n):
    if name not in CROSS:
        return

    def step(it, par, ends):
        if active(it, 0, ends):
            if positive(k.before("cross", name) * TILES + it - 1):
                sp.wait_ge(k.src_done, k.before("cross", name) * TILES + it - 1)
            sp.dma_start(k.ctxT[:, par, :], k.d["ctxT"][:, bass.ds(it * P, P)]).then_inc(k.ctx_loaded[par], 16)
        if name == "L1_xattn" and active(it, 3, ends):
            sp.wait_ge(k.on_done, 2 * (n * TILES + it - 2))
            for b in range(2):
                sp.dma_start(k.z_dram[bass.ds((it - 3) * P + S * b, S), :]
                              .rearrange("s c -> (s c)").rearrange("(h q d) -> q h d", h=HEADS, d=HD),
                             k.o[S * b:S * b + S, 1 - par, :].rearrange("p (h d) -> p h d", d=HD)
                             ).then_inc(k.z_stored[1 - par], 16)
        if name == "L1_xattn" and active(it, 4, ends):
            sp.wait_ge(k.z_stored[par], 16 * (it - 2 - par))
            if ends is not None:
                if positive(2 * (k.before("post", name) * TILES + it - 5)):
                    sp.wait_ge(k.post_sum, 2 * (k.before("post", name) * TILES + it - 5))
            sp.dma_start(k.z[:, par, :], k.z_dram[bass.ds((it - 4) * P, P), :]).then_inc(k.z_loaded[par], 16)
    tile_pipeline(sp, step, depth_of(name))


def attention_pool(k, pool, name, n):
    nc = k.nc

    def step(it, par, ends):
        if active(it, 0, ends):
            g = n * TILES + it
            pool.wait_ge(k.var_done, g + 1)
            if positive(g - 1):
                pool.wait_ge(k.xn_done, g - 1)
            nc.gpsimd.tensor_tensor(k.rstd[:, par, 0:1], k.vareps[:, par, 0:1], k.half_power[:, 0:1],
                                    ALU.pow).then_inc(k.rstd_done, 1)
            if name in POST_NORM:
                pool.wait_ge(k.xn_done, g + 1)
                nc.gpsimd.tensor_copy(k.held[:, bass.ds(it * P, P)], k.xn[:, par, :]).then_inc(k.held_done, 1)
        back = SUM_BACK.get(name)
        if back and active(it, back, ends):
            q = k.before("post", name) * TILES + it - back
            buf = (par + back) % 2
            pool.wait_ge(k.post_var_done, q + 1)
            if positive(q - 1):
                pool.wait_ge(k.post_scaled, q - 1)
            nc.gpsimd.tensor_tensor(k.rstd[:, buf, 1:2], k.vareps[:, buf, 1:2], k.half_power[:, 0:1],
                                    ALU.pow).then_inc(k.post_rstd_done, 1)
    tile_pipeline(pool, step, depth_of(name))


def attention_pe(k, pe, name, n):
    nc = k.nc
    w = k.attn_w[:, ATTENTIONS.index(name), :, :]
    wq, wk, wv, wo = (w[:, m, :] for m in range(4))
    cross = name in CROSS
    project_out = name != "L1_xattn"

    def step(it, par, ends):
        if active(it, 4, ends) and project_out:
            g = n * TILES + it - 4
            pe.wait_ge(k.on_done, 2 * (g + 1))
            if positive(g):
                pe.wait_ge(k.res_done, g)
            if positive(g):
                pe.wait_ge(k.oT_done, g)
            if active(it, 2, ends):
                pe.wait_ge(k.xT_done, g + 3)
            nc.tensor.transpose(k.ps_oT, k.o[:, par, :], k.ident).then_inc(k.oT_psum, 1)
        elif active(it, 4, ends):
            pe.sem_inc(k.oT_psum, 1)
            pe.sem_inc(k.y_psum, 1)
        if active(it, 1, ends):
            g = n * TILES + it - 1
            pe.wait_ge(k.xn_done, g + 1)
            if positive(g - 3):
                pe.wait_ge(k.res_done, g - 3)
            if positive(g):
                pe.wait_ge(k.xT_done, g)
            nc.tensor.transpose(k.ps_xT, k.xn[:, 1 - par, :], k.ident).then_inc(k.xT_psum, 1)
        if active(it, 3, ends):
            g = n * TILES + it - 3
            pe.wait_ge(k.exp_done, g + 1)
            if positive(2 * g):
                pe.wait_ge(k.on_done, 2 * g)
            for half in range(2):
                if positive(2 * g + half - 1):
                    pe.wait_ge(k.pT_done, 2 * g + half - 1)
                for j in range(4):
                    mm = nc.tensor.transpose(k.ps_pT[:, half, j * P:(j + 1) * P],
                                             k.prob[:, 1 - par, (4 * half + j) * P:(4 * half + j + 1) * P], k.ident)
                mm.then_inc(k.pT_psum, 1)
        if active(it, 1, ends):
            g = n * TILES + it - 1
            pe.wait_ge(k.xT_done, g + 1)
            if positive(g):
                pe.wait_ge(k.q_done, g)
            if positive(g):
                pe.wait_ge(k.k_done, g)
            if positive(2 * g):
                pe.wait_ge(k.v_done, 2 * g)
            if cross:
                pe.wait_ge(k.src_done, k.before("cross", name) * TILES + it)
            src = k.srcT[:, 1 - par, :, 0, :]
            for b in range(2):
                twice = k.srcT[:, 1 - par, b, :, :].rearrange("p o s -> p (o s)")
                nc.tensor.matmul(k.ps_v[:, b, :], twice, wv, start=True, stop=True)
            nc.tensor.matmul(k.ps_q, wq, k.xnT[:, 1 - par, :] if cross else src, start=True, stop=True)
            nc.tensor.matmul(k.ps_k, wk, src, start=True, stop=True).then_inc(k.qk_psum, 1)
        if active(it, 4, ends) and project_out:
            g = n * TILES + it - 4
            pe.wait_ge(k.oT_done, g + 1)
            nc.tensor.matmul(k.ps_y, k.oT[:, par, :], wo, start=True, stop=True).then_inc(k.y_psum, 1)
        if active(it, 3, ends):
            g = n * TILES + it - 3
            pe.wait_ge(k.v_done, 2 * (g + 1))
            pe.wait_ge(k.pT_done, 2 * (g + 1))
            for j in range(HEADS // 2):
                mm = nc.tensor.matmul(k.ps_o[:, 2 * VW * j:2 * VW * (j + 1)], k.probT[:, 1 - par, j * P:(j + 1) * P],
                                      k.vblock[:, 1 - par, j, :, :].rearrange("p b c -> p (b c)"), start=True, stop=True)
            mm.then_inc(k.o_psum, 1)
        if active(it, 1, ends):
            g = n * TILES + it - 1
            pe.wait_ge(k.q_done, g + 1)
            pe.wait_ge(k.k_done, g + 1)
            if positive(g):
                pe.wait_ge(k.sub_done, g)
            for b in range(2):
                for q in range(GROUPS):
                    rows = slice(32 * q, 32 * q + 32)
                    mm = nc.tensor.matmul(
                        k.scores[S * b:S * b + S, q, 0:GH * S],
                        k.qT[rows, 1 - par, S * b:S * b + S],
                        k.kblock[rows, 1 - par, :, S * b:S * b + S],
                        start=True, stop=True, tile_position=(32 * q, S * b))
            mm.then_inc(k.s_psum, 1)
    tile_pipeline(pe, step, depth_of(name))


def attention_act(k, act, name, n):
    nc = k.nc

    def twice(ap):
        return ap.rearrange("p (b o s) -> p b o s", b=2, o=1).broadcast_to([P, 2, 2, S])

    def step(it, par, ends):
        if active(it, 1, ends):
            g = n * TILES + it - 1
            act.wait_ge(k.xT_psum, g + 1)
            if positive(g - 1):
                act.wait_ge(k.qk_psum, g - 1)
            if name == "L3_ffn":
                nc.scalar.activation(k.srcT[:, 1 - par, :, :, :], twice(k.ps_xT), ACT.Identity, scale=k.norm_cols[:, 0:1],
                                     bias=k.norm_cols[:, 1:2]).then_inc(k.xT_done, 1)
            elif name in CROSS:
                nc.scalar.activation(k.xnT[:, 1 - par, :], k.ps_xT, ACT.Copy).then_inc(k.xT_done, 1)
            else:
                nc.scalar.activation(k.srcT[:, 1 - par, :, :, :], twice(k.ps_xT), ACT.Copy).then_inc(k.xT_done, 1)
        if active(it, 4, ends) and name != "L1_xattn":
            g = n * TILES + it - 4
            act.wait_ge(k.oT_psum, g + 1)
            if positive(g - 1):
                act.wait_ge(k.y_psum, g - 1)
            nc.scalar.activation(k.oT[:, par, :], k.ps_oT, ACT.Copy).then_inc(k.oT_done, 1)
        elif active(it, 4, ends):
            act.sem_inc(k.oT_done, 1)
        if active(it, 3, ends):
            g = n * TILES + it - 3
            if positive(g - 1):
                act.wait_ge(k.o_psum, g - 1)
            for half in range(2):
                act.wait_ge(k.pT_psum, 2 * g + half + 1)
                nc.scalar.activation(k.probT[:, 1 - par, half * 512:half * 512 + 512], k.ps_pT[:, half, :],
                                     ACT.Copy).then_inc(k.pT_done, 1)
        if active(it, 2, ends):
            g = n * TILES + it - 2
            act.wait_ge(k.sub_done, g + 1)
            if name != "L3_xattn":
                nc.scalar.activation(k.prob[:, par, :], k.prob[:, par, :], ACT.Exp).then_inc(k.exp_done, 1)
            else:
                act.sem_inc(k.exp_done, 1)
        if active(it, 0, ends) and name in CROSS:
            act.wait_ge(k.ctx_loaded[par], 8 * (k.before("cross", name) * TILES + ends_free(it, par)))
            if positive(n * TILES + it - 1):
                act.wait_ge(k.qk_psum, n * TILES + it - 1)
            nc.scalar.activation(k.srcT[:, par, :, :, :], twice(k.ctxT[:, par, :]), ACT.Copy).then_inc(k.src_done, 1)
    tile_pipeline(act, step, depth_of(name))


def attention_dve(k, dve, name, n):
    nc = k.nc
    a = ATTENTIONS.index(name)
    scale = SCALES[name]
    scores = k.scores[:, :, 0:GH * S]
    heads4 = scores.rearrange("p g (h s) -> p g h s", h=GH)
    colmask = k.consts[:, C_HEAD:C_HEAD + GH]
    softmax = name != "L3_xattn"
    back = SUM_BACK.get(name)
    stream = k.held if name == "L3_ffn" else k.x

    def post_norm_stats(t, buf, g):
        q = k.before("post", name) * TILES + t
        post, src = k.post[:, buf, :], k.held[:, bass.ds(t * P, P)]
        dve.wait_ge(k.held_done, q + 1)
        if positive(q - 1):
            dve.wait_ge(k.post_done, q - 1)
        if name == "L1_xattn":
            dve.wait_ge(k.z_loaded[buf], 8 * (t - buf + 2))
            nc.vector.tensor_tensor(post, k.z[:, buf, :], src, ALU.add).then_inc(k.post_sum, 2)
        else:
            nc.vector.tensor_tensor(post, src, k.bo[:, a, :], ALU.add).then_inc(k.post_sum, 1)
            dve.wait_ge(k.post_sum, 2 * q + 1)
            dve.wait_ge(k.y_psum, g + 1)
            nc.vector.tensor_tensor(post, post, k.ps_y, ALU.add).then_inc(k.post_sum, 1)
            dve.wait_ge(k.post_sum, 2 * (q + 1))
            dve.sem_inc(k.res_done, 1)
        dve.wait_ge(k.post_sum, 2 * (q + 1))
        nc.vector.bn_stats(k.post_stats[:, buf, :], post).then_inc(k.post_stats_done, 1)
        dve.wait_ge(k.post_stats_done, q + 1)
        nc.vector.memset(k.pause[:, 1:2], 0.0)
        nc.vector.bn_aggr(k.post_meanvar[:, buf, 0:2], k.post_stats[:, buf, :]).then_inc(k.post_mv_done, 1)
        dve.wait_ge(k.post_mv_done, q + 1)
        nc.vector.tensor_scalar(k.vareps[:, buf, 1:2], k.post_meanvar[:, buf, 1:2], EPS, None,
                                ALU.add).then_inc(k.post_var_done, 1)

    def post_norm_finish(t, buf):
        q = k.before("post", name) * TILES + t
        post, xt = k.post[:, buf, :], k.x[:, bass.ds(t * P, P)]
        m = POST_NORM[name]
        dve.wait_ge(k.post_rstd_done, q + 1)
        nc.vector.tensor_scalar(post, post, k.post_meanvar[:, buf, 0:1], k.rstd[:, buf, 1:2], ALU.subtract,
                                ALU.mult).then_inc(k.post_scaled, 1)
        dve.wait_ge(k.post_scaled, q + 1)
        nc.vector.tensor_tensor(post, post, k.post_gain[:, 2 * m, :], ALU.mult).then_inc(k.post_gained, 1)
        nc.vector.tensor_tensor(xt, xt, k.post_gain[:, 2 * m + 1, :], ALU.add).then_inc(k.post_shifted, 1)
        dve.wait_ge(k.post_gained, q + 1)
        dve.wait_ge(k.post_shifted, q + 1)
        nc.vector.tensor_tensor(xt, xt, post, ALU.add).then_inc(k.post_done, 1)

    def step(it, par, ends):
        if active(it, 0, ends):
            g = n * TILES + it
            if positive(g):
                dve.wait_ge(k.xn_done, g)
            nc.vector.bn_stats(k.stats[:, par, :], stream[:, bass.ds(it * P, P)]).then_inc(k.stats_done, 1)
            dve.wait_ge(k.stats_done, g + 1)
            nc.vector.memset(k.pause[:, 0:1], 0.0)
            nc.vector.bn_aggr(k.meanvar[:, par, 0:2], k.stats[:, par, :]).then_inc(k.mv_done, 1)
            dve.wait_ge(k.mv_done, g + 1)
            nc.vector.tensor_scalar(k.vareps[:, par, 0:1], k.meanvar[:, par, 1:2], EPS, None,
                                    ALU.add).then_inc(k.var_done, 1)
        if active(it, 2, ends):
            g = n * TILES + it - 2
            prob4 = k.prob[:, par, :].rearrange("p (g h s) -> p g h s", g=GROUPS, h=GH)
            rowmax = k.rowmax[:, par, :]
            dve.wait_ge(k.s_psum, g + 1)
            if name in BIASED:
                if positive(2 * (g - 1)):
                    dve.wait_ge(k.pT_psum, 2 * (g - 1))
                if name == "L1_xattn":
                    biased = nc.vector.tensor_scalar(prob4, heads4, LOWEST, None, ALU.max)
                else:
                    if name == "L1_attn":
                        add = k.relpos[:, :].rearrange("p (g h s) -> p g h s", g=GROUPS, h=GH)
                    else:
                        if name == "L3_xattn":
                            dve.wait_ge(k.maskadd_done, it - 1)
                            add = k.maskadd[:, par, :]
                        else:
                            c = C_CAUSAL if name == "L0_xattn" else C_FUTURE
                            add = k.consts[:, c:c + S]
                        add = add.rearrange("p (g h s) -> p g h s", g=1, h=1).broadcast_to([P, GROUPS, GH, S])
                    biased = nc.vector.tensor_tensor(prob4, heads4, add, ALU.add)
                biased.then_inc(k.biased_done, 1)
                dve.wait_ge(k.biased_done, k.before("biased", name) * TILES + it - 1)
            if softmax:
                nc.vector.tensor_reduce(rowmax.rearrange("p (g h) -> p g h", g=GROUPS),
                                        prob4 if name in BIASED else heads4, AX.X, ALU.max).then_inc(k.max_done, 1)
            if name == "L1_xattn":
                dve.wait_ge(k.max_done, g + 1)
                nc.vector.tensor_scalar(rowmax, rowmax, LOWEST / 3, None, ALU.max).then_inc(k.guarded, 1)
        if active(it, 0, ends):
            g = n * TILES + it
            dve.wait_ge(k.rstd_done, g + 1)
            if positive(g - 1):
                dve.wait_ge(k.xT_psum, g - 1)
            nc.vector.tensor_scalar(k.xn[:, par, :], stream[:, bass.ds(it * P, P)], k.meanvar[:, par, 0:1],
                                    k.rstd[:, par, 0:1], ALU.subtract, ALU.mult).then_inc(k.xn_done, 1)
        if active(it, 2, ends):
            g = n * TILES + it - 2
            if softmax:
                dve.wait_ge(k.max_done, g + 1)
                if name == "L1_xattn":
                    dve.wait_ge(k.guarded, it - 1)
                if positive(2 * (g - 1)):
                    dve.wait_ge(k.pT_psum, 2 * (g - 1))
                nc.vector.tensor_tensor(
                    prob4, prob4 if name in BIASED else heads4,
                    rowmax.rearrange("p (g h o) -> p g h o", g=GROUPS, o=1)
                          .broadcast_to([P, GROUPS, GH, S]), ALU.subtract).then_inc(k.sub_done, 1)
            else:
                dve.sem_inc(k.max_done, 1)
                dve.sem_inc(k.sub_done, 1)
        if active(it, 1, ends):
            g = n * TILES + it - 1
            dve.wait_ge(k.qk_psum, g + 1)
            if positive(g - 1):
                dve.wait_ge(k.s_psum, g - 1)
            nc.vector.scalar_tensor_tensor(
                k.kblock[:, 1 - par, :, :], k.ps_k.rearrange("p (o s) -> p o s", o=1).broadcast_to([P, GH, P]),
                k.bqk[:, a, 1:2], colmask.rearrange("p (h o) -> p h o", o=1).broadcast_to([P, GH, P]),
                ALU.add, ALU.mult).then_inc(k.k_done, 1)
            nc.vector.tensor_scalar(k.qT[:, 1 - par, :], k.ps_q, k.bqk[:, a, 0:1], scale, ALU.add,
                                    ALU.mult).then_inc(k.q_done, 1)
        if active(it, 4, ends) and name not in POST_NORM:
            g = n * TILES + it - 4
            xt = stream[:, bass.ds((it - 4) * P, P)]
            if name in OUT_BIAS:
                nc.vector.tensor_tensor(xt, xt, k.bo[:, a, :], ALU.add).then_inc(k.bias_done, 1)
                dve.wait_ge(k.bias_done, k.before("out", name) * TILES + it - 3)
            dve.wait_ge(k.y_psum, g + 1)
            nc.vector.tensor_tensor(xt, xt, k.ps_y, ALU.add).then_inc(k.res_done, 1)
        if back and active(it, back, ends):
            post_norm_stats(it - back, (par + back) % 2, n * TILES + it - back)
        if name == "L1_xattn" and active(it, 4, ends):
            dve.sem_inc(k.res_done, 1)
        if active(it, 3, ends):
            g = n * TILES + it - 3
            mix = 1 - par
            dve.wait_ge(k.o_psum, g + 1)
            if positive(g - 1):
                dve.wait_ge(k.oT_psum, g - 1)
            if name == "L1_xattn":
                if positive(16 * (it - 4 + par)):
                    dve.wait_ge(k.z_stored[mix], 16 * (it - 4 + par))
            own = []
            for b in range(2):
                rows = slice(S * b, S * b + S)
                psum = k.ps_o[rows, :].rearrange("p (j b h c) -> p j b h c", j=HEADS // 2, b=2, h=2)[:, :, b, :, :]
                out = k.o[rows, mix, :].rearrange("p (j h d) -> p j h d", h=2, d=HD)
                sums = k.rowinv[rows, mix, :].rearrange("p (j h o) -> p j h o", h=2, o=1)
                own.append((psum, out, sums))
            if softmax:
                for psum, out, sums in own:
                    if name == "L1_xattn":
                        nc.vector.tensor_scalar(sums, psum[:, :, :, HD:HD + 1], 1e-30, None,
                                                ALU.max).then_inc(k.sum_done, 1)
                    else:
                        nc.vector.reciprocal(sums, psum[:, :, :, HD:HD + 1]).then_inc(k.inv_done, 1)
                if name == "L1_xattn":
                    dve.wait_ge(k.sum_done, 2 * (it - 2))
                    nc.vector.reciprocal(k.rowinv[:, mix, :], k.rowinv[:, mix, :]).then_inc(k.inv_done, 2)
                dve.wait_ge(k.inv_done, 2 * (g + 1))
                for psum, out, sums in own:
                    nc.vector.tensor_tensor(out, psum[:, :, :, 0:HD], sums.broadcast_to([S, HEADS // 2, 2, HD]),
                                            ALU.mult).then_inc(k.on_done, 1)
            else:
                dve.sem_inc(k.inv_done, 2)
                for psum, out, sums in own:
                    nc.vector.tensor_copy(out, psum[:, :, :, 0:HD]).then_inc(k.on_done, 1)
        if active(it, 1, ends):
            g = n * TILES + it - 1
            dve.wait_ge(k.qk_psum, g + 1)
            if positive(g - 1):
                dve.wait_ge(k.o_psum, g - 1)
            value, bias = k.ps_v, k.bv[:, a, :].rearrange("p (o c) -> p o c", o=1).broadcast_to([P, 2, D])
            if name == "L1_xattn":
                if positive(2 * g):
                    dve.wait_ge(k.v_done, 2 * g)
                nc.vector.tensor_tensor(k.v_low[:, :, :], value, bias, ALU.add).then_inc(k.v_guard, 1)
                dve.wait_ge(k.v_guard, 3 * it - 2)
                nc.vector.tensor_scalar(k.v_high[:, :, :], k.v_low[:, :, :], 0.0, None, ALU.max).then_inc(k.v_guard, 1)
                dve.wait_ge(k.v_guard, 3 * it - 1)
                nc.vector.tensor_scalar(k.v_low[:, :, :], k.v_low[:, :, :], 0.0, None, ALU.min).then_inc(k.v_guard, 1)
                dve.wait_ge(k.v_guard, 3 * it)
                value, bias = k.v_low, k.v_high[:, :, :]
            for odd in range(2):
                rows = slice(S * odd, S * odd + S)
                v, add = (t[rows, :, :].rearrange("p b (j e d) -> p b j e d", e=2, d=HD)[:, :, :, odd, :]
                          for t in (value, bias))
                out = k.vblock[rows, 1 - par, :, :, (HD + 1) * odd:(HD + 1) * odd + HD].rearrange("p j b d -> p b j d")
                nc.vector.tensor_tensor(out, v, add, ALU.add).then_inc(k.v_done, 1)
            if name == "L3_xattn":
                if positive(k.before("biased", name) * TILES + it - 2):
                    dve.wait_ge(k.biased_done, k.before("biased", name) * TILES + it - 2)
                mask = k.mask_raw[:, bass.ds((it - 1) * (S // 4), S // 4)].bitcast(U8)
                nc.vector.tensor_scalar(k.maskadd[:, 1 - par, :], mask, LOWEST, -LOWEST, ALU.mult,
                                        ALU.mult).then_inc(k.maskadd_done, 1)
        if back and active(it, back + 1, ends):
            post_norm_finish(it - back - 1, (par + back + 1) % 2)
    tile_pipeline(dve, step, depth_of(name))


def relative_bias(k, ps):
    nc, emb, table, tableT = k.nc, k.rel_emb, k.rel_table, k.rel_tableT
    with nc.Block() as block:
        @block.sync
        def _(sp):
            sp.dma_start(emb[:, :, :], k.d["rel_rev"].rearrange("(a p) c -> p a c", p=P)).then_inc(k.rel_in, 16)
            sp.wait_ge(k.rel_T, 1)
            sp.dma_start(k.rel_dram, tableT[:, :]).then_inc(k.rel_out, 16)
            sp.wait_ge(k.rel_out, 16)
            for b in range(2):
                for q in range(S):
                    p = S * b + q
                    sp.dma_start(k.relpos[p:p + 1, :].rearrange("p (h s) -> p h s", h=HEADS),
                                 k.rel_dram[:, P - 1 - q:P - 1 - q + S].rearrange("h (o s) -> o h s", o=1)
                                 ).then_inc(k.rel_rows, 16)
            sp.wait_ge(k.rel_rows, 16 * P)

        @block.vector
        def _(dve):
            dve.wait_ge(k.rel_in, 16)
            nc.vector.tensor_reduce(table[:, :, :], emb[:, :, :].rearrange("p a (h d) -> p a h d", d=HD), AX.X,
                                    ALU.add).then_inc(k.rel_sum, 1)
            dve.wait_ge(k.rel_rows, 16 * P)
            future = k.consts[:, C_FUTURE:C_FUTURE + S].rearrange("p (o s) -> p o s", o=1).broadcast_to([P, HEADS, S])
            bias = k.relpos[:, :].rearrange("p (h s) -> p h s", h=HEADS)
            nc.vector.tensor_tensor(bias, bias, future, ALU.add).then_inc(k.rel_masked, 1)
            dve.wait_ge(k.rel_masked, 1)

        @block.tensor
        def _(pe):
            pe.wait_ge(k.rel_sum, 1)
            for a in range(2):
                nc.tensor.transpose(ps[0:HEADS, 1, a * P:(a + 1) * P], table[:, a, :],
                                    k.ident).then_inc(k.rel_psum, 1)

        @block.scalar
        def _(act):
            act.wait_ge(k.rel_psum, 2)
            nc.scalar.activation(tableT[:, :], ps[0:HEADS, 1, 0:2 * P], ACT.Copy).then_inc(k.rel_T, 1)



def front_dve_stats(k, dve, m, stream, it, par):
    nc, g = k.nc, m * TILES + it
    if positive(g - 1):
        dve.wait_ge(k.f_xn, g - 1)
    nc.vector.bn_stats(k.stats[:, par, :], stream[:, bass.ds(it * P, P)]).then_inc(k.f_stats, 1)
    dve.wait_ge(k.f_stats, g + 1)
    nc.vector.memset(k.pause[:, 0:1], 0.0)
    nc.vector.bn_aggr(k.meanvar[:, par, 0:2], k.stats[:, par, :]).then_inc(k.f_mv, 1)
    dve.wait_ge(k.f_mv, g + 1)
    nc.vector.tensor_scalar(k.vareps[:, par, 0:1], k.meanvar[:, par, 1:2], EPS, None, ALU.add).then_inc(k.f_var, 1)


def front_pool(k, pool, m, it, par):
    nc, g = k.nc, m * TILES + it
    pool.wait_ge(k.f_var, g + 1)
    if positive(g - 1):
        pool.wait_ge(k.f_xn, g - 1)
    nc.gpsimd.tensor_tensor(k.rstd[:, par, 0:1], k.vareps[:, par, 0:1], k.half_power[:, 0:1],
                            ALU.pow).then_inc(k.f_rstd, 1)


def front_dve_norm(k, dve, m, stream, it, par, out):
    nc, g = k.nc, m * TILES + it
    dve.wait_ge(k.f_rstd, g + 1)
    nc.vector.tensor_scalar(out, stream[:, bass.ds(it * P, P)], k.meanvar[:, par, 0:1], k.rstd[:, par, 0:1],
                            ALU.subtract, ALU.mult).then_inc(k.f_xn, 1)


def pool_pause(k, pool, done, column, t):
    if positive(t):
        pool.wait_ge(done, t)
    k.nc.gpsimd.tensor_tensor(k.pause[:, column:column + 1], k.half_power[:, 0:1], k.half_power[:, 0:1],
                              ALU.add).then_inc(done, 1)


class Count:

    def __init__(self, tile, length):
        self.before, self.length, self.passed = tile * length, length, 0

    def next(self):
        self.passed += 1
        assert self.passed <= self.length
        return self.before + self.passed


def prenorm_pass(k, m):
    nc = k.nc
    with nc.Block() as block:
        @block.vector
        def _(dve):
            def step(it, par, ends):
                if active(it, 0, ends):
                    front_dve_stats(k, dve, m, k.x, it, par)
                if active(it, 1, ends):
                    front_dve_norm(k, dve, m, k.x, it - 1, 1 - par, k.held[:, bass.ds((it - 1) * P, P)])
            tile_pipeline(dve, step, 2)
            dve.wait_ge(k.f_xn, (m + 1) * TILES)

        @block.gpsimd
        def _(pool):
            tile_pipeline(pool, lambda it, par, ends: front_pool(k, pool, m, it, par) if active(it, 0, ends) else None, 2)


MAGIC = 1.5 * 2.0 ** 23
INNER = 512
QMAX = 127.0


def bitlinear_weights(k, ps):
    nc = k.nc
    with nc.Block() as block:
        @block.sync
        def _(sp):
            sp.dma_start(k.bit_raw, k.d["bit_w"]).then_inc(k.bit_loaded, 16)

        @block.vector
        def _(dve):
            dve.wait_ge(k.bit_loaded, 16)
            count = Count(0, 99)
            for w in range(3):
                raw = k.bit_raw[:, w, :]
                nc.vector.tensor_reduce(k.bit_sum[:, w:w + 1], raw, AX.X, ALU.add, apply_absolute_value=True).then_inc(k.bw_chain, 1)
                dve.wait_ge(k.bw_chain, count.next())
            nc.vector.tensor_copy(k.ident_bf[:, :], k.ident).then_inc(k.bw_sum, 1)
            dve.wait_ge(k.bw_psum, 1)
            nc.vector.tensor_scalar(k.bit_mean[:, 0:3], ps[:, 0, 0:3], 1.0 / (INNER * D), 1e-5, ALU.mult, ALU.max).then_inc(k.bw_chain, 1)
            dve.wait_ge(k.bw_chain, count.next())
            nc.vector.reciprocal(k.bit_inv[:, 0:3], k.bit_mean[:, 0:3]).then_inc(k.bw_chain, 1)
            dve.wait_ge(k.bw_chain, count.next())
            nc.vector.tensor_scalar(k.bit_mean[:, 0:3], k.bit_mean[:, 0:3], 1.0 / QMAX, None, ALU.mult).then_inc(k.bw_chain, 1)
            dve.wait_ge(k.bw_chain, count.next())
            for w in range(3):
                raw = k.bit_raw[:, w, :]
                nc.vector.tensor_scalar(raw, raw, k.bit_inv[:, w:w + 1], MAGIC, ALU.mult, ALU.add).then_inc(k.bw_chain, 1)
                dve.wait_ge(k.bw_chain, count.next())
                nc.vector.tensor_scalar(raw, raw, MAGIC, 1.0, ALU.subtract, ALU.min).then_inc(k.bw_chain, 1)
                dve.wait_ge(k.bw_chain, count.next())
                nc.vector.tensor_scalar(k.bit_w[:, w, :], raw, -1.0, None, ALU.max).then_inc(k.bw_chain, 1)
                dve.wait_ge(k.bw_chain, count.next())

        @block.tensor
        def _(pe):
            pe.wait_ge(k.bw_sum, 1)
            pe.wait_ge(k.bw_chain, 3)
            nc.tensor.matmul(ps[:, 0, 0:3], k.ones[:, :], k.bit_sum[:, 0:3], start=True, stop=True).then_inc(k.bw_psum, 1)


def bitlinear_pass(k, ps, m):
    nc = k.nc
    QL, HL = 5, 6

    def quantise(dve, chained, count, src, amax, inv, out, scratch):
        nc.vector.tensor_reduce(amax, src, AX.X, ALU.max, apply_absolute_value=True).then_inc(chained, 1)
        dve.wait_ge(chained, count.next())
        nc.vector.tensor_scalar(amax, amax, 1e-5, None, ALU.max).then_inc(chained, 1)
        dve.wait_ge(chained, count.next())
        nc.vector.reciprocal(inv, amax).then_inc(chained, 1)
        dve.wait_ge(chained, count.next())
        nc.vector.tensor_scalar(inv, inv, QMAX, None, ALU.mult).then_inc(chained, 1)
        dve.wait_ge(chained, count.next())
        nc.vector.tensor_scalar(scratch, src, inv, MAGIC, ALU.mult, ALU.add).then_inc(chained, 1)
        dve.wait_ge(chained, count.next())
        return nc.vector.tensor_scalar(out, scratch, MAGIC, QMAX, ALU.subtract, ALU.min)

    with nc.Block() as block:
        @block.gpsimd
        def _(pool):
            tile_pipeline(pool, lambda it, par, ends: front_pool(k, pool, m, it, par) if active(it, 0, ends) else None, 4)

        @block.vector
        def _(dve):
            def step(it, par, ends):
                if active(it, 0, ends):
                    front_dve_stats(k, dve, m, k.x, it, par)
                if active(it, 2, ends):
                    t, b = it - 2, par
                    dve.wait_ge(k.b_up, t + 1)
                    dve.wait_ge(k.b_silu, t + 1)
                    count = Count(t, HL)
                    nc.vector.scalar_tensor_tensor(k.b_h[:, b, :], ps[:, 2 + b, :], k.b_scale[:, b, 1:2],
                                                   k.b_h[:, b, :], ALU.mult, ALU.mult).then_inc(k.b_hchain, 1)
                    dve.wait_ge(k.b_hchain, count.next())
                    if positive(t - 1):
                        dve.wait_ge(k.b_hT_psum, t - 1)
                    quantise(dve, k.b_hchain, count, k.b_h[:, b, :], k.b_hmax[:, b, 0:1], k.b_hmax[:, b, 1:2], k.b_hq[:, b, :],
                             k.b_h[:, b, :]).then_inc(k.b_hq_done, 1)
                if active(it, 0, ends):
                    front_dve_norm(k, dve, m, k.x, it, par, k.xn[:, par, :])
                    dve.wait_ge(k.f_xn, m * TILES + it + 1)
                    count = Count(it, QL)
                    if positive(it - 1):
                        dve.wait_ge(k.b_xT_psum, it - 1)
                    q = quantise(dve, k.b_qchain, count, k.xn[:, par, :], k.b_xmax[:, par, 0:1], k.b_xmax[:, par, 1:2],
                                 k.b_xq[:, par, :], k.xn[:, par, :])
                    q.then_inc(k.b_xq_done, 1)
                    if positive(it - 1):
                        dve.wait_ge(k.b_silu, it - 1)
                    nc.vector.tensor_scalar(k.b_scale[:, par, 0:2], k.bit_mean[:, 0:2], k.b_xmax[:, par, 0:1], None,
                                            ALU.mult).then_inc(k.b_scaled, 1)
                if active(it, 3, ends):
                    t, b = it - 3, 1 - par
                    dve.wait_ge(k.b_down, t + 1)
                    nc.vector.tensor_scalar(k.b_hmax[:, b, 2:3], k.b_hmax[:, b, 0:1], k.bit_mean[:, 2:3], None,
                                            ALU.mult).then_inc(k.b_hscaled, 1)
                    dve.wait_ge(k.b_hscaled, t + 1)
                    xt = k.x[:, bass.ds(t * P, P)]
                    nc.vector.scalar_tensor_tensor(xt, ps[:, 6, 0:P], k.b_hmax[:, b, 2:3], xt, ALU.mult,
                                                   ALU.add).then_inc(k.b_res, 1)
            tile_pipeline(dve, step, 4)

        @block.tensor
        def _(pe):
            def step(it, par, ends):
                if active(it, 1, ends):
                    t, b = it - 1, 1 - par
                    pe.wait_ge(k.b_xT, t + 1)
                    if positive(t - 1):
                        pe.wait_ge(k.b_silu, t - 1)
                    nc.tensor.matmul(ps[:, b, :], k.b_xqT[:, b, :], k.bit_w[:, 0, :], start=True,
                                     stop=True).then_inc(k.b_gate, 1)
                    if positive(HL * (t - 2) + HL):
                        pe.wait_ge(k.b_hchain, HL * (t - 2) + HL)
                    nc.tensor.matmul(ps[:, 2 + b, :], k.b_xqT[:, b, :], k.bit_w[:, 1, :], start=True,
                                     stop=True).then_inc(k.b_up, 1)
                if active(it, 0, ends):
                    pe.wait_ge(k.b_xq_done, it + 1)
                    if positive(it):
                        pe.wait_ge(k.b_xT, it)
                    nc.tensor.transpose(ps[:, 4, 0:P // 2].bitcast(BF16), k.b_xq[:, par, :],
                                        k.ident_bf[:, :]).then_inc(k.b_xT_psum, 1)
                if active(it, 2, ends):
                    t, b = it - 2, par
                    pe.wait_ge(k.b_hq_done, t + 1)
                    if positive(t):
                        pe.wait_ge(k.b_hT, t)
                    hT = ps[:, 5, 0:INNER // 2].bitcast(BF16)
                    for c in range(4):
                        mm = nc.tensor.transpose(hT[:, c * P:(c + 1) * P], k.b_hq[:, b, c * P:(c + 1) * P],
                                                 k.ident_bf[:, :])
                    mm.then_inc(k.b_hT_psum, 1)
                    pe.wait_ge(k.b_hT, t + 1)
                    if positive(t):
                        pe.wait_ge(k.b_res, t)
                    for c in range(4):
                        mm = nc.tensor.matmul(ps[:, 6, 0:P], k.b_hqT[:, b, c * P:(c + 1) * P],
                                              k.bit_w[:, 2, c * P:(c + 1) * P], start=c == 0, stop=c == 3)
                    mm.then_inc(k.b_down, 1)
            tile_pipeline(pe, step, 4)

        @block.scalar
        def _(act):
            def step(it, par, ends):
                if active(it, 0, ends):
                    act.wait_ge(k.b_xT_psum, it + 1)
                    if positive(it - 1):
                        act.wait_ge(k.b_up, it - 1)
                    nc.scalar.activation(k.b_xqT[:, par, :], ps[:, 4, 0:P // 2].bitcast(BF16), ACT.Copy).then_inc(k.b_xT, 1)
                if active(it, 1, ends):
                    t, b = it - 1, 1 - par
                    act.wait_ge(k.b_gate, t + 1)
                    act.wait_ge(k.b_scaled, t + 1)
                    if positive(t - 1):
                        act.wait_ge(k.b_hq_done, t - 1)
                    nc.scalar.activation(k.b_h[:, b, :], ps[:, b, :], ACT.Silu, scale=k.b_scale[:, b, 0:1]).then_inc(k.b_silu, 1)
                if active(it, 2, ends):
                    t, b = it - 2, par
                    act.wait_ge(k.b_hT_psum, t + 1)
                    if positive(t - 1):
                        act.wait_ge(k.b_down, t - 1)
                    nc.scalar.activation(k.b_hqT[:, b, :], ps[:, 5, 0:INNER // 2].bitcast(BF16), ACT.Copy).then_inc(k.b_hT, 1)
            tile_pipeline(act, step, 4)


ME = 8
MH = 64


def dense_moe_pass(k, ps, m):
    nc = k.nc
    GL = 8

    with nc.Block() as block:
        @block.gpsimd
        def _(pool):
            tile_pipeline(pool, lambda it, par, ends: front_pool(k, pool, m, it, par) if active(it, 0, ends) else None, 3)

        @block.vector
        def _(dve):
            def step(it, par, ends):
                if active(it, 0, ends):
                    front_dve_stats(k, dve, m, k.held, it, par)
                    if positive(k.tf(m) * TILES + it - 1):
                        dve.wait_ge(k.f_xT_psum, k.tf(m) * TILES + it - 1)
                    front_dve_norm(k, dve, m, k.held, it, par, k.xn[:, par, :])
                if active(it, 1, ends):
                    t, b = it - 1, 1 - par
                    count = Count(t, GL)
                    dve.wait_ge(k.m_gate, t + 1)
                    nc.vector.tensor_copy(k.m_logit[:, b, :], ps[:, 2, 0:ME]).then_inc(k.m_chain, 1)
                    dve.wait_ge(k.m_chain, count.next())
                    nc.vector.memset(k.pause[:, 0:1], 0.0)
                    nc.vector.max(k.m_top[:, b, :], k.m_logit[:, b, :]).then_inc(k.m_chain, 1)
                    dve.wait_ge(k.m_chain, count.next())
                    nc.vector.memset(k.pause[:, 0:1], 0.0)
                    nc.vector.max_index(k.m_place[:, b, :], k.m_top[:, b, :], k.m_logit[:, b, :]).then_inc(k.m_chain, 1)
                    dve.wait_ge(k.m_chain, count.next())
                    nc.vector.tensor_scalar(k.m_neg[:, b, :], k.m_top[:, b, 0:1], -1.0, None,
                                            ALU.mult).then_inc(k.m_neg_done, 1)
                    nc.vector.tensor_tensor(
                   k.m_eq[:, b, :, :],
                   k.m_place[:, b, 0:2].rearrange("p (o j) -> p o j", o=1).broadcast_to([P, ME, 2]),
                   k.consts[:, C_EIGHT:C_EIGHT + ME].rearrange("p (e o) -> p e o", o=1).broadcast_to([P, ME, 2]),
                   ALU.is_equal).then_inc(k.m_chain, 1)
                    dve.wait_ge(k.m_chain, count.next())
                    nc.vector.tensor_reduce(k.m_sel[:, b, :], k.m_eq[:, b, :, :], AX.X, ALU.add).then_inc(k.m_chain, 1)
                    dve.wait_ge(k.m_chain, count.next())
                    dve.wait_ge(k.m_exp, t + 1)
                    nc.vector.scalar_tensor_tensor(k.m_w[:, b, :], k.m_ex[:, b, :], 1.0, k.m_sel[:, b, :], ALU.mult,
                                                   ALU.mult, accum_out=k.m_sum[:, b, 0:1]).then_inc(k.m_chain, 1)
                    dve.wait_ge(k.m_chain, count.next())
                    nc.vector.reciprocal(k.m_sum[:, b, 1:2], k.m_sum[:, b, 0:1]).then_inc(k.m_chain, 1)
                    dve.wait_ge(k.m_chain, count.next())
                    nc.vector.tensor_scalar(k.m_w[:, b, :], k.m_w[:, b, :], k.m_sum[:, b, 1:2], None, ALU.mult).then_inc(k.m_chain, 1)
                    dve.wait_ge(k.m_chain, count.next())
                    dve.wait_ge(k.m_hidden, t + 1)
                    if positive(t - 1):
                        dve.wait_ge(k.m_hT_psum, t - 1)
                    nc.vector.scalar_tensor_tensor(
                        k.m_h[:, b, :].rearrange("p (e h) -> p e h", e=ME), ps[:, b, :].rearrange("p (e h) -> p e h", e=ME),
                        0.0, k.m_w[:, b, :].rearrange("p (e o) -> p e o", o=1).broadcast_to([P, ME, MH]), ALU.max,
                        ALU.mult).then_inc(k.m_h_done, 1)
                if active(it, 2, ends):
                    t = it - 2
                    xt = k.x[:, bass.ds(t * P, P)]
                    nc.vector.tensor_tensor(xt, xt, k.held[:, bass.ds(t * P, P)], ALU.add).then_inc(k.m_held, 1)
                    dve.wait_ge(k.m_down, t + 1)
                    dve.wait_ge(k.m_held, t + 1)
                    nc.vector.tensor_tensor(xt, xt, ps[:, 6, 0:P], ALU.add).then_inc(k.m_res, 1)
            tile_pipeline(dve, step, 3)

        @block.tensor
        def _(pe):
            def step(it, par, ends):
                if active(it, 0, ends):
                    f = k.tf(m) * TILES + it
                    pe.wait_ge(k.f_xn, m * TILES + it + 1)
                    if positive(f):
                        pe.wait_ge(k.f_xT, f)
                    nc.tensor.transpose(k.ps_xT, k.xn[:, par, :], k.ident).then_inc(k.f_xT_psum, 1)
                if active(it, 1, ends):
                    t, b = it - 1, 1 - par
                    pe.wait_ge(k.f_xT, k.tf(m) * TILES + t + 1)
                    if positive(GL * (t - 1) + 1):
                        pe.wait_ge(k.m_chain, GL * (t - 1) + 1)
                    nc.tensor.matmul(ps[:, 2, 0:ME], k.xnT[:, b, :], k.moe_gate[:, :], start=True, stop=True).then_inc(k.m_gate, 1)
                    if positive(t - 1):
                        pe.wait_ge(k.m_h_done, t - 1)
                    nc.tensor.matmul(ps[:, b, :], k.xnT[:, b, :], k.moe_w1[:, :], start=True, stop=True).then_inc(k.m_hidden, 1)
                if active(it, 2, ends):
                    t, b = it - 2, par
                    pe.wait_ge(k.m_h_done, t + 1)
                    if positive(t):
                        pe.wait_ge(k.m_hT, t)
                    for c in range(4):
                        mm = nc.tensor.transpose(ps[:, 4, c * P:(c + 1) * P], k.m_h[:, b, c * P:(c + 1) * P], k.ident)
                    mm.then_inc(k.m_hT_psum, 1)
                    pe.wait_ge(k.m_hT, t + 1)
                    if positive(t):
                        pe.wait_ge(k.m_res, t)
                    for c in range(4):
                        mm = nc.tensor.matmul(ps[:, 6, 0:P], k.m_hTs[:, b, c * P:(c + 1) * P], k.moe_w2[:, c, :],
                                              start=c == 0, stop=c == 3)
                    mm.then_inc(k.m_down, 1)
            tile_pipeline(pe, step, 3)

        @block.scalar
        def _(act):
            def step(it, par, ends):
                if active(it, 0, ends):
                    act.wait_ge(k.f_xT_psum, k.tf(m) * TILES + it + 1)
                    if positive(it - 1):
                        act.wait_ge(k.m_hidden, it - 1)
                    nc.scalar.activation(k.xnT[:, par, :], k.ps_xT, ACT.Identity, scale=k.norm_cols[:, 2:3],
                                         bias=k.norm_cols[:, 3:4]).then_inc(k.f_xT, 1)
                if active(it, 1, ends):
                    t, b = it - 1, 1 - par
                    act.wait_ge(k.m_neg_done, t + 1)
                    if positive(GL * (t - 2) + GL):
                        act.wait_ge(k.m_chain, GL * (t - 2) + GL)
                    nc.scalar.activation(k.m_ex[:, b, :], k.m_logit[:, b, :], ACT.Exp, bias=k.m_neg[:, b, :]).then_inc(k.m_exp, 1)
                if active(it, 2, ends):
                    t, b = it - 2, par
                    act.wait_ge(k.m_hT_psum, t + 1)
                    if positive(t - 1):
                        act.wait_ge(k.m_down, t - 1)
                    nc.scalar.activation(k.m_hTs[:, b, :], ps[:, 4, :], ACT.Copy).then_inc(k.m_hT, 1)
            tile_pipeline(act, step, 3)



class Routed:

    def __init__(self, name, experts, blocks, shared, scratch):
        self.name = name
        self.E = experts
        self.NB = blocks
        self.FC = shared // P
        self.TW = D + experts
        self.units = experts * blocks
        self.table = scratch["table"]


def shared_pass(k, ps, m, r):
    nc = k.nc
    E, FC = r.E, r.FC
    FW = FC * P
    choose = r.name == "L0_ffn"
    CL = 22 if choose else 0
    front = k.tf(m) * TILES
    w_tile = k.r_w if choose else k.r_score

    with nc.Block() as block:
        @block.gpsimd
        def _(pool):
            tile_pipeline(pool, lambda it, par, ends: front_pool(k, pool, m, it, par) if active(it, 0, ends) else None, 3)

        @block.sync
        def _(sp):
            def step(it, par, ends):
                if active(it, 0, ends):
                    sp.wait_ge(k.f_xn, m * TILES + it + 1)
                    sp.dma_start(r.table[bass.ds(it * P, P), 0:D], k.xn[:, par, :]).then_inc(k.x_out_ready[par], 16)
                if active(it, 1, ends):
                    t, b = it - 1, 1 - par
                    if choose:
                        sp.wait_ge(k.r_chain, CL * (t + 1))
                    else:
                        sp.wait_ge(k.score_ready, t + 1)
                    sp.dma_start(r.table[bass.ds(t * P, P), D:D + E], w_tile[:, b, 0:E]).then_inc(k.w_out_ready[b], 16)
            tile_pipeline(sp, step, 3)
            for p2 in range(2):
                sp.wait_ge(k.x_out_ready[p2], 8 * TILES)
                sp.wait_ge(k.w_out_ready[p2], 8 * TILES)

        @block.vector
        def _(dve):
            if choose:
                nc.vector.memset(k.r_carry[:, :], 0.0).then_inc(k.r_cum, 1)
                dve.wait_ge(k.r_cum, 1)

            def route(t, b):
                count = Count(t, CL)
                score, sfc = k.r_score[:, b, 0:E], k.r_sfc[:, b, :]
                dve.wait_ge(k.score_ready, t + 1)
                nc.vector.tensor_tensor(sfc, score, k.e_bias[:, :], ALU.add).then_inc(k.r_chain, 1)
                dve.wait_ge(k.r_chain, count.next())
                nc.vector.memset(k.pause[:, 0:1], 0.0)
                for g in range(8):
                    nc.vector.max(k.r_gmax[:, b, g, :], k.r_sfc[:, b, 8 * g:8 * g + 8]).then_inc(k.r_chain, 1)
                    after = count.next()
                    if g == 7:
                        dve.wait_ge(k.r_chain, after)
                nc.vector.tensor_tensor(k.r_gs[:, b, :].rearrange("p (g o) -> p g o", o=1), k.r_gmax[:, b, :, 0:1],
                                        k.r_gmax[:, b, :, 1:2], ALU.add).then_inc(k.r_chain, 1)
                dve.wait_ge(k.r_chain, count.next())
                nc.vector.memset(k.pause[:, 0:1], 0.0)
                nc.vector.max(k.r_gtop[:, b, :], k.r_gs[:, b, :]).then_inc(k.r_chain, 1)
                dve.wait_ge(k.r_chain, count.next())
                nc.vector.memset(k.pause[:, 0:1], 0.0)
                nc.vector.max_index(k.r_gplace[:, b, :], k.r_gtop[:, b, :], k.r_gs[:, b, :]).then_inc(k.r_chain, 1)
                dve.wait_ge(k.r_chain, count.next())
                nc.vector.tensor_tensor(
               k.r_geq[:, b, :, :],
               k.r_gplace[:, b, 0:4].rearrange("p (o j) -> p o j", o=1).broadcast_to([P, 8, 4]),
               k.consts[:, C_EIGHT:C_EIGHT + 8].rearrange("p (e o) -> p e o", o=1).broadcast_to([P, 8, 4]),
               ALU.is_equal).then_inc(k.r_chain, 1)
                dve.wait_ge(k.r_chain, count.next())
                nc.vector.tensor_reduce(k.r_gmask[:, b, :], k.r_geq[:, b, :, :], AX.X, ALU.add).then_inc(k.r_chain, 1)
                dve.wait_ge(k.r_chain, count.next())
                nc.vector.tensor_tensor(
               sfc.rearrange("p (g e) -> p g e", g=8), sfc.rearrange("p (g e) -> p g e", g=8),
               k.r_gmask[:, b, :].rearrange("p (g o) -> p g o", o=1).broadcast_to([P, 8, 8]), ALU.mult).then_inc(k.r_chain, 1)
                dve.wait_ge(k.r_chain, count.next())
                nc.vector.memset(k.pause[:, 0:1], 0.0)
                nc.vector.max(k.r_top[:, b, :], sfc).then_inc(k.r_chain, 1)
                dve.wait_ge(k.r_chain, count.next())
                nc.vector.memset(k.pause[:, 0:1], 0.0)
                nc.vector.match_replace(k.r_left[:, b, :], k.r_top[:, b, :], sfc, LOWEST).then_inc(k.r_chain, 1)
                dve.wait_ge(k.r_chain, count.next())
                if positive(t - 1):
                    dve.wait_ge(k.r_cum_psum, t - 1)
                nc.vector.tensor_tensor(k.r_sel[:, b, :], k.r_left[:, b, :], sfc, ALU.not_equal).then_inc(k.r_chain, 1)
                dve.wait_ge(k.r_chain, count.next())
                if positive(8 * (t - b)):
                    dve.wait_ge(k.w_out_ready[b], 8 * (t - b))
                nc.vector.scalar_tensor_tensor(k.r_w[:, b, :], score, 1.0, k.r_sel[:, b, :], ALU.mult, ALU.mult,
                                               accum_out=k.r_sum[:, b, 0:1]).then_inc(k.r_chain, 1)
                dve.wait_ge(k.r_chain, count.next())
                nc.vector.tensor_scalar(k.r_sum[:, b, 1:2], k.r_sum[:, b, 0:1], 1e-20, None, ALU.add).then_inc(k.r_chain, 1)
                dve.wait_ge(k.r_chain, count.next())
                nc.vector.reciprocal(k.r_sum[:, b, 2:3], k.r_sum[:, b, 1:2]).then_inc(k.r_chain, 1)
                dve.wait_ge(k.r_chain, count.next())
                nc.vector.tensor_scalar(k.r_w[:, b, :], k.r_w[:, b, :], k.r_sum[:, b, 2:3], ROUTE_SCALE, ALU.mult,
                                        ALU.mult).then_inc(k.r_chain, 1)
                dve.wait_ge(k.r_chain, count.next())
                assert count.passed == CL

            def step(it, par, ends):
                if active(it, 0, ends):
                    front_dve_stats(k, dve, m, k.x, it, par)
                    if positive(front + it - 1):
                        dve.wait_ge(k.f_xT_psum, front + it - 1)
                    if positive(8 * (it - par)):
                        dve.wait_ge(k.x_out_ready[par], 8 * (it - par))
                    front_dve_norm(k, dve, m, k.x, it, par, k.xn[:, par, :])
                if active(it, 1, ends):
                    t, b = it - 1, 1 - par
                    dve.wait_ge(k.sig_ready, t + 1)
                    if positive(t - 1):
                        dve.wait_ge(k.down_ready, t - 1)
                    h = k.r_h[:, b, 0:FW]
                    nc.vector.tensor_tensor(h, ps[:, 0, 0:FW], k.r_sig[:, b, 0:FW], ALU.mult).then_inc(k.gated_ready, 1)
                    dve.wait_ge(k.gated_ready, t + 1)
                    dve.wait_ge(k.up_ready, t + 1)
                    nc.vector.tensor_tensor(h, h, ps[:, 1, 0:FW], ALU.mult).then_inc(k.hidden_ready, 1)
                    if choose:
                        route(t, b)
                if active(it, 2, ends):
                    t = it - 2
                    if choose:
                        dve.wait_ge(k.r_cum_psum, t + 1)
                        nc.vector.tensor_scalar(k.held[0:E, bass.ds(t * P, P)], ps[0:E, 3, 0:P], k.r_carry[0:E, 0:1], None,
                                                ALU.add).then_inc(k.r_cum, 1)
                        dve.wait_ge(k.r_cum, 2 * t + 2)
                        nc.vector.tensor_scalar(k.r_carry[0:E, 0:1], ps[0:E, 3, P - 1:P], k.r_carry[0:E, 0:1], None,
                                                ALU.add).then_inc(k.r_cum, 1)
                        dve.wait_ge(k.r_cum, 2 * t + 3)
                    dve.wait_ge(k.down_ready, t + 1)
                    xt = k.x[:, bass.ds(t * P, P)]
                    nc.vector.tensor_tensor(xt, xt, ps[:, 6, 0:P], ALU.add).then_inc(k.res_ready, 1)
            tile_pipeline(dve, step, 3)

        @block.tensor
        def _(pe):
            def step(it, par, ends):
                if active(it, 0, ends):
                    pe.wait_ge(k.f_xn, m * TILES + it + 1)
                    if positive(front + it):
                        pe.wait_ge(k.f_xT, front + it)
                    nc.tensor.transpose(k.ps_xT, k.xn[:, par, :], k.ident).then_inc(k.f_xT_psum, 1)
                if active(it, 1, ends):
                    t, b = it - 1, 1 - par
                    xT = k.xnT[:, b, :]
                    pe.wait_ge(k.f_xT, front + t + 1)
                    if positive(t):
                        pe.wait_ge(k.gated_ready, t)
                    for c in range(FC):
                        mm = nc.tensor.matmul(ps[:, 0, c * P:(c + 1) * P], k.sh_gate[r.name][:, c * P:(c + 1) * P], xT,
                                              start=True, stop=True)
                    mm.then_inc(k.gate_ready, 1)
                    if positive(t):
                        pe.wait_ge(k.score_ready, t)
                    nc.tensor.matmul(ps[:, 2, 0:E], xT, k.router[r.name][:, :], start=True,
                                     stop=True).then_inc(k.logit_ready, 1)
                    if not choose:
                        if positive(t):
                            pe.wait_ge(k.r_scoreT, t)
                        nc.tensor.matmul(ps[0:E, 3, 0:P], k.router[r.name][:, :], xT, start=True,
                                         stop=True).then_inc(k.r_logitT, 1)
                    if positive(t):
                        pe.wait_ge(k.hidden_ready, t)
                    for c in range(FC):
                        mm = nc.tensor.matmul(ps[:, 1, c * P:(c + 1) * P], k.sh_up[r.name][:, c * P:(c + 1) * P], xT,
                                              start=True, stop=True)
                    mm.then_inc(k.up_ready, 1)
                if active(it, 2, ends):
                    t, b = it - 2, par
                    pe.wait_ge(k.hidden_ready, t + 1)
                    if positive(t):
                        pe.wait_ge(k.res_ready, t)
                    for c in range(FC):
                        mm = nc.tensor.matmul(ps[:, 6, 0:P], k.r_h[:, b, c * P:(c + 1) * P], k.sh_down[r.name][:, c, :],
                                              start=c == 0, stop=c == FC - 1)
                    mm.then_inc(k.down_ready, 1)
                    if choose:
                        pe.wait_ge(k.r_chain, CL * (t + 1))
                        pe.wait_ge(k.r_cum, 2 * t + 1)
                        nc.tensor.matmul(ps[0:E, 3, 0:P], k.r_sel[:, b, :], k.consts[:, C_UPPER:C_UPPER + P], start=True,
                                         stop=True).then_inc(k.r_cum_psum, 1)
            tile_pipeline(pe, step, 3)

        @block.scalar
        def _(act):
            def step(it, par, ends):
                if active(it, 0, ends):
                    act.wait_ge(k.f_xT_psum, front + it + 1)
                    if positive(it - 1):
                        act.wait_ge(k.up_ready, it - 1)
                    nc.scalar.activation(k.xnT[:, par, :], k.ps_xT, ACT.Copy).then_inc(k.f_xT, 1)
                if active(it, 1, ends):
                    t, b = it - 1, 1 - par
                    act.wait_ge(k.gate_ready, t + 1)
                    if positive(t - 1):
                        act.wait_ge(k.gated_ready, t - 1)
                    nc.scalar.activation(k.r_sig[:, b, 0:FW], ps[:, 0, 0:FW], ACT.Sigmoid).then_inc(k.sig_ready, 1)
                    act.wait_ge(k.logit_ready, t + 1)
                    if choose:
                        if positive(CL * (t - 1)):
                            act.wait_ge(k.r_chain, CL * (t - 1))
                    else:
                        if positive(8 * (t - b)):
                            act.wait_ge(k.w_out_ready[b], 8 * (t - b))
                    nc.scalar.activation(k.r_score[:, b, 0:E], ps[:, 2, 0:E], ACT.Sigmoid).then_inc(k.score_ready, 1)
                    if not choose:
                        act.wait_ge(k.r_logitT, t + 1)
                        nc.scalar.activation(k.held[0:E, bass.ds(t * P, P)], ps[0:E, 3, 0:P],
                                             ACT.Sigmoid).then_inc(k.r_scoreT, 1)
            tile_pipeline(act, step, 3)


def choose_tokens(k, ps, r):
    nc = k.nc
    W = T // 8
    cap = float(r.NB * P)
    score, work, work2, cum = k.prob[:, 0, :], k.prob[:, 1, :], k.probT[:, 0, :], k.probT[:, 1, :]
    chunk, earlier = k.consts[:, C_CHUNK:C_CHUNK + P], k.consts[:, C_EARLIER:C_EARLIER + P]
    with nc.Block() as block:
        @block.sync
        def _(sp):
            sp.dma_start(k.score_dram, k.held[0:r.E, :]).then_inc(k.c_io, 16)
            sp.wait_ge(k.c_io, 16)
            sp.dma_start(score, k.score_dram.rearrange("e (c n) -> (e c) n", c=8)).then_inc(k.c_io, 16)
            sp.wait_ge(k.c_io, 32)

        @block.gpsimd
        def _(pool):
            nc.gpsimd.memset(k.c_thr[:, 0, :], 0.0).then_inc(k.c_zero, 1)

        @block.vector
        def _(dve):
            dve.wait_ge(k.c_zero, 1)
            dve.wait_ge(k.c_io, 32)
            thr, cand = k.c_thr[:, 0, :], k.c_thr[:, 1, :]
            with dve.Fori(0, 30) as bit:
                count = Count(bit, 4)
                nc.vector.tensor_tensor(cand.bitcast(I32), thr.bitcast(I32), k.bits[:, bass.ds(bit, 1)],
                                        ALU.bitwise_or).then_inc(k.c_chain, 1)
                dve.wait_ge(k.c_chain, count.next())
                nc.vector.tensor_scalar(work, score, cand, None, ALU.is_ge, ALU.add, accum_out=k.c_count[:, 0:1]).then_inc(k.c_chain, 1)
                dve.wait_ge(k.c_chain, count.next())
                dve.wait_ge(k.c_psum, bit + 1)
                nc.vector.tensor_scalar(cand, ps[:, 0, 0:1], cap, cand, ALU.is_ge, ALU.mult).then_inc(k.c_chain, 1)
                dve.wait_ge(k.c_chain, count.next())
                nc.vector.tensor_tensor(thr, thr, cand, ALU.max).then_inc(k.c_chain, 1)
                dve.wait_ge(k.c_chain, count.next())
            count = Count(0, 99)
            nc.vector.tensor_scalar(work, score, thr, None, ALU.is_gt, ALU.add, accum_out=k.c_count[:, 1:2]).then_inc(k.c_chain2, 1)
            dve.wait_ge(k.c_chain2, count.next())
            nc.vector.tensor_scalar(work2, score, thr, None, ALU.is_equal, ALU.add, accum_out=k.c_count[:, 2:3]).then_inc(k.c_chain2, 1)
            dve.wait_ge(k.c_chain2, count.next())
            nc.vector.tensor_tensor_scan(cum, work2, work2, 0.0, ALU.add, ALU.max).then_inc(k.c_chain2, 1)
            dve.wait_ge(k.c_chain2, count.next())
            dve.wait_ge(k.c_psum, 32)
            nc.vector.tensor_scalar(k.c_count[:, 3:4], ps[:, 0, 1:2], -cap, None, ALU.add).then_inc(k.c_chain2, 1)
            dve.wait_ge(k.c_chain2, count.next())
            nc.vector.tensor_tensor(k.c_count[:, 4:5], k.c_count[:, 3:4], ps[:, 0, 2:3], ALU.add).then_inc(k.c_chain2, 1)
            dve.wait_ge(k.c_chain2, count.next())
            nc.vector.tensor_scalar(cum, cum, k.c_count[:, 4:5], 0.0, ALU.add, ALU.is_le).then_inc(k.c_chain2, 1)
            dve.wait_ge(k.c_chain2, count.next())
            nc.vector.tensor_tensor(work2, work2, cum, ALU.mult).then_inc(k.c_chain2, 1)
            dve.wait_ge(k.c_chain2, count.next())
            nc.vector.tensor_tensor(work, work, work2, ALU.add).then_inc(k.c_chain2, 1)
            dve.wait_ge(k.c_chain2, count.next())
            nc.vector.tensor_tensor_scan(cum, work, work, 0.0, ALU.add, ALU.max).then_inc(k.c_chain2, 1)
            dve.wait_ge(k.c_chain2, count.next())
            nc.vector.tensor_copy(k.c_count[:, 5:6], cum[:, W - 1:W]).then_inc(k.c_total, 1)
            dve.wait_ge(k.c_psum, 33)
            nc.vector.tensor_scalar(cum, cum, ps[:, 0, 3:4], None, ALU.add).then_inc(k.c_chain2, 1)
            dve.wait_ge(k.c_chain2, count.next())

        @block.tensor
        def _(pe):
            with pe.Fori(0, 30) as bit:
                pe.wait_ge(k.c_chain, 4 * bit + 2)
                nc.tensor.matmul(ps[:, 0, 0:1], chunk, k.c_count[:, 0:1], start=True, stop=True).then_inc(k.c_psum, 1)
            pe.wait_ge(k.c_chain, 120)
            pe.wait_ge(k.c_chain2, 2)
            nc.tensor.matmul(ps[:, 0, 1:2], chunk, k.c_count[:, 1:2], start=True, stop=True).then_inc(k.c_psum, 1)
            nc.tensor.matmul(ps[:, 0, 2:3], earlier, k.c_count[:, 2:3], start=True, stop=True).then_inc(k.c_psum, 1)
            pe.wait_ge(k.c_total, 1)
            pe.wait_ge(k.c_chain2, 5)
            nc.tensor.matmul(ps[:, 0, 3:4], earlier, k.c_count[:, 5:6], start=True, stop=True).then_inc(k.c_psum, 1)


def find_slots(k, ps, r):
    nc = k.nc
    E, NB = r.E, r.NB
    cend = k.x[:, 0:E * TILES]
    le = k.x[:, TILES * D // 2:TILES * D // 2 + E * TILES]
    parts = E if r.name == "L0_ffn" else P
    per = E * TILES // parts
    counts = (k.held[0:E, :] if r.name == "L0_ffn" else k.probT[:, 1, :])
    LOADS = 8

    with nc.Block() as block:
        @block.sync
        def _(sp):
            xs = k.x_dram[0:T, :].rearrange("(n p) c -> p n c", p=P)
            for c in range(LOADS):
                w = TILES // LOADS
                sp.dma_start(xs[:, c * w:(c + 1) * w, :],
                             k.x[:, c * w * D:(c + 1) * w * D].rearrange("p (n c) -> p n c", c=D)
                             ).then_inc(k.spill_ready, 16)
            sp.dma_start(k.cum_dram[0:E * TILES, :].rearrange("(p n) t -> p (n t)", p=parts), counts).then_inc(k.spill_ready, 16)
            sp.wait_ge(k.zero_ready, 1)
            sp.dma_start(k.x_dram[T:T + P, :], k.zeros[:, 0:D]).then_inc(k.spill_ready, 16)
            sp.dma_start(r.table[T:T + P, :], k.zeros[:, 0:r.TW]).then_inc(k.spill_ready, 16)
            sp.wait_ge(k.ends_ready, 1)
            sp.dma_start(k.cend_dram[0:E * TILES].rearrange("(p n) -> p n", p=parts), k.tile_ends[0:parts, 0:per]).then_inc(k.spill_ready, 16)
            sp.wait_ge(k.spill_ready, 16 * (LOADS + 4))
            sp.dma_start(cend, k.cend_dram[0:E * TILES].partition_broadcast(P)).then_inc(k.spill_ready, 16)
            sp.wait_ge(k.spill_ready, 16 * (LOADS + 5))

        @block.gpsimd
        def _(pool):
            nc.gpsimd.memset(k.zeros[:, :], 0.0).then_inc(k.zero_ready, 1)

        @block.vector
        def _(dve):
            nc.vector.tensor_copy(k.tile_ends[0:parts, 0:per].rearrange("p (n o) -> p n o", o=1),
                                  counts.rearrange("p (n t) -> p n t", t=P)[:, :, P - 1:P]).then_inc(k.ends_ready, 1)
            dve.wait_ge(k.spill_ready, 16 * (LOADS + 5))
            count = Count(0, 99)
            tiles = k.slot_tile[:, 0:r.units].rearrange("p (e b) -> p e b", b=NB)
            rows = k.slot_row[:, 0:r.units].rearrange("p (e b) -> p e b", b=NB)
            for b in range(NB):
                nc.vector.tensor_scalar(le, cend, k.consts[:, C_SLOT + b:C_SLOT + b + 1], None, ALU.is_le).then_inc(k.slotchain_ready, 1)
                dve.wait_ge(k.slotchain_ready, count.next())
                nc.vector.tensor_reduce(tiles[:, :, b:b + 1].rearrange("p e o -> p (e o)"),
                                        le.rearrange("p (e n) -> p e n", n=TILES), AX.X, ALU.add).then_inc(k.slotchain_ready, 1)
                dve.wait_ge(k.slotchain_ready, count.next())
            base = k.consts[:, C_TOKEN0:C_TOKEN0 + E].rearrange("p (e o) -> p e o", o=1).broadcast_to([P, E, NB])
            nc.vector.scalar_tensor_tensor(rows, tiles, float(TILES - 1), base, ALU.min, ALU.add).then_inc(k.slotchain_ready, 1)
            dve.wait_ge(k.slotchain_ready, count.next())

    G = 4
    steps = r.units // G
    with nc.Block() as block:
        @block.gpsimd
        def _(pool):
            def step(it, par, ends):
                if active(it, 0, ends):
                    pool.wait_ge(k.index_ready, it + 1)
                    if positive(G * (it - 1)):
                        pool.wait_ge(k.within_ready, G * (it - 1))
                    pool_pause(k, pool, k.pause_find, 4, it)
                    for q in range(G):
                        nc.gpsimd.indirect_dma_start(
                            out=k.rows[:, par, q, :], out_offset=None, in_=k.cum_dram[0:E * TILES, :],
                            in_offset=bass.IndirectOffsetOnAxis(ap=k.slot_index[:, par, q:q + 1], axis=0),
                            bounds_check=E * TILES - 1, oob_is_err=True).then_inc(k.rows_ready[par], 16)
            tile_pipeline(pool, step, 2, count=steps)

        @block.vector
        def _(dve):
            def step(it, par, ends):
                if active(it, 0, ends):
                    if positive((8 * G) * (it - par)):
                        dve.wait_ge(k.rows_ready[par], (8 * G) * (it - par))
                    nc.vector.tensor_scalar(k.slot_index[:, par, :], k.slot_row[:, bass.ds(G * it, G)], 0.0, None, ALU.add).then_inc(k.index_ready, 1)
                if active(it, 1, ends):
                    t, buf = it - 1, 1 - par
                    dve.wait_ge(k.rows_ready[buf], (8 * G) * (t - buf + 2))
                    for q in range(G):
                        b = (G * buf + q) % NB
                        nc.vector.tensor_scalar(k.row_le[:, q, :], k.rows[:, buf, q, :],
                                                k.consts[:, C_SLOT + b:C_SLOT + b + 1], None, ALU.is_le, ALU.add,
                                                accum_out=k.slot_within[:, bass.ds(G * t + q, 1)]).then_inc(k.within_ready, 1)
                        dve.wait_ge(k.within_ready, G * t + q + 1)
            tile_pipeline(dve, step, 2, count=steps)
            count = Count(0, 99)
            tiles, within = k.slot_tile[:, 0:r.units], k.slot_within[:, 0:r.units]
            nc.vector.scalar_tensor_tensor(within, tiles, float(P), within, ALU.mult, ALU.add).then_inc(k.tokenchain_ready, 1)
            dve.wait_ge(k.tokenchain_ready, count.next())
            nc.vector.tensor_scalar(k.slot_token[:, 0:r.units], within, k.consts[:, C_SLOT + 8:C_SLOT + 9], None, ALU.min).then_inc(k.tokenchain_ready, 1)
            dve.wait_ge(k.tokenchain_ready, count.next())


def small_experts(k, ps, r):
    nc = k.nc
    E, F = r.E, 64
    xe = k.x[:, 0:2 * r.TW].rearrange("p (b n) -> p b n", b=2)
    at = 2 * r.TW
    w13 = k.x[:, at:at + 2 * 2 * F].rearrange("p (b n) -> p b n", b=2)
    at += 4 * F
    w2 = k.x[0:F, at:at + 2 * D].rearrange("p (b n) -> p b n", b=2)
    at += 2 * D
    xeT = k.x[:, at:at + 2 * P].rearrange("p (b n) -> p b n", b=2)
    at += 2 * P
    sig = k.x[0:F, at:at + 2 * P].rearrange("p (b n) -> p b n", b=2)
    at += 2 * P
    eh = k.x[0:F, at:at + 2 * P].rearrange("p (b n) -> p b n", b=2)
    at += 2 * P
    ys = k.x[:, at:at + 2 * D].rearrange("p (b n) -> p b n", b=2)

    with nc.Block() as block:
        @block.sync
        def _(sp):
            def step(it, par, ends):
                if active(it, 0, ends):
                    if positive(it - 1):
                        sp.wait_ge(k.e_y, it - 1)
                    sp.dma_start(w13[:, par, :], k.d["e_w13"][bass.ds(it * D, D), :]).then_inc(k.e_w_ready[par], 16)
                    sp.dma_start(w2[:, par, :], k.d["e_w2"][bass.ds(it * F, F), :]).then_inc(k.e_w_ready[par], 16)
            tile_pipeline(sp, step, 3, count=E)

        @block.gpsimd
        def _(pool):
            def step(it, par, ends):
                if active(it, 0, ends):
                    pool.wait_ge(k.e_index, it + 1)
                    if positive(it - 1):
                        pool.wait_ge(k.e_xT_psum, it - 1)
                    if positive(it - 1):
                        pool.wait_ge(k.e_col, it - 1)
                    pool_pause(k, pool, k.pause_gather, 5, it)
                    nc.gpsimd.indirect_dma_start(
                        out=xe[:, par, :], out_offset=None, in_=r.table,
                        in_offset=bass.IndirectOffsetOnAxis(ap=k.e_gidx[:, par, 0:1], axis=0),
                        bounds_check=T + P - 1, oob_is_err=True).then_inc(k.e_x_ready[par], 16)
                if active(it, 2, ends):
                    t = it - 2
                    pool.wait_ge(k.e_scaled, t + 1)
                    if positive(16 * t):
                        pool.wait_ge(k.e_added, 16 * t)
                    pool_pause(k, pool, k.pause_add, 6, t)
                    nc.gpsimd.indirect_dma_start(
                        out=k.x_dram, out_offset=bass.IndirectOffsetOnAxis(ap=k.e_sidx[:, par, 0:1], axis=0),
                        in_=ys[:, par, :], in_offset=None, bounds_check=T + P - 1, oob_is_err=True,
                        compute_op=ALU.add).then_inc(k.e_added, 16)
            tile_pipeline(pool, step, 3, count=E)
            pool.wait_ge(k.e_added, 16 * E)

        @block.vector
        def _(dve):
            def step(it, par, ends):
                if active(it, 0, ends):
                    if positive(8 * (it - par)):
                        dve.wait_ge(k.e_x_ready[par], 8 * (it - par))
                    nc.vector.tensor_scalar(k.e_gidx[:, par, 0:1], k.slot_token[:, bass.ds(it, 1)], 0.0, None, ALU.add).then_inc(k.e_index, 1)
                if active(it, 1, ends):
                    t, b = it - 1, 1 - par
                    dve.wait_ge(k.e_x_ready[b], 8 * (t - b + 2))
                    if positive(t - 1):
                        dve.wait_ge(k.e_scaled, t - 1)
                    nc.vector.tensor_scalar(k.e_wcol[:, b, 0:1], xe[:, b, bass.ds(D + t, 1)], 0.0, None, ALU.add).then_inc(k.e_col, 1)
                    if positive(16 * (t - 1)):
                        dve.wait_ge(k.e_added, 16 * (t - 1))
                    nc.vector.tensor_scalar(k.e_sidx[:, b, 0:1], k.slot_token[:, bass.ds(t, 1)], 0.0, None, ALU.add).then_inc(k.e_sindex, 1)
                    dve.wait_ge(k.e_sig, t + 1)
                    if positive(t - 1):
                        dve.wait_ge(k.e_y, t - 1)
                    nc.vector.tensor_tensor(eh[:, b, :], ps[0:F, 0, 0:P], sig[:, b, :], ALU.mult).then_inc(k.e_gated, 1)
                    dve.wait_ge(k.e_gated, t + 1)
                    dve.wait_ge(k.e_h3, t + 1)
                    nc.vector.tensor_tensor(eh[:, b, :], eh[:, b, :], ps[0:F, 1, 0:P], ALU.mult).then_inc(k.e_hid, 1)
                if active(it, 2, ends):
                    t = it - 2
                    dve.wait_ge(k.e_y, t + 1)
                    dve.wait_ge(k.e_col, t + 1)
                    dve.wait_ge(k.e_sindex, t + 1)
                    if positive(16 * (t - 1)):
                        dve.wait_ge(k.e_added, 16 * (t - 1))
                    nc.vector.tensor_scalar(ys[:, par, :], ps[:, 2, 0:D], k.e_wcol[:, par, 0:1], None,
                                            ALU.mult).then_inc(k.e_scaled, 1)
            tile_pipeline(dve, step, 3, count=E)

        @block.tensor
        def _(pe):
            def step(it, par, ends):
                if active(it, 1, ends):
                    t, b = it - 1, 1 - par
                    pe.wait_ge(k.e_x_ready[b], 8 * (t - b + 2))
                    if positive(t):
                        pe.wait_ge(k.e_xT, t)
                    nc.tensor.transpose(ps[:, 4, 0:P], xe[:, b, 0:D], k.ident).then_inc(k.e_xT_psum, 1)
                    pe.wait_ge(k.e_xT, t + 1)
                    pe.wait_ge(k.e_w_ready[b], 16 * (t - b + 2))
                    if positive(t):
                        pe.wait_ge(k.e_gated, t)
                    nc.tensor.matmul(ps[0:F, 0, 0:P], w13[:, b, 0:F], xeT[:, b, :], start=True, stop=True).then_inc(k.e_h1, 1)
                    if positive(t):
                        pe.wait_ge(k.e_hid, t)
                    nc.tensor.matmul(ps[0:F, 1, 0:P], w13[:, b, F:2 * F], xeT[:, b, :], start=True, stop=True).then_inc(k.e_h3, 1)
                if active(it, 2, ends):
                    t = it - 2
                    pe.wait_ge(k.e_hid, t + 1)
                    if positive(t):
                        pe.wait_ge(k.e_scaled, t)
                    nc.tensor.matmul(ps[:, 2, 0:D], eh[:, par, :], w2[:, par, :], start=True, stop=True).then_inc(k.e_y, 1)
            tile_pipeline(pe, step, 3, count=E)

        @block.scalar
        def _(act):
            def step(it, par, ends):
                if active(it, 1, ends):
                    t, b = it - 1, 1 - par
                    act.wait_ge(k.e_xT_psum, t + 1)
                    if positive(t - 1):
                        act.wait_ge(k.e_h3, t - 1)
                    nc.scalar.activation(xeT[:, b, :], ps[:, 4, 0:P], ACT.Copy).then_inc(k.e_xT, 1)
                    act.wait_ge(k.e_h1, t + 1)
                    if positive(t - 1):
                        act.wait_ge(k.e_gated, t - 1)
                    nc.scalar.activation(sig[:, b, :], ps[0:F, 0, 0:P], ACT.Sigmoid).then_inc(k.e_sig, 1)
            tile_pipeline(act, step, 3, count=E)


def large_experts(k, ps, r):
    nc = k.nc
    H = 512
    NC = 4
    WC = 3 * 512 + 2 * NC + D
    steps = r.E * r.NB * P // H
    w = k.held[:, 0:2 * WC].rearrange("p (b n) -> p b n", b=2)
    hid = k.held[:, 2 * WC:2 * WC + 2 * NC * H].rearrange("p (b c n) -> p b c n", b=2, c=NC)
    xg = k.x[:, 0:2 * 4 * r.TW].rearrange("p (b q n) -> p b q n", b=2, q=4)
    at = 2 * 4 * r.TW
    xgT = k.x[:, at:at + 2 * H].rearrange("p (b n) -> p b n", b=2)
    at += 2 * H
    gate = k.x[:, at:at + 2 * H].rearrange("p (b n) -> p b n", b=2)
    at += 2 * H
    ys = k.x[:, at:at + 2 * H].rearrange("p (b n) -> p b n", b=2)

    def expert(it, u):
        return it // 2 if isinstance(it, int) else (it - u % 2) // 2

    with nc.Block() as block:
        @block.sync
        def _(sp):
            def step(it, u, ends):
                if active(it, 0, ends) and u % 2 == 0:
                    if positive(it - 2):
                        sp.wait_ge(k.g_biased, it - 2)
                    sp.dma_start(w[:, u // 2, :], k.d["g_w"][bass.ds(it * (P // 2), P), :]).then_inc(k.g_w_ready[u // 2], 16)
            tile_pipeline(sp, step, 3, count=steps, unroll=4)

        @block.gpsimd
        def _(pool):
            def step(it, u, ends):
                if active(it, 0, ends):
                    pool.wait_ge(k.g_index, it + 1)
                    if positive(it - 1):
                        pool.wait_ge(k.g_xT_psum, it - 1)
                    if positive(it - 1):
                        pool.wait_ge(k.g_col, it - 1)
                    pool_pause(k, pool, k.pause_gather, 5, it)
                    for q in range(4):
                        nc.gpsimd.indirect_dma_start(
                            out=xg[:, u % 2, q, :], out_offset=None, in_=r.table,
                            in_offset=bass.IndirectOffsetOnAxis(ap=k.g_gidx[:, u % 2, q:q + 1], axis=0),
                            bounds_check=T - 1, oob_is_err=True).then_inc(k.g_x_ready[u % 2], 16)
                if active(it, 2, ends):
                    t = it - 2
                    pool.wait_ge(k.g_scaled, t + 1)
                    if u % 2 == 0:
                        if positive(64 * t):
                            pool.wait_ge(k.g_added, 64 * t)
                    pool_pause(k, pool, k.pause_add, 6, t)
                    for q in range(4):
                        nc.gpsimd.indirect_dma_start(
                            out=k.x_dram, out_offset=bass.IndirectOffsetOnAxis(ap=k.g_sidx[:, u % 2, q:q + 1], axis=0),
                            in_=ys[:, u % 2, q * D:(q + 1) * D], in_offset=None, bounds_check=T - 1, oob_is_err=True,
                            compute_op=ALU.add).then_inc(k.g_added, 16)
            tile_pipeline(pool, step, 3, count=steps, unroll=4)
            pool.wait_ge(k.g_added, 64 * steps)

        @block.vector
        def _(dve):
            def step(it, u, ends):
                par = u % 2
                if active(it, 0, ends):
                    if positive(32 * (it - par)):
                        dve.wait_ge(k.g_x_ready[par], 32 * (it - par))
                    nc.vector.tensor_scalar(k.g_gidx[:, par, :], k.slot_token[:, bass.ds(4 * it, 4)], 0.0, None, ALU.add).then_inc(k.g_index, 1)
                if active(it, 1, ends):
                    t, b = it - 1, 1 - par
                    dve.wait_ge(k.g_x_ready[b], 32 * (t - b + 2))
                    if positive(t - 1):
                        dve.wait_ge(k.g_scaled, t - 1)
                    nc.vector.tensor_scalar(k.g_wcol[:, b, :].rearrange("p (q o) -> p q o", o=1),
                                            xg[:, b, :, bass.ds(D + expert(t, u + 3), 1)], 0.0, None, ALU.add).then_inc(k.g_col, 1)
                    if positive(64 * (t - 1)):
                        dve.wait_ge(k.g_added, 64 * (t - 1))
                    nc.vector.tensor_scalar(k.g_sidx[:, b, :], k.slot_token[:, bass.ds(4 * t, 4)], 0.0, None, ALU.add).then_inc(k.g_sindex, 1)
                    if positive(t - 1):
                        dve.wait_ge(k.g_y, t - 1)
                    wb = (u + 3) % 4 // 2
                    for c in range(NC):
                        dve.wait_ge(k.g_silu, NC * t + c + 1)
                        dve.wait_ge(k.g_up, NC * t + c + 1)
                        nc.vector.scalar_tensor_tensor(hid[:, b, c, :], ps[:, 2 + c % 2, :],
                                                       w[:, wb, 1536 + NC + c:1536 + NC + c + 1], gate[:, c % 2, :],
                                                       ALU.add, ALU.mult).then_inc(k.g_hid, 1)
                if active(it, 2, ends):
                    t = it - 2
                    wb = (u + 2) % 4 // 2
                    dve.wait_ge(k.g_y, t + 1)
                    if positive(64 * (t - 1)):
                        dve.wait_ge(k.g_added, 64 * (t - 1))
                    bias = w[:, wb, 1536 + 2 * NC:WC].rearrange("p (o d) -> p o d", o=1).broadcast_to([P, 4, D])
                    y3 = ys[:, par, :].rearrange("p (q d) -> p q d", d=D)
                    nc.vector.tensor_tensor(y3, ps[:, 5, :].rearrange("p (q d) -> p q d", d=D), bias,
                                            ALU.add).then_inc(k.g_biased, 1)
                    dve.wait_ge(k.g_biased, t + 1)
                    dve.wait_ge(k.g_col, t + 1)
                    dve.wait_ge(k.g_sindex, t + 1)
                    nc.vector.tensor_tensor(
                        y3, y3, k.g_wcol[:, par, :].rearrange("p (q o) -> p q o", o=1).broadcast_to([P, 4, D]),
                        ALU.mult).then_inc(k.g_scaled, 1)
            tile_pipeline(dve, step, 3, count=steps, unroll=4)

        @block.tensor
        def _(pe):
            def step(it, u, ends):
                par = u % 2
                if active(it, 1, ends):
                    t, b = it - 1, 1 - par
                    wb = (u + 3) % 4 // 2
                    pe.wait_ge(k.g_x_ready[b], 32 * (t - b + 2))
                    if positive(t):
                        pe.wait_ge(k.g_xT, t)
                    for q in range(4):
                        mm = nc.tensor.transpose(ps[:, 4, q * P:(q + 1) * P], xg[:, b, q, 0:D], k.ident)
                    mm.then_inc(k.g_xT_psum, 1)
                    pe.wait_ge(k.g_xT, t + 1)
                    pe.wait_ge(k.g_w_ready[wb], 4 * (t - (u + 3) % 4 + 4))
                    for c in range(NC):
                        if positive(NC * t + c - 1):
                            pe.wait_ge(k.g_silu, NC * t + c - 1)
                        nc.tensor.matmul(ps[:, c % 2, :], w[:, wb, c * P:(c + 1) * P], xgT[:, b, :], start=True,
                                         stop=True).then_inc(k.g_gate, 1)
                        if positive(NC * t + c - 1):
                            pe.wait_ge(k.g_hid, NC * t + c - 1)
                        nc.tensor.matmul(ps[:, 2 + c % 2, :], w[:, wb, 512 + c * P:512 + (c + 1) * P], xgT[:, b, :],
                                         start=True, stop=True).then_inc(k.g_up, 1)
                if active(it, 2, ends):
                    t = it - 2
                    wb = (u + 2) % 4 // 2
                    pe.wait_ge(k.g_hid, NC * (t + 1))
                    if positive(t):
                        pe.wait_ge(k.g_biased, t)
                    for q in range(4):
                        for c in range(NC):
                            mm = nc.tensor.matmul(ps[:, 5, q * D:(q + 1) * D], hid[:, par, c, q * P:(q + 1) * P],
                                                  w[:, wb, 1024 + c * D:1024 + (c + 1) * D], start=c == 0, stop=c == NC - 1)
                    mm.then_inc(k.g_y, 1)
            tile_pipeline(pe, step, 3, count=steps, unroll=4)

        @block.scalar
        def _(act):
            def step(it, u, ends):
                par = u % 2
                if active(it, 1, ends):
                    t, b = it - 1, 1 - par
                    wb = (u + 3) % 4 // 2
                    act.wait_ge(k.g_xT_psum, t + 1)
                    if positive(NC * (t - 1)):
                        act.wait_ge(k.g_up, NC * (t - 1))
                    nc.scalar.activation(xgT[:, b, :], ps[:, 4, :], ACT.Copy).then_inc(k.g_xT, 1)
                    for c in range(NC):
                        act.wait_ge(k.g_gate, NC * t + c + 1)
                        if positive(NC * t + c - 1):
                            act.wait_ge(k.g_hid, NC * t + c - 1)
                        nc.scalar.activation(gate[:, c % 2, :], ps[:, c % 2, :], ACT.Silu,
                                             bias=w[:, wb, 1536 + c:1536 + c + 1]).then_inc(k.g_silu, 1)
            tile_pipeline(act, step, 3, count=steps, unroll=4)


def reload_x(k, r):
    LOADS = 8
    with k.nc.Block() as block:
        @block.sync
        def _(sp):
            xs = k.x_dram[0:T, :].rearrange("(n p) c -> p n c", p=P)
            for c in range(LOADS):
                w = TILES // LOADS
                sp.dma_start(k.x[:, c * w * D:(c + 1) * w * D].rearrange("p (n c) -> p n c", c=D),
                             xs[:, c * w:(c + 1) * w, :]).then_inc(k.reload_ready, 16)
            sp.wait_ge(k.reload_ready, 16 * LOADS)


def build(nc, d, stages):
    k = Kernel()
    k.nc, k.d, k.phases = nc, d, 0
    with ExitStack() as ctx:
        def sb(name, shape, dt=F32):
            return ctx.enter_context(nc.sbuf_tensor(name, shape, dt))

        def sem(name):
            return ctx.enter_context(nc.semaphore(name))

        k.x = sb("x_res", [P, TILES * D])
        k.held = sb("held", [P, TILES * D])
        k.consts = sb("consts", [P, C_END])
        k.attn_w = sb("attn_w", [P, NA, 4, D])
        k.bqk = sb("bqk", [P, NA, 2])
        k.bv = sb("bv", [P, NA, D])
        k.bo = sb("bo", [P, NA, D])
        k.ctxT = sb("ctxT", [P, 2, P])
        k.stats = sb("stats", [P, 2, 6])
        k.meanvar = sb("meanvar", [P, 2, 2])
        k.vareps = sb("vareps", [P, 2, 2])
        k.rstd = sb("rstd", [P, 2, 2])
        k.half_power = sb("half_power", [P, 1])
        k.pause = sb("pause", [P, 8])
        k.xn = sb("xn", [P, 2, D])
        k.xnT = sb("xnT", [P, 2, P])
        k.srcT = sb("srcT", [P, 2, 2, 2, S])
        k.qT = sb("qT", [P, 2, P])
        k.kblock = sb("kblock", [P, 2, GH, P])
        k.vblock = sb("vblock", [P, 2, HEADS // 2, 2, VW])
        k.rowmax = sb("rowmax", [P, 2, HEADS])
        k.prob = sb("prob", [P, 2, HEADS * S])
        k.probT = sb("probT", [P, 2, HEADS // 2 * P])
        k.rowinv = sb("rowinv", [P, 2, HEADS])
        k.o = sb("o", [P, 2, D])
        k.oT = sb("oT", [P, 2, P])
        k.post = sb("post", [P, 2, D])
        k.z = sb("z", [P, 2, D])
        k.v_low = sb("v_low", [P, 2, D])
        k.v_high = sb("v_high", [P, 2, D])
        k.z_dram = nc.dram_tensor("z_dram", (T, D), F32, kind="Internal").ap()
        k.post_stats = sb("post_stats", [P, 2, 6])
        k.post_meanvar = sb("post_meanvar", [P, 2, 2])
        k.post_gain = sb("post_gain", [P, 4, D])
        k.norm_cols = sb("norm_cols", [P, 4])
        k.mask_raw = sb("mask_raw", [P, TILES * S // 4], U32)
        k.maskadd = sb("maskadd", [P, 2, S])
        k.relpos = sb("relpos", [P, HEADS * S])
        k.ones = sb("ones", [P, P])
        k.ident_bf = sb("ident_bf", [P, P], BF16)
        k.bit_raw = k.held[:, 0:3 * INNER].rearrange("p (w n) -> p w n", w=3)
        k.bit_w = sb("bit_w", [P, 3, INNER], BF16)
        k.bit_sum = sb("bit_sum", [P, 4])
        k.bit_mean = sb("bit_mean", [P, 4])
        k.bit_inv = sb("bit_inv", [P, 4])
        k.b_xq = sb("b_xq", [P, 2, D], BF16)
        k.b_xqT = sb("b_xqT", [P, 2, P], BF16)
        k.b_xmax = sb("b_xmax", [P, 2, 2])
        k.b_scale = sb("b_scale", [P, 2, 2])
        k.b_h = k.prob[:, :, 0:INNER]
        k.b_hmax = sb("b_hmax", [P, 2, 4])
        k.b_hq = sb("b_hq", [P, 2, INNER], BF16)
        k.b_hqT = sb("b_hqT", [P, 2, INNER], BF16)
        k.moe_gate = sb("moe_gate", [P, ME])
        k.moe_w1 = sb("moe_w1", [P, ME * MH])
        k.moe_w2 = sb("moe_w2", [P, 4, D])
        k.m_logit = sb("m_logit", [P, 2, ME])
        k.m_top = sb("m_top", [P, 2, ME])
        k.m_place = sb("m_place", [P, 2, ME], U32)
        k.m_neg = sb("m_neg", [P, 2, 1])
        k.m_eq = sb("m_eq", [P, 2, ME, 2])
        k.m_sel = sb("m_sel", [P, 2, ME])
        k.m_ex = sb("m_ex", [P, 2, ME])
        k.m_w = sb("m_w", [P, 2, ME])
        k.m_sum = sb("m_sum", [P, 2, 2])
        k.m_h = k.prob[:, :, 0:ME * MH]
        k.m_hTs = k.probT[:, :, 0:ME * MH]
        k.e_bias = sb("e_bias", [P, 64])
        k.sh_gate = {"L0_ffn": sb("sh_gate0", [P, P]), "L2_ffn": sb("sh_gate2", [P, 2 * P])}
        k.sh_up = {"L0_ffn": sb("sh_up0", [P, P]), "L2_ffn": sb("sh_up2", [P, 2 * P])}
        k.sh_down = {"L0_ffn": sb("sh_down0", [P, 1, D]), "L2_ffn": sb("sh_down2", [P, 2, D])}
        k.router = {"L0_ffn": sb("router0", [P, 64]), "L2_ffn": sb("router2", [P, 16])}
        k.bits = sb("bits", [P, 30], I32)
        k.r_sig = k.kblock[:, :, 0:2, :].rearrange("p b c n -> p b (c n)")
        k.r_h = k.kblock[:, :, 2:4, :].rearrange("p b c n -> p b (c n)")
        k.r_score = sb("r_score", [P, 2, 64])
        k.r_sfc = sb("r_sfc", [P, 2, 64])
        k.r_left = sb("r_left", [P, 2, 64])
        k.r_sel = sb("r_sel", [P, 2, 64])
        k.r_w = sb("r_w", [P, 2, 64])
        k.r_gmax = sb("r_gmax", [P, 2, 8, 8])
        k.r_gs = sb("r_gs", [P, 2, 8])
        k.r_gtop = sb("r_gtop", [P, 2, 8])
        k.r_gplace = sb("r_gplace", [P, 2, 8], U32)
        k.r_geq = sb("r_geq", [P, 2, 8, 4])
        k.r_gmask = sb("r_gmask", [P, 2, 8])
        k.r_top = sb("r_top", [P, 2, 8])
        k.r_sum = sb("r_sum", [P, 2, 4])
        k.r_carry = sb("r_carry", [P, 1])
        k.tile_ends = sb("tile_ends", [P, TILES])
        k.zeros = sb("zeros", [P, 192])
        k.slot_tile = sb("slot_tile", [P, 128])
        k.slot_row = sb("slot_row", [P, 128], U32)
        k.slot_index = sb("slot_index", [P, 2, 4], U32)
        k.slot_within = sb("slot_within", [P, 128])
        k.slot_token = sb("slot_token", [P, 128], U32)
        k.rows = k.prob[:, :, 0:4 * P].rearrange("p b (q n) -> p b q n", q=4)
        k.row_le = sb("row_le", [P, 4, P], BF16)
        k.c_thr = sb("c_thr", [P, 2, 1])
        k.c_count = sb("c_count", [P, 8])
        k.e_gidx = sb("e_gidx", [P, 2, 1], U32)
        k.e_sidx = sb("e_sidx", [P, 2, 1], U32)
        k.e_wcol = sb("e_wcol", [P, 2, 1])
        k.g_gidx = sb("g_gidx", [P, 2, 4], U32)
        k.g_sidx = sb("g_sidx", [P, 2, 4], U32)
        k.g_wcol = sb("g_wcol", [P, 2, 4])

        def dram(name, shape):
            return nc.dram_tensor(name, shape, F32, kind="Internal").ap()
        k.x_dram = dram("x_dram", (T + P, D))
        k.cum_dram = dram("cum_dram", (64 * TILES, P))
        k.cend_dram = dram("cend_dram", (64 * TILES,))
        k.score_dram = dram("score_dram", (16, T))
        routed = {"L0_ffn": Routed("L0_ffn", 64, 1, 128, {"table": dram("table0", (T + P, D + 64))}),
                  "L2_ffn": Routed("L2_ffn", 16, 8, 256, {"table": dram("table2", (T + P, D + 16))})}
        k.rel_emb = sb("rel_emb", [P, 2, D])
        k.rel_table = sb("rel_table", [P, 2, HEADS])
        k.rel_tableT = sb("rel_tableT", [HEADS, 2 * P])
        k.rel_dram = nc.dram_tensor("rel_dram", (HEADS, 2 * P), F32, kind="Internal").ap()
        lora = sb("lora", [16, 8, D])
        ps = ctx.enter_context(nc.psum_tensor("ps", [P, 8, 512], F32))
        k.ident = k.consts[:, C_ID:C_ID + P]
        k.scores = ps[:, 0:4, :]
        k.ps_o = ps[:, 4, 0:2 * 8 * VW]
        k.ps_pT = ps[:, 4:6, :]
        k.ps_q = ps[:, 6, 0:128]
        k.ps_k = ps[:, 6, 128:256]
        k.ps_v = ps[:, 6, 256:512].rearrange("p (b d) -> p b d", b=2)
        k.ps_y = ps[:, 7, 256:384]
        k.ps_xT = ps[:, 7, 0:128]
        k.ps_oT = ps[:, 7, 128:256]

        lasting_semaphores(k, sem)
        run = [s for s in stages if s in ATTENTIONS]
        kinds = {"cross": CROSS, "out": OUT_BIAS - set(POST_NORM), "post": set(POST_NORM), "biased": BIASED}

        def before(kind, name):
            return sum(r in kinds[kind] for r in run[:run.index(name)])
        k.before = before

        LOADS = 8
        fronts = [s for s in stages if s in FFNS or s == "L3_ffn"]
        k.tf = lambda m: sum(s in WITH_TRANSPOSE for s in fronts[:m])

        with nc.Block() as block:
            @block.sync
            def _(sp):
                for dst, src in [(k.consts[:, :], d["consts"]), (k.attn_w[:, :, :, :], d["attn_w"]),
                                 (k.bqk[:, :, :], d["bqk"]), (lora[:, :, :], d["lora"]),
                                 (k.norm_cols[:, :], d["norm_cols"]), (k.moe_gate[:, :], d["moe_gate"]),
                                 (k.moe_w1[:, :], d["moe_w1"]), (k.moe_w2[:, :, :], d["moe_w2"]),
                                 (k.bits[:, :], d["bits"]),
                                 *[(dst[n][tuple([slice(None)] * len(dst[n].shape))], d[f"{what}_{n}"])
                                   for what, dst in [("sh_gate", k.sh_gate), ("sh_up", k.sh_up), ("sh_down", k.sh_down),
                                                     ("router", k.router)] for n in routed]]:
                    sp.dma_start(dst, src).then_inc(k.loaded, 16)
                for dst, src in [(k.bv, d["bv"]), (k.bo, d["bo"]), (k.post_gain, d["post_gain"])]:
                    sp.dma_start(dst[:, :, :], src.partition_broadcast(P)).then_inc(k.loaded, 16)
                xs = d["x"].rearrange("(n p) c -> p n c", p=P)
                for c in range(LOADS):
                    w = TILES // LOADS
                    sp.dma_start(k.x[:, c * w * D:(c + 1) * w * D].rearrange("p (n c) -> p n c", c=D),
                                 xs[:, c * w:(c + 1) * w, :]).then_inc(k.loaded, 16)
                sp.dma_start(k.e_bias[:, :], d["e_bias"].partition_broadcast(P)).then_inc(k.loaded, 16)
                sp.dma_start(k.mask_raw[:, :].rearrange("p (n s) -> p n s", s=S // 4),
                             d["mask"].rearrange("(n p) s -> p n s", p=P)).then_inc(k.loaded, 16)
                sp.wait_ge(k.loaded, 16 * (22 + LOADS))

            @block.gpsimd
            def _(pool):
                nc.gpsimd.memset(k.half_power[:, :], -0.5).then_inc(k.made, 1)
                nc.gpsimd.memset(k.ones[:, :], 1.0).then_inc(k.made, 1)
                nc.gpsimd.memset(k.vblock[:, :, :, :, :], 0.0).then_inc(k.made, 1)
                pool.wait_ge(k.made, 3)
                nc.gpsimd.memset(k.vblock[0:S, :, :, :, HD:HD + 1], 1.0).then_inc(k.made, 1)
                nc.gpsimd.memset(k.vblock[S:P, :, :, :, VW - 1:VW], 1.0).then_inc(k.made, 1)
                pool.wait_ge(k.made, 5)

            @block.tensor
            def _(pe):
                pe.wait_ge(k.loaded, 16 * (22 + LOADS))
                for m in range(4):
                    nc.tensor.matmul(ps[:, 0, m * P:(m + 1) * P], lora[:, m, :], lora[:, 4 + m, :], start=True,
                                     stop=True).then_inc(k.lora_psum, 1)

            @block.vector
            def _(dve):
                dve.wait_ge(k.lora_psum, 4)
                for m in range(4):
                    nc.vector.scalar_tensor_tensor(k.attn_w[:, 0, m, :], ps[:, 0, m * P:(m + 1) * P], 1.0 / 16,
                                                   k.attn_w[:, 0, m, :], ALU.mult, ALU.add).then_inc(k.lora_done, 1)
                dve.wait_ge(k.lora_done, 4)

        if "L1_attn" in stages:
            with phase(k, relative_bias_semaphores):
                relative_bias(k, ps)
        n = 0
        for stage in stages:
            m = sum(s in FFNS or s == "L3_ffn" for s in stages[:stages.index(stage)])
            if stage == "L1_ffn":
                with phase(k, bitlinear_semaphores):
                    bitlinear_weights(k, ps)
                    bitlinear_pass(k, ps, m)
            if stage in routed:
                r = routed[stage]
                with phase(k, routed_semaphores, small_experts_semaphores if stage == "L0_ffn" else large_experts_semaphores):
                    shared_pass(k, ps, m, r)
                    if stage == "L2_ffn":
                        choose_tokens(k, ps, r)
                    find_slots(k, ps, r)
                    (small_experts if stage == "L0_ffn" else large_experts)(k, ps, r)
                    reload_x(k, r)
            if stage == "L3_moe":
                with phase(k, dense_moe_semaphores):
                    dense_moe_pass(k, ps, m)
            if stage == "L3_ffn":
                prenorm_pass(k, m)
            if stage in ATTENTIONS:
                with nc.Block() as block:
                    @block.sync
                    def _(sp):
                        attention_loads(k, sp, stage, n)

                    @block.gpsimd
                    def _(pool):
                        attention_pool(k, pool, stage, n)

                    @block.tensor
                    def _(pe):
                        attention_pe(k, pe, stage, n)

                    @block.scalar
                    def _(act):
                        attention_act(k, act, stage, n)

                    @block.vector
                    def _(dve):
                        attention_dve(k, dve, stage, n)
                n += 1

        with nc.Block() as block:
            @block.sync
            def _(sp):
                out = d["out"].rearrange("(n p) c -> p n c", p=P)
                for c in range(LOADS):
                    w = TILES // LOADS
                    sp.dma_start(out[:, c * w:(c + 1) * w, :],
                                 k.x[:, c * w * D:(c + 1) * w * D].rearrange("p (n c) -> p n c", c=D)
                                 ).then_inc(k.stored, 16)
                sp.wait_ge(k.stored, 16 * LOADS)


def constants():
    c = np.zeros((P, C_END), np.float32)
    c[:, C_ID:C_ID + P] = np.eye(P)
    p = np.arange(P)
    for h in range(GH):
        c[:, C_HEAD + h] = (p // HD) % GH == h
    c[:, C_CAUSAL:C_CAUSAL + S] = MASKED * (np.arange(S)[None, :] > (p % S)[:, None])
    c[:, C_FUTURE:C_FUTURE + S] = LOWEST * (np.arange(S)[None, :] > (p % S)[:, None])
    c[:, C_SLOT:C_SLOT + 8] = p[:, None] + P * np.arange(8)[None, :]
    c[:, C_SLOT + 8] = T + p
    c[:, C_EIGHT:C_EIGHT + 8] = np.arange(8)
    c[:, C_CHUNK:C_CHUNK + P] = p[:, None] // 8 == p[None, :] // 8
    c[:, C_EARLIER:C_EARLIER + P] = (p[:, None] // 8 == p[None, :] // 8) & (p[:, None] < p[None, :])
    c[:, C_TOKEN0:C_TOKEN0 + 64] = TILES * np.arange(64)
    c[:, C_UPPER:C_UPPER + P] = p[:, None] <= p[None, :]
    return c


def lay_out(i):
    z = np.zeros((D,), np.float32)
    zz = np.zeros((D, D), np.float32)
    qkv, b3 = i["L1_attn_qkv_w"], i["L1_attn_qkv_b"]

    def rep(w, times):
        return np.repeat(w.reshape(-1, HD, *w.shape[1:]), times, axis=0).reshape(-1, *w.shape[1:])
    weights = [
        [i["L0_attn_Wq"].T, i["L0_attn_Wk"].T, i["L0_attn_Wv"].T, i["L0_attn_Wo"].T],
        [i["L0_xattn_w_q"], i["L0_xattn_w_k"], i["L0_xattn_w_v"], i["L0_xattn_w_o"]],
        [qkv[0:D].T, qkv[D:2 * D].T, qkv[2 * D:].T, i["L1_attn_proj_w"].T],
        [i["L1_xattn_Wq"].T, i["L1_xattn_Wk"].T, i["L1_xattn_Wv"].T, zz],
        [i["L2_attn_wq"].T, rep(i["L2_attn_wk"], 4).T, rep(i["L2_attn_wv"], 4).T, i["L2_attn_wo"].T],
        [i["L2_xattn_wq"].T, i["L2_xattn_wk"].T, i["L2_xattn_wv"].T, i["L2_xattn_wo"].T],
        [i["L3_attn_Wq"].T, rep(i["L3_attn_Wk"], 16).T, rep(i["L3_attn_Wv"], 16).T, i["L3_attn_Wo"].T],
        [i["L3_xattn_wq_w"].T, i["L3_xattn_wk_w"].T, i["L3_xattn_wv_w"].T, i["L3_xattn_wo_w"].T],
        [i["L3_ffn_Wq"], i["L3_ffn_Wk"], i["L3_ffn_Wv"], i["L3_ffn_Wo"]],
    ]
    bq = [z, i["L0_xattn_b_q"], b3[0:D], i["L1_xattn_bq"], z, z, i["L3_attn_bq"], i["L3_xattn_wq_b"], z]
    bk = [z, i["L0_xattn_b_k"], b3[D:2 * D], i["L1_xattn_bk"], z, z, z, i["L3_xattn_wk_b"], z]
    bv = [z, i["L0_xattn_b_v"], b3[2 * D:], i["L1_xattn_bv"], z, z, rep(i["L3_attn_bv"], 16), i["L3_xattn_wv_b"], z]
    bo = [i["L0_attn_bo"], i["L0_xattn_b_o"], i["L1_attn_proj_b"], z, z, i["L2_xattn_bo"], i["L3_attn_bo"],
          i["L3_xattn_wo_b"], z]
    return {
        "rel_rev": np.concatenate([i["L1_attn_rel_pos_emb"][::-1], np.zeros((1, D), np.float32)]),
        "bit_w": np.stack([i["L1_ffn_w_gate"].T, i["L1_ffn_w_up"].T,
                           i["L1_ffn_w_down"].T.reshape(4, P, D).transpose(1, 0, 2).reshape(P, 4 * D)]).transpose(1, 0, 2),
        "bits": np.broadcast_to((1 << np.arange(29, -1, -1)).astype(np.int32), (P, 30)),
        "e_bias": i["L0_ffn_e_bias"],
        "sh_gate_L0_ffn": i["L0_ffn_shared_gate"].T,
        "sh_up_L0_ffn": i["L0_ffn_shared_up"].T,
        "sh_down_L0_ffn": i["L0_ffn_shared_down"].T.reshape(1, P, D).transpose(1, 0, 2),
        "router_L0_ffn": i["L0_ffn_gate_weight"].T,
        "e_w13": np.concatenate([i["L0_ffn_w1"], i["L0_ffn_w3"]], axis=1).transpose(0, 2, 1).reshape(64 * D, 128),
        "e_w2": i["L0_ffn_w2"].transpose(0, 2, 1).reshape(64 * 64, D),
        "sh_gate_L2_ffn": i["L2_ffn_sh_gate_w"].T,
        "sh_up_L2_ffn": i["L2_ffn_sh_up_w"].T,
        "sh_down_L2_ffn": i["L2_ffn_sh_down_w"].T.reshape(2, P, D).transpose(1, 0, 2),
        "router_L2_ffn": i["L2_ffn_gate_w"].T,
        "g_w": np.concatenate([
            i["L2_ffn_gw"].transpose(0, 2, 1), i["L2_ffn_up_w"].transpose(0, 2, 1),
            i["L2_ffn_down_w"].transpose(0, 2, 1).reshape(16, 4, P, D).transpose(0, 2, 1, 3).reshape(16, P, 4 * D),
            i["L2_ffn_gb"].reshape(16, 4, P).transpose(0, 2, 1), i["L2_ffn_up_b"].reshape(16, 4, P).transpose(0, 2, 1),
            np.broadcast_to(i["L2_ffn_down_b"][:, None, :], (16, P, D))], axis=2).reshape(16 * P, -1),
        "moe_gate": i["L3_ffn_Wg"],
        "moe_w1": i["L3_ffn_W1"].transpose(1, 0, 2).reshape(D, ME * MH),
        "moe_w2": i["L3_ffn_W2"].reshape(4, P, D).transpose(1, 0, 2),
        "x": i["x"].reshape(T, D),
        "ctxT": i["ctx_1024"].reshape(T, D).T,
        "consts": constants(),
        "attn_w": np.stack([np.stack(w) for w in weights]).transpose(2, 0, 1, 3),
        "bqk": np.stack([np.stack(bq), np.stack(bk)]).transpose(2, 1, 0),
        "post_gain": np.stack([i["L1_xattn_gamma"], i["L1_xattn_beta"], i["L3_xattn_ln_g"], i["L3_xattn_ln_b"]]),
        "norm_cols": np.stack([i["L3_ffn_g1"], i["L3_ffn_b1"], i["L3_ffn_g2"], i["L3_ffn_b2"]]).T,
        "mask": i["mask_Bx1xSxS2_bf0"].reshape(T, S).view(np.uint32),
        "bv": np.stack(bv),
        "bo": np.stack(bo),
        "lora": np.stack([i[f"L0_attn_A{m}"] for m in "qkvo"] + [i[f"L0_attn_B{m}"].T for m in "qkvo"]).transpose(1, 0, 2),
    }


FFNS = ["L0_ffn", "L1_ffn", "L2_ffn", "L3_moe"]
WITH_TRANSPOSE = {"L0_ffn", "L2_ffn", "L3_moe"}
STAGES = ["L0_attn", "L0_xattn", "L0_ffn", "L1_attn", "L1_xattn", "L1_ffn", "L2_attn", "L2_xattn", "L2_ffn",
          "L3_attn", "L3_xattn", "L3_ffn", "L3_moe"]


def kernel(**inputs):
    import concourse.bacc as bacc
    from concourse.bass_utils import run_bass_kernel_spmd

    nc = bacc.Bacc("TRN2", target_bir_lowering=False, num_devices=1)
    given = {n: np.ascontiguousarray(a) for n, a in lay_out({n: np.asarray(a) for n, a in inputs.items()}).items()}
    d = {n: nc.dram_tensor(f"in_{n}", a.shape, mybir.dt.from_np(a.dtype), kind="ExternalInput").ap()
         for n, a in given.items()}
    d["out"] = nc.dram_tensor("out_x", (T, D), F32, kind="ExternalOutput").ap()
    build(nc, d, STAGES)
    got = run_bass_kernel_spmd(nc, [{f"in_{n}": a for n, a in given.items()}], core_ids=[0])
    return got.results[0]["out_x"].reshape(B, S, D)
```

```python
from contextlib import ExitStack, contextmanager

import numpy as np

import concourse.bass as bass
from concourse import mybir

F32 = mybir.dt.float32
U8 = mybir.dt.uint8
U32 = mybir.dt.uint32
I32 = mybir.dt.int32
BF16 = mybir.dt.bfloat16
ALU = mybir.AluOpType
ACT = mybir.ActivationFunctionType
AX = mybir.AxisListType

P = 128
D = 128
S = 64
B = 128
T = B * S
TILES = T // P
QUADS = TILES // 4
QW = 4 * P
HEADS = 16
HD = D // HEADS
GROUPS = 4
GH = HEADS // GROUPS
VW = 2 * (HD + 1)
EPS = 1e-5
MASKED = -1e9
LOWEST = -3e38

ATTENTIONS = ["L0_attn", "L0_xattn", "L1_attn", "L1_xattn", "L2_attn", "L2_xattn", "L3_attn", "L3_xattn", "L3_ffn"]
NA = len(ATTENTIONS)
CROSS = {"L0_xattn", "L1_xattn", "L2_xattn", "L3_xattn"}
SCALES = {a: HD ** -0.5 for a in ATTENTIONS}
SCALES["L1_xattn"] = 1.0
SCALES["L3_xattn"] = 1.0 / (float(np.float32(np.sqrt(np.float16(HD)))) + 1e-8)
OUT_BIAS = {"L0_attn", "L0_xattn", "L1_attn", "L2_xattn", "L3_attn", "L3_xattn"}
POST_NORM = {"L1_xattn": 0, "L3_xattn": 1}
BIASED = {"L0_xattn", "L1_attn", "L2_attn", "L3_xattn"}

C_ID, C_HEAD, C_CAUSAL, C_FUTURE, C_UPPER = 0, 128, 132, 196, 260
C_SLOT = 388 + 384
C_EIGHT = 397 + 384
C_CHUNK = 405 + 384
C_EARLIER = 533 + 384
C_TOKEN0 = 661 + 384
C_END = 725 + 384
ROUTE_SCALE = 2.5



def lasting_semaphores(k, new):
    k.loaded = new("loaded")
    k.made = new("made")
    k.stats_done = new("stats_done")
    k.mv_done = new("mv_done")
    k.var_done = new("var_done")
    k.rstd_done = new("rstd_done")
    k.xn_done = new("xn_done")
    k.held_done = new("held_done")
    k.xT_psum = new("xT_psum")
    k.xT_done = new("xT_done")
    k.qk_psum = new("qk_psum")
    k.q_done = new("q_done")
    k.k_done = new("k_done")
    k.v_psum = new("v_psum")
    k.v_done = new("v_done")
    k.s_psum = new("s_psum")
    k.max_done = new("max_done")
    k.sub_done = new("sub_done")
    k.exp_done = new("exp_done")
    k.pT_psum = new("pT_psum")
    k.pT_done = new("pT_done")
    k.o_psum = new("o_psum")
    k.inv_done = new("inv_done")
    k.on_done = new("on_done")
    k.bias_done = new("bias_done")
    k.oT_psum = new("oT_psum")
    k.oT_done = new("oT_done")
    k.y_psum = new("y_psum")
    k.res_done = new("res_done")
    k.lora_psum = new("lora_psum")
    k.f_stats = new("f_stats")
    k.f_mv = new("f_mv")
    k.f_var = new("f_var")
    k.f_rstd = new("f_rstd")
    k.f_xn = new("f_xn")
    k.f_xT_psum = new("f_xT_psum")
    k.f_xT = new("f_xT")
    k.biased_done = new("biased_done")
    k.maskadd_done = new("maskadd_done")
    k.post_sum = new("post_sum")
    k.post_stats_done = new("post_stats_done")
    k.post_mv_done = new("post_mv_done")
    k.post_var_done = new("post_var_done")
    k.post_rstd_done = new("post_rstd_done")
    k.post_scaled = new("post_scaled")
    k.post_gained = new("post_gained")
    k.post_shifted = new("post_shifted")
    k.post_done = new("post_done")
    k.z_stored = [new("z_stored0"), new("z_stored1")]
    k.z_loaded = [new("z_loaded0"), new("z_loaded1")]
    k.lora_done = new("lora_done")
    k.stored = new("stored")
    k.loaded_late = new("loaded_late")
    k.ctx_loaded = [new("ctx0"), new("ctx1")]
    k.guarded = new("guarded")
    k.sub_part = new("sub_part")
    k.sum_done = new("sum_done")
    k.v_guard = new("v_guard")
    k.src_done = new("src_done")


def relative_bias_semaphores(k, new):
    k.rel_in = new("rel_in")
    k.rel_T = new("rel_T")
    k.rel_out = new("rel_out")
    k.rel_rows = new("rel_rows")
    k.rel_sum = new("rel_sum")
    k.rel_masked = new("rel_masked")
    k.rel_psum = new("rel_psum")


def bitlinear_semaphores(k, new):
    k.bw_chain = new("bw_chain")
    k.bw_sum = new("bw_sum")
    k.bw_psum = new("bw_psum")
    k.b_up = new("b_up")
    k.b_silu = new("b_silu")
    k.b_hchain = new("b_hchain")
    k.b_hT_psum = new("b_hT_psum")
    k.b_hq_done = new("b_hq_done")
    k.b_qchain = new("b_qchain")
    k.b_xT_psum = new("b_xT_psum")
    k.b_xq_done = new("b_xq_done")
    k.b_scaled = new("b_scaled")
    k.b_down = new("b_down")
    k.b_hscaled = new("b_hscaled")
    k.b_res = new("b_res")
    k.b_gate = new("b_gate")
    k.b_xT = new("b_xT")
    k.b_hT = new("b_hT")
    k.bit_loaded = new("bit_loaded")


def dense_moe_semaphores(k, new):
    k.m_chain = new("m_chain")
    k.m_gate = new("m_gate")
    k.m_less = new("m_less")
    k.m_exp = new("m_exp")
    k.m_hidden = new("m_hidden")
    k.m_hT_psum = new("m_hT_psum")
    k.m_h_done = new("m_h_done")
    k.m_held = new("m_held")
    k.m_down = new("m_down")
    k.m_res = new("m_res")
    k.m_hT = new("m_hT")


def routed_semaphores(k, new):
    k.x_out_ready = [new("x_out0"), new("x_out1")]
    k.w_out_ready = [new("w_out0"), new("w_out1")]
    k.score_ready = new("score_ready")
    k.sig_ready = new("sig_ready")
    k.down_ready = new("down_ready")
    k.gated_ready = new("gated_ready")
    k.up_ready = new("up_ready")
    k.hidden_ready = new("hidden_ready")
    k.res_ready = new("res_ready")
    k.gate_ready = new("gate_ready")
    k.logit_ready = new("logit_ready")
    k.spill_ready = new("spill_ready")
    k.zero_ready = new("zero_ready")
    k.ends_ready = new("ends_ready")
    k.slotchain_ready = new("slotchain_ready")
    k.index_ready = new("index_ready")
    k.within_ready = new("within_ready")
    k.rows_ready = [new("rows0"), new("rows1")]
    k.tokenchain_ready = new("tokenchain_ready")
    k.reload_ready = new("reload_ready")
    k.pause_find = new("pause_find")
    k.pause_gather = new("pause_gather")
    k.pause_add = new("pause_add")


def small_experts_semaphores(k, new):
    k.r_chain = new("r_chain")
    k.r_cum = new("r_cum")
    k.r_cum_psum = new("r_cum_psum")
    k.e_y = new("e_y")
    k.e_index = new("e_index")
    k.e_xT_psum = new("e_xT_psum")
    k.e_col = new("e_col")
    k.e_scaled = new("e_scaled")
    k.e_added = new("e_added")
    k.e_sindex = new("e_sindex")
    k.e_sig = new("e_sig")
    k.e_gated = new("e_gated")
    k.e_h3 = new("e_h3")
    k.e_hid = new("e_hid")
    k.e_xT = new("e_xT")
    k.e_h1 = new("e_h1")
    k.e_w_ready = [new(f"e_w{b}") for b in range(4)]
    k.e_x_ready = [new(f"e_x{b}") for b in range(4)]


def large_experts_semaphores(k, new):
    k.r_scoreT = new("r_scoreT")
    k.r_logitT = new("r_logitT")
    k.c_io = new("c_io")
    k.c_zero = new("c_zero")
    k.c_chain = new("c_chain")
    k.c_psum = new("c_psum")
    k.c_chain2 = new("c_chain2")
    k.c_total = new("c_total")
    k.g_biased = new("g_biased")
    k.g_index = new("g_index")
    k.g_xT_psum = new("g_xT_psum")
    k.g_col = new("g_col")
    k.g_scaled = new("g_scaled")
    k.g_added = [new("g_added0"), new("g_added1")]
    k.g_sindex = new("g_sindex")
    k.g_y = new("g_y")
    k.g_silu = new("g_silu")
    k.g_up = new("g_up")
    k.g_hid = new("g_hid")
    k.g_xT = new("g_xT")
    k.g_gate = new("g_gate")
    k.g_w_ready = [new("g_w0"), new("g_w1")]
    k.g_x_ready = [new("g_x0"), new("g_x1")]


class Kernel:
    pass


SUM_BACK = {"L1_xattn": 5, "L3_xattn": 4}


@contextmanager
def phase(k, *makers):
    handles = []
    k.phases += 1

    def new(name):
        handles.append(k.nc.alloc_semaphore(name=f"{name}_phase{k.phases}"))
        return handles[-1]
    for semaphores in makers:
        semaphores(k, new)
    yield
    k.nc.clear_and_free_semaphores(handles)
    k.nc.all_engine_barrier()


def depth_of(name):
    return SUM_BACK[name] + 2 if name in POST_NORM else 5


def tile_pipeline(eng, step, depth, count=TILES, unroll=2):
    lead = -(-depth // unroll) * unroll
    for it in range(lead):
        step(it, it % unroll, count)
    with eng.Fori(lead // unroll, count // unroll) as group:
        for u in range(unroll):
            step(unroll * group + u, u, None)
    for it in range(count, count + depth - 1):
        step(it, it % unroll, count)


def ends_free(it, par):
    return it - par + 2


def active(it, back, ends):
    return ends is None or 0 <= it - back < ends


def positive(value):
    return not isinstance(value, int) or value > 0



def attention_loads(k, sp, name, n):
    if name not in CROSS:
        return

    def step(it, par, ends):
        if active(it, 0, ends):
            if positive(k.before("cross", name) * TILES + it - 1):
                sp.wait_ge(k.src_done, k.before("cross", name) * TILES + it - 1)
            sp.dma_start(k.ctxT[:, par, :], k.d["ctxT"][:, bass.ds(it * P, P)]).then_inc(k.ctx_loaded[par], 16)
        if name == "L1_xattn" and active(it, 3, ends):
            sp.wait_ge(k.on_done, 2 * (n * TILES + it - 2))
            for b in range(2):
                sp.dma_start(k.z_dram[bass.ds((it - 3) * P + S * b, S), :]
                              .rearrange("s c -> (s c)").rearrange("(h q d) -> q h d", h=HEADS, d=HD),
                             k.o[S * b:S * b + S, 1 - par, :].rearrange("p (h d) -> p h d", d=HD)
                             ).then_inc(k.z_stored[1 - par], 16)
        if name == "L1_xattn" and active(it, 4, ends):
            sp.wait_ge(k.z_stored[par], 16 * (it - 2 - par))
            if ends is not None:
                if positive(2 * (k.before("post", name) * TILES + it - 5)):
                    sp.wait_ge(k.post_sum, 2 * (k.before("post", name) * TILES + it - 5))
            sp.dma_start(k.z[:, par, :], k.z_dram[bass.ds((it - 4) * P, P), :]).then_inc(k.z_loaded[par], 16)
    tile_pipeline(sp, step, depth_of(name))


def attention_pool(k, pool, name, n):
    nc = k.nc

    def step(it, par, ends):
        if active(it, 0, ends):
            g = n * TILES + it
            pool.wait_ge(k.var_done, g + 1)
            if positive(g - 1):
                pool.wait_ge(k.xn_done, g - 1)
            nc.gpsimd.tensor_tensor(k.rstd[:, par, 0:1], k.vareps[:, par, 0:1], k.half_power[:, 0:1],
                                    ALU.pow).then_inc(k.rstd_done, 1)
            if name in POST_NORM:
                pool.wait_ge(k.xn_done, g + 1)
                nc.gpsimd.tensor_copy(k.held[:, bass.ds(it * P, P)], k.xn[:, par, :]).then_inc(k.held_done, 1)
        back = SUM_BACK.get(name)
        if back and active(it, back, ends):
            q = k.before("post", name) * TILES + it - back
            buf = (par + back) % 2
            pool.wait_ge(k.post_var_done, q + 1)
            if positive(q - 1):
                pool.wait_ge(k.post_scaled, q - 1)
            nc.gpsimd.tensor_tensor(k.rstd[:, buf, 1:2], k.vareps[:, buf, 1:2], k.half_power[:, 0:1],
                                    ALU.pow).then_inc(k.post_rstd_done, 1)
    tile_pipeline(pool, step, depth_of(name))


def attention_pe(k, pe, name, n):
    nc = k.nc
    w = k.attn_w[:, ATTENTIONS.index(name), :, :]
    wq, wk, wv, wo = (w[:, m, :] for m in range(4))
    cross = name in CROSS
    project_out = name != "L1_xattn"

    def mix_values(t, b, half):
        g = n * TILES + t
        pe.wait_ge(k.v_done, 2 * (g + 1))
        pe.wait_ge(k.pT_done, 2 * g + half + 1)
        for j in range(4 * half, 4 * half + 4):
            mm = nc.tensor.matmul(k.ps_o[:, 2 * VW * j:2 * VW * (j + 1)], k.probT[:, b, j * P:(j + 1) * P],
                                  k.vblock[:, b, j, :, :].rearrange("p b c -> p (b c)"), start=True, stop=True)
        if half:
            mm.then_inc(k.o_psum, 1)

    def step(it, par, ends):
        if active(it, 4, ends) and project_out:
            g = n * TILES + it - 4
            pe.wait_ge(k.on_done, 2 * (g + 1))
            if positive(g):
                pe.wait_ge(k.res_done, g)
            if positive(g):
                pe.wait_ge(k.oT_done, g)
            if active(it, 2, ends):
                pe.wait_ge(k.xT_done, g + 3)
                pe.wait_ge(k.v_done, 2 * (g + 3))
            nc.tensor.transpose(k.ps_oT, k.o[:, par, :], k.ident).then_inc(k.oT_psum, 1)
        elif active(it, 4, ends):
            pe.sem_inc(k.oT_psum, 1)
            pe.sem_inc(k.y_psum, 1)
        if active(it, 1, ends):
            g = n * TILES + it - 1
            pe.wait_ge(k.xn_done, g + 1)
            if positive(g - 3):
                pe.wait_ge(k.res_done, g - 3)
            if positive(g):
                pe.wait_ge(k.xT_done, g)
                pe.wait_ge(k.v_done, 2 * g)
            nc.tensor.transpose(k.ps_xT, k.xn[:, 1 - par, :], k.ident).then_inc(k.xT_psum, 1)
        if active(it, 3, ends):
            g = n * TILES + it - 3
            pe.wait_ge(k.exp_done, g + 1)
            if positive(2 * g):
                pe.wait_ge(k.on_done, 2 * g)
            for half in range(2):
                if positive(2 * g + half - 1):
                    pe.wait_ge(k.pT_done, 2 * g + half - 1)
                for j in range(4):
                    mm = nc.tensor.transpose(k.ps_pT[:, half, j * P:(j + 1) * P],
                                             k.prob[:, 1 - par, (4 * half + j) * P:(4 * half + j + 1) * P], k.ident)
                mm.then_inc(k.pT_psum, 1)
        if active(it, 1, ends):
            g = n * TILES + it - 1
            pe.wait_ge(k.xT_done, g + 1)
            if positive(g):
                pe.wait_ge(k.q_done, g)
                pe.wait_ge(k.k_done, GH * g)
            if cross:
                pe.wait_ge(k.src_done, k.before("cross", name) * TILES + it)
            src = k.srcT[:, 1 - par, :, 0, :]
            nc.tensor.matmul(k.ps_q, wq, k.xnT[:, 1 - par, :] if cross else src, start=True, stop=True)
            nc.tensor.matmul(k.ps_k, wk, src, start=True, stop=True).then_inc(k.qk_psum, 1)
        if active(it, 3, ends):
            mix_values(it - 3, 1 - par, 0)
        if active(it, 1, ends):
            if active(it, 4, ends):
                pe.wait_ge(k.oT_done, g - 2)
            for b in range(2):
                twice = k.srcT[:, 1 - par, b, :, :].rearrange("p o s -> p (o s)")
                mm = nc.tensor.matmul(k.ps_v[:, b, :], twice, wv, start=True, stop=True)
            mm.then_inc(k.v_psum, 1)
        if active(it, 4, ends) and project_out:
            g = n * TILES + it - 4
            pe.wait_ge(k.oT_done, g + 1)
            nc.tensor.matmul(k.ps_y, k.oT[:, par, :], wo, start=True, stop=True).then_inc(k.y_psum, 1)
        if active(it, 3, ends):
            mix_values(it - 3, 1 - par, 1)
        if active(it, 1, ends):
            g = n * TILES + it - 1
            pe.wait_ge(k.q_done, g + 1)
            pe.wait_ge(k.k_done, GH * (g + 1))
            if positive(g):
                pe.wait_ge(k.sub_done, g)
            for b in range(2):
                for q in range(GROUPS):
                    rows = slice(32 * q, 32 * q + 32)
                    mm = nc.tensor.matmul(
                        k.scores[S * b:S * b + S, q, 0:GH * S],
                        k.qT[rows, 1 - par, S * b:S * b + S],
                        k.kblock[rows, 1 - par, :, S * b:S * b + S],
                        start=True, stop=True, tile_position=(32 * q, S * b))
            mm.then_inc(k.s_psum, 1)
    tile_pipeline(pe, step, depth_of(name))


def attention_act(k, act, name, n):
    nc = k.nc
    a = ATTENTIONS.index(name)

    def twice(ap):
        return ap.rearrange("p (b o s) -> p b o s", b=2, o=1).broadcast_to([P, 2, 2, S])

    def step(it, par, ends):
        if active(it, 1, ends):
            g = n * TILES + it - 1
            act.wait_ge(k.xT_psum, g + 1)
            if positive(g - 1):
                act.wait_ge(k.v_psum, g - 1)
            if name == "L3_ffn":
                nc.scalar.activation(k.srcT[:, 1 - par, :, :, :], twice(k.ps_xT), ACT.Identity, scale=k.norm_cols[:, 0:1],
                                     bias=k.norm_cols[:, 1:2]).then_inc(k.xT_done, 1)
            elif name in CROSS:
                nc.scalar.activation(k.xnT[:, 1 - par, :], k.ps_xT, ACT.Copy).then_inc(k.xT_done, 1)
            else:
                nc.scalar.activation(k.srcT[:, 1 - par, :, :, :], twice(k.ps_xT), ACT.Copy).then_inc(k.xT_done, 1)
        if active(it, 4, ends) and name != "L1_xattn":
            g = n * TILES + it - 4
            act.wait_ge(k.oT_psum, g + 1)
            if positive(g - 1):
                act.wait_ge(k.y_psum, g - 1)
            nc.scalar.activation(k.oT[:, par, :], k.ps_oT, ACT.Copy).then_inc(k.oT_done, 1)
        elif active(it, 4, ends):
            act.sem_inc(k.oT_done, 1)
        if active(it, 3, ends):
            g = n * TILES + it - 3
            if positive(g - 1):
                act.wait_ge(k.o_psum, g - 1)
            for half in range(2):
                act.wait_ge(k.pT_psum, 2 * g + half + 1)
                nc.scalar.activation(k.probT[:, 1 - par, half * 512:half * 512 + 512], k.ps_pT[:, half, :],
                                     ACT.Copy).then_inc(k.pT_done, 1)
        if active(it, 1, ends):
            g = n * TILES + it - 1
            act.wait_ge(k.qk_psum, g + 1)
            if positive(g - 1):
                act.wait_ge(k.s_psum, g - 1)
            nc.scalar.activation(k.qT[:, 1 - par, :], k.ps_q, ACT.Identity, bias=k.bqk[:, a, 0:1]).then_inc(k.q_done, 1)
            for h in range(GH):
                nc.scalar.activation(k.kblock[:, 1 - par, h, :], k.ps_k, ACT.Identity, scale=k.key_scale[:, a, h:h + 1],
                                     bias=k.key_bias[:, a, h:h + 1]).then_inc(k.k_done, 1)
        if active(it, 2, ends):
            g = n * TILES + it - 2
            act.wait_ge(k.sub_done, g + 1)
            if name != "L3_xattn":
                nc.scalar.activation(k.prob[:, par, :], k.prob[:, par, :], ACT.Exp).then_inc(k.exp_done, 1)
            else:
                act.sem_inc(k.exp_done, 1)
        if active(it, 0, ends) and name in CROSS:
            act.wait_ge(k.ctx_loaded[par], 8 * (k.before("cross", name) * TILES + ends_free(it, par)))
            if positive(n * TILES + it - 1):
                act.wait_ge(k.v_psum, n * TILES + it - 1)
            nc.scalar.activation(k.srcT[:, par, :, :, :], twice(k.ctxT[:, par, :]), ACT.Copy).then_inc(k.src_done, 1)
    tile_pipeline(act, step, depth_of(name))


def attention_dve(k, dve, name, n):
    nc = k.nc
    a = ATTENTIONS.index(name)
    scores = k.scores[:, :, 0:GH * S]
    heads4 = scores.rearrange("p g (h s) -> p g h s", h=GH)
    softmax = name != "L3_xattn"
    back = SUM_BACK.get(name)
    stream = k.held if name == "L3_ffn" else k.x

    def post_norm_stats(t, buf, g):
        q = k.before("post", name) * TILES + t
        post, src = k.post[:, buf, :], k.held[:, bass.ds(t * P, P)]
        dve.wait_ge(k.held_done, q + 1)
        if positive(q - 1):
            dve.wait_ge(k.post_done, q - 1)
        if name == "L1_xattn":
            dve.wait_ge(k.z_loaded[buf], 8 * (t - buf + 2))
            nc.vector.tensor_tensor(post, k.z[:, buf, :], src, ALU.add).then_inc(k.post_sum, 2)
        else:
            nc.vector.tensor_tensor(post, src, k.bo[:, a, :], ALU.add).then_inc(k.post_sum, 1)
            dve.wait_ge(k.post_sum, 2 * q + 1)
            dve.wait_ge(k.y_psum, g + 1)
            nc.vector.tensor_tensor(post, post, k.ps_y, ALU.add).then_inc(k.post_sum, 1)
            dve.wait_ge(k.post_sum, 2 * (q + 1))
            dve.sem_inc(k.res_done, 1)
        dve.wait_ge(k.post_sum, 2 * (q + 1))
        nc.vector.bn_stats(k.post_stats[:, buf, :], post).then_inc(k.post_stats_done, 1)
        dve.wait_ge(k.post_stats_done, q + 1)
        nc.vector.memset(k.pause[:, 1:2], 0.0)
        nc.vector.bn_aggr(k.post_meanvar[:, buf, 0:2], k.post_stats[:, buf, :]).then_inc(k.post_mv_done, 1)
        dve.wait_ge(k.post_mv_done, q + 1)
        nc.vector.tensor_scalar(k.vareps[:, buf, 1:2], k.post_meanvar[:, buf, 1:2], EPS, None,
                                ALU.add).then_inc(k.post_var_done, 1)

    def post_norm_finish(t, buf):
        q = k.before("post", name) * TILES + t
        post, xt = k.post[:, buf, :], k.x[:, bass.ds(t * P, P)]
        m = POST_NORM[name]
        dve.wait_ge(k.post_rstd_done, q + 1)
        nc.vector.tensor_scalar(post, post, k.post_meanvar[:, buf, 0:1], k.rstd[:, buf, 1:2], ALU.subtract,
                                ALU.mult).then_inc(k.post_scaled, 1)
        dve.wait_ge(k.post_scaled, q + 1)
        nc.vector.tensor_tensor(post, post, k.post_gain[:, 2 * m, :], ALU.mult).then_inc(k.post_gained, 1)
        nc.vector.tensor_tensor(xt, xt, k.post_gain[:, 2 * m + 1, :], ALU.add).then_inc(k.post_shifted, 1)
        dve.wait_ge(k.post_gained, q + 1)
        dve.wait_ge(k.post_shifted, q + 1)
        nc.vector.tensor_tensor(xt, xt, post, ALU.add).then_inc(k.post_done, 1)

    def values_of(it, par):
        g = n * TILES + it - 1
        dve.wait_ge(k.v_psum, g + 1)
        if positive(g - 1):
            dve.wait_ge(k.o_psum, g - 1)
        value, bias = k.ps_v, k.bv[:, a, :].rearrange("p (o c) -> p o c", o=1).broadcast_to([P, 2, D])
        if name == "L1_xattn":
            if positive(2 * g):
                dve.wait_ge(k.v_done, 2 * g)
            nc.vector.tensor_tensor(k.v_low[:, :, :], value, bias, ALU.add).then_inc(k.v_guard, 1)
            dve.wait_ge(k.v_guard, 3 * it - 2)
            nc.vector.tensor_scalar(k.v_high[:, :, :], k.v_low[:, :, :], 0.0, None, ALU.max).then_inc(k.v_guard, 1)
            dve.wait_ge(k.v_guard, 3 * it - 1)
            nc.vector.tensor_scalar(k.v_low[:, :, :], k.v_low[:, :, :], 0.0, None, ALU.min).then_inc(k.v_guard, 1)
            dve.wait_ge(k.v_guard, 3 * it)
            value, bias = k.v_low, k.v_high[:, :, :]
        for odd in range(2):
            rows = slice(S * odd, S * odd + S)
            v, add = (t[rows, :, :].rearrange("p b (j e d) -> p b j e d", e=2, d=HD)[:, :, :, odd, :]
                      for t in (value, bias))
            out = k.vblock[rows, 1 - par, :, :, (HD + 1) * odd:(HD + 1) * odd + HD].rearrange("p j b d -> p b j d")
            nc.vector.tensor_tensor(out, v, add, ALU.add).then_inc(k.v_done, 1)
        if name == "L3_xattn":
            if positive(k.before("biased", name) * TILES + it - 2):
                dve.wait_ge(k.biased_done, k.before("biased", name) * TILES + it - 2)
            mask = k.mask_raw[:, bass.ds((it - 1) * (S // 4), S // 4)].bitcast(U8)
            nc.vector.tensor_scalar(k.maskadd[:, 1 - par, :], mask, LOWEST, -LOWEST, ALU.mult,
                                    ALU.mult).then_inc(k.maskadd_done, 1)

    def outputs_of(it, par):
        g = n * TILES + it - 3
        mix = 1 - par
        dve.wait_ge(k.o_psum, g + 1)
        if positive(g - 1):
            dve.wait_ge(k.oT_psum, g - 1)
        if name == "L1_xattn":
            if positive(16 * (it - 4 + par)):
                dve.wait_ge(k.z_stored[mix], 16 * (it - 4 + par))
        own = []
        for b in range(2):
            rows = slice(S * b, S * b + S)
            psum = k.ps_o[rows, :].rearrange("p (j b h c) -> p j b h c", j=HEADS // 2, b=2, h=2)[:, :, b, :, :]
            out = k.o[rows, mix, :].rearrange("p (j h d) -> p j h d", h=2, d=HD)
            sums = k.rowinv[rows, mix, :].rearrange("p (j h o) -> p j h o", h=2, o=1)
            own.append((psum, out, sums))
        if softmax:
            for psum, out, sums in own:
                if name == "L1_xattn":
                    nc.vector.tensor_scalar(sums, psum[:, :, :, HD:HD + 1], 1e-30, None,
                                            ALU.max).then_inc(k.sum_done, 1)
                else:
                    nc.vector.reciprocal(sums, psum[:, :, :, HD:HD + 1]).then_inc(k.inv_done, 1)
            if name == "L1_xattn":
                dve.wait_ge(k.sum_done, 2 * (it - 2))
                nc.vector.reciprocal(k.rowinv[:, mix, :], k.rowinv[:, mix, :]).then_inc(k.inv_done, 2)
            dve.wait_ge(k.inv_done, 2 * (g + 1))
            for psum, out, sums in own:
                nc.vector.tensor_tensor(out, psum[:, :, :, 0:HD], sums.broadcast_to([S, HEADS // 2, 2, HD]),
                                        ALU.mult).then_inc(k.on_done, 1)
        else:
            dve.sem_inc(k.inv_done, 2)
            for psum, out, sums in own:
                nc.vector.tensor_copy(out, psum[:, :, :, 0:HD]).then_inc(k.on_done, 1)

    def step(it, par, ends):
        if active(it, 0, ends):
            g = n * TILES + it
            if positive(g):
                dve.wait_ge(k.xn_done, g)
            nc.vector.bn_stats(k.stats[:, par, :], stream[:, bass.ds(it * P, P)]).then_inc(k.stats_done, 1)
            dve.wait_ge(k.stats_done, g + 1)
            nc.vector.memset(k.pause[:, 0:1], 0.0)
            nc.vector.bn_aggr(k.meanvar[:, par, 0:2], k.stats[:, par, :]).then_inc(k.mv_done, 1)
            dve.wait_ge(k.mv_done, g + 1)
            nc.vector.tensor_scalar(k.vareps[:, par, 0:1], k.meanvar[:, par, 1:2], EPS, None,
                                    ALU.add).then_inc(k.var_done, 1)
        if active(it, 2, ends):
            g = n * TILES + it - 2
            prob4 = k.prob[:, par, :].rearrange("p (g h s) -> p g h s", g=GROUPS, h=GH)
            rowmax = k.rowmax[:, par, :]
            dve.wait_ge(k.s_psum, g + 1)
            if name in BIASED:
                if positive(2 * (g - 1)):
                    dve.wait_ge(k.pT_psum, 2 * (g - 1))
                if name == "L1_attn":
                    add = k.relpos[:, :].rearrange("p (g h s) -> p g h s", g=GROUPS, h=GH)
                else:
                    if name == "L3_xattn":
                        dve.wait_ge(k.maskadd_done, it - 1)
                        add = k.maskadd[:, par, :]
                    else:
                        c = C_CAUSAL if name == "L0_xattn" else C_FUTURE
                        add = k.consts[:, c:c + S]
                    add = add.rearrange("p (g h s) -> p g h s", g=1, h=1).broadcast_to([P, GROUPS, GH, S])
                nc.vector.tensor_tensor(prob4, heads4, add, ALU.add).then_inc(k.biased_done, 1)
                dve.wait_ge(k.biased_done, k.before("biased", name) * TILES + it - 1)
            if softmax:
                nc.vector.tensor_reduce(rowmax.rearrange("p (g h) -> p g h", g=GROUPS),
                                        prob4 if name in BIASED else heads4, AX.X, ALU.max).then_inc(k.max_done, 1)
            if name == "L1_xattn":
                dve.wait_ge(k.max_done, g + 1)
                nc.vector.tensor_scalar(rowmax, rowmax, LOWEST / 3, None, ALU.max).then_inc(k.guarded, 1)
        if active(it, 0, ends):
            g = n * TILES + it
            dve.wait_ge(k.rstd_done, g + 1)
            if positive(g - 1):
                dve.wait_ge(k.xT_psum, g - 1)
            nc.vector.tensor_scalar(k.xn[:, par, :], stream[:, bass.ds(it * P, P)], k.meanvar[:, par, 0:1],
                                    k.rstd[:, par, 0:1], ALU.subtract, ALU.mult).then_inc(k.xn_done, 1)
        if active(it, 2, ends):
            g = n * TILES + it - 2
            if softmax:
                dve.wait_ge(k.max_done, g + 1)
                if name == "L1_xattn":
                    dve.wait_ge(k.guarded, it - 1)
                if positive(2 * (g - 1)):
                    dve.wait_ge(k.pT_psum, 2 * (g - 1))
                if name == "L1_xattn":
                    for q in range(GROUPS):
                        nc.vector.scalar_tensor_tensor(
                            prob4[:, q, :, :], heads4[:, q, :, :], LOWEST,
                            rowmax[:, GH * q:GH * (q + 1)].rearrange("p (h o) -> p h o", o=1).broadcast_to([P, GH, S]),
                            ALU.max, ALU.subtract).then_inc(k.sub_part, 1)
                    dve.wait_ge(k.sub_part, GROUPS * (it - 1))
                    dve.sem_inc(k.sub_done, 1)
                else:
                    nc.vector.tensor_tensor(
                        prob4, prob4 if name in BIASED else heads4,
                        rowmax.rearrange("p (g h o) -> p g h o", g=GROUPS, o=1)
                              .broadcast_to([P, GROUPS, GH, S]), ALU.subtract).then_inc(k.sub_done, 1)
            else:
                dve.sem_inc(k.max_done, 1)
                dve.sem_inc(k.sub_done, 1)
        if active(it, 4, ends) and name not in POST_NORM:
            g = n * TILES + it - 4
            xt = stream[:, bass.ds((it - 4) * P, P)]
            if name in OUT_BIAS:
                nc.vector.tensor_tensor(xt, xt, k.bo[:, a, :], ALU.add).then_inc(k.bias_done, 1)
                dve.wait_ge(k.bias_done, k.before("out", name) * TILES + it - 3)
            dve.wait_ge(k.y_psum, g + 1)
            nc.vector.tensor_tensor(xt, xt, k.ps_y, ALU.add).then_inc(k.res_done, 1)
        if back and active(it, back, ends):
            post_norm_stats(it - back, (par + back) % 2, n * TILES + it - back)
        if name == "L1_xattn" and active(it, 4, ends):
            dve.sem_inc(k.res_done, 1)
        for stage, behind in [(values_of, 1), (outputs_of, 3)][::1 if name in BIASED else -1]:
            if active(it, behind, ends):
                stage(it, par)
        if back and active(it, back + 1, ends):
            post_norm_finish(it - back - 1, (par + back + 1) % 2)
    tile_pipeline(dve, step, depth_of(name))


def relative_bias(k, ps):
    nc, emb, table, tableT = k.nc, k.rel_emb, k.rel_table, k.rel_tableT
    with nc.Block() as block:
        @block.sync
        def _(sp):
            sp.dma_start(emb[:, :, :], k.d["rel_rev"].rearrange("(a p) c -> p a c", p=P)).then_inc(k.rel_in, 16)
            sp.wait_ge(k.rel_T, 1)
            sp.dma_start(k.rel_dram, tableT[:, :]).then_inc(k.rel_out, 16)
            sp.wait_ge(k.rel_out, 16)

        @block.vector
        def _(dve):
            dve.wait_ge(k.rel_in, 16)
            nc.vector.tensor_reduce(table[:, :, :], emb[:, :, :].rearrange("p a (h d) -> p a h d", d=HD), AX.X,
                                    ALU.add).then_inc(k.rel_sum, 1)

        @block.tensor
        def _(pe):
            pe.wait_ge(k.rel_sum, 1)
            for a in range(2):
                nc.tensor.transpose(ps[0:HEADS, 1, a * P:(a + 1) * P], table[:, a, :],
                                    k.ident).then_inc(k.rel_psum, 1)

        @block.scalar
        def _(act):
            act.wait_ge(k.rel_psum, 2)
            nc.scalar.activation(tableT[:, :], ps[0:HEADS, 1, 0:2 * P], ACT.Copy).then_inc(k.rel_T, 1)


def relative_rows(k, sp):
    for q in range(S):
        sp.dma_start(k.relpos[q:q + 1, :].rearrange("p (h s) -> p h s", h=HEADS),
                     k.rel_dram[:, P - 1 - q:P - 1 - q + S].rearrange("h (o s) -> o h s", o=1)
                     ).then_inc(k.rel_rows, 16)
    sp.wait_ge(k.rel_rows, 16 * S)
    sp.dma_start(k.relpos[S:P, :], k.relpos[0:S, :]).then_inc(k.rel_rows, 16)
    sp.wait_ge(k.rel_rows, 16 * (S + 1))


def relative_mask(k):
    nc = k.nc
    with nc.Block() as block:
        @block.vector
        def _(dve):
            future = k.consts[:, C_FUTURE:C_FUTURE + S].rearrange("p (o s) -> p o s", o=1).broadcast_to([P, HEADS, S])
            bias = k.relpos[:, :].rearrange("p (h s) -> p h s", h=HEADS)
            nc.vector.tensor_tensor(bias, bias, future, ALU.add).then_inc(k.rel_masked, 1)
            dve.wait_ge(k.rel_masked, 1)



def pool_pause(k, pool, done, column, t):
    if positive(t):
        pool.wait_ge(done, t)
    k.nc.gpsimd.tensor_tensor(k.pause[:, column:column + 1], k.half_power[:, 0:1], k.half_power[:, 0:1],
                              ALU.add).then_inc(done, 1)


class Count:

    def __init__(self, tile, length):
        self.before, self.length, self.passed = tile * length, length, 0

    def next(self):
        self.passed += 1
        assert self.passed <= self.length
        return self.before + self.passed


def prenorm_pass(k, m):
    nc = k.nc
    with nc.Block() as block:
        @block.vector
        def _(dve):
            def step(it, par, ends):
                if active(it, 0, ends):
                    quad_stats(k, dve, m, k.x, it, par)
                if active(it, 1, ends):
                    quad_norm(k, dve, m, k.x, it - 1, 1 - par, k.held[:, bass.ds((it - 1) * QW, QW)])
            tile_pipeline(dve, step, 2, count=QUADS)
            dve.wait_ge(k.f_xn, (m + 1) * TILES)

        @block.gpsimd
        def _(pool):
            def step(it, par, ends):
                if active(it, 0, ends):
                    quad_pool(k, pool, m, it, par)
            tile_pipeline(pool, step, 2, count=QUADS)


MAGIC = 1.5 * 2.0 ** 23
INNER = 512
QMAX = 127.0


def bitlinear_weights(k, ps):
    nc = k.nc
    with nc.Block() as block:
        @block.sync
        def _(sp):
            sp.dma_start(k.bit_raw, k.d["bit_w"]).then_inc(k.bit_loaded, 16)

        @block.vector
        def _(dve):
            dve.wait_ge(k.bit_loaded, 16)
            count = Count(0, 99)
            for w in range(3):
                raw = k.bit_raw[:, w, :]
                nc.vector.tensor_reduce(k.bit_sum[:, w:w + 1], raw, AX.X, ALU.add, apply_absolute_value=True).then_inc(k.bw_chain, 1)
                dve.wait_ge(k.bw_chain, count.next())
            nc.vector.tensor_copy(k.ident_bf[:, :], k.ident).then_inc(k.bw_sum, 1)
            dve.wait_ge(k.bw_psum, 1)
            nc.vector.tensor_scalar(k.bit_mean[:, 0:3], ps[:, 0, 0:3], 1.0 / (INNER * D), 1e-5, ALU.mult, ALU.max).then_inc(k.bw_chain, 1)
            dve.wait_ge(k.bw_chain, count.next())
            nc.vector.reciprocal(k.bit_inv[:, 0:3], k.bit_mean[:, 0:3]).then_inc(k.bw_chain, 1)
            dve.wait_ge(k.bw_chain, count.next())
            nc.vector.tensor_scalar(k.bit_mean[:, 0:3], k.bit_mean[:, 0:3], 1.0 / QMAX, None, ALU.mult).then_inc(k.bw_chain, 1)
            dve.wait_ge(k.bw_chain, count.next())
            for w in range(3):
                raw = k.bit_raw[:, w, :]
                nc.vector.tensor_scalar(raw, raw, k.bit_inv[:, w:w + 1], MAGIC, ALU.mult, ALU.add).then_inc(k.bw_chain, 1)
                dve.wait_ge(k.bw_chain, count.next())
                nc.vector.tensor_scalar(raw, raw, MAGIC, 1.0, ALU.subtract, ALU.min).then_inc(k.bw_chain, 1)
                dve.wait_ge(k.bw_chain, count.next())
                nc.vector.tensor_scalar(k.bit_w[:, w, :], raw, -1.0, None, ALU.max).then_inc(k.bw_chain, 1)
                dve.wait_ge(k.bw_chain, count.next())

        @block.tensor
        def _(pe):
            pe.wait_ge(k.bw_sum, 1)
            pe.wait_ge(k.bw_chain, 3)
            nc.tensor.matmul(ps[:, 0, 0:3], k.ones[:, :], k.bit_sum[:, 0:3], start=True, stop=True).then_inc(k.bw_psum, 1)


def bitlinear_pass(k, ps, m):
    nc = k.nc
    QL, HL = 8, 12

    def scale_up(dve, chained, count, amax, inv):
        nc.vector.tensor_scalar(amax, amax, 1e-5, None, ALU.max).then_inc(chained, 1)
        dve.wait_ge(chained, count.next())
        nc.vector.reciprocal(inv, amax).then_inc(chained, 1)
        dve.wait_ge(chained, count.next())
        nc.vector.tensor_scalar(inv, inv, QMAX, None, ALU.mult).then_inc(chained, 1)
        dve.wait_ge(chained, count.next())

    with nc.Block() as block:
        @block.gpsimd
        def _(pool):
            def step(it, par, ends):
                if active(it, 0, ends):
                    quad_pool(k, pool, m, it, par)
            tile_pipeline(pool, step, 3, count=QUADS)

        @block.vector
        def _(dve):
            def step(it, par, ends):
                if active(it, 0, ends):
                    quad_stats(k, dve, m, k.x, it, par)
                if active(it, 1, ends):
                    t, b = it - 1, 1 - par
                    count = Count(t, HL)
                    for q in range(4):
                        dve.wait_ge(k.b_up, 4 * t + q + 1)
                        dve.wait_ge(k.b_silu, 4 * t + q + 1)
                        nc.vector.scalar_tensor_tensor(k.b_h[:, q, :], ps[:, 2 + q % 2, :], k.b_scale[:, b, q, 1:2],
                                                       k.b_h[:, q, :], ALU.mult, ALU.mult).then_inc(k.b_hchain, 1)
                        after = count.next()
                    dve.wait_ge(k.b_hchain, after)
                    amax = k.b_hmax[:, b, :]
                    nc.vector.tensor_reduce(amax, k.b_h[:, :, :], AX.X, ALU.max,
                                            apply_absolute_value=True).then_inc(k.b_hchain, 1)
                    dve.wait_ge(k.b_hchain, count.next())
                    scale_up(dve, k.b_hchain, count, amax, k.b_hinv[:, :])
                    for q in range(4):
                        nc.vector.tensor_scalar(k.b_h[:, q, :], k.b_h[:, q, :], k.b_hinv[:, q:q + 1], MAGIC, ALU.mult,
                                                ALU.add).then_inc(k.b_hchain, 1)
                        after = count.next()
                    assert count.passed == HL
                    dve.wait_ge(k.b_hchain, after)
                    for q in range(4):
                        if positive(4 * t + q - 3):
                            dve.wait_ge(k.b_hT_psum, 4 * t + q - 3)
                        nc.vector.tensor_scalar(k.b_hq[:, q, :], k.b_h[:, q, :], MAGIC, QMAX, ALU.subtract,
                                                ALU.min).then_inc(k.b_hq_done, 1)
                if active(it, 0, ends):
                    xn = k.b_xn[:, par, :]
                    if positive(4 * it - 4):
                        dve.wait_ge(k.b_xq_done, 4 * it - 4)
                    quad_norm(k, dve, m, k.x, it, par, xn)
                    dve.wait_ge(k.f_xn, m * TILES + 4 * it + 4)
                    count = Count(it, QL)
                    if positive(4 * it - 4):
                        dve.wait_ge(k.b_silu, 4 * it - 4)
                    amax = k.b_xmax[:, par, :]
                    nc.vector.tensor_reduce(amax, xn.rearrange("p (q c) -> p q c", q=4), AX.X, ALU.max,
                                            apply_absolute_value=True).then_inc(k.b_qchain, 1)
                    dve.wait_ge(k.b_qchain, count.next())
                    scale_up(dve, k.b_qchain, count, amax, k.b_xinv[:, :])
                    for q in range(4):
                        nc.vector.tensor_scalar(xn[:, q * P:(q + 1) * P], xn[:, q * P:(q + 1) * P], k.b_xinv[:, q:q + 1],
                                                MAGIC, ALU.mult, ALU.add).then_inc(k.b_qchain, 1)
                        after = count.next()
                    assert count.passed == QL
                    dve.wait_ge(k.b_qchain, after)
                    if positive(it - 1):
                        dve.wait_ge(k.b_xT_psum, it - 1)
                    nc.vector.tensor_scalar(k.b_xq[:, par, :], xn, MAGIC, QMAX, ALU.subtract,
                                            ALU.min).then_inc(k.b_xq_done, 4)
                    nc.vector.tensor_tensor(
                        k.b_scale[:, par, :, :], amax.rearrange("p (q o) -> p q o", o=1).broadcast_to([P, 4, 2]),
                        k.bit_mean[:, 0:2].rearrange("p (o w) -> p o w", o=1).broadcast_to([P, 4, 2]),
                        ALU.mult).then_inc(k.b_scaled, 1)
                if active(it, 2, ends):
                    t, b = it - 2, par
                    if positive(4 * t):
                        dve.wait_ge(k.b_res, 4 * t)
                    nc.vector.tensor_scalar(k.b_hscale[:, :], k.b_hmax[:, b, :], k.bit_mean[:, 2:3], None,
                                            ALU.mult).then_inc(k.b_hscaled, 1)
                    dve.wait_ge(k.b_down, 4 * t + 4)
                    dve.wait_ge(k.b_hscaled, t + 1)
                    for q in range(4):
                        xt = k.x[:, bass.ds((4 * t + q) * P, P)]
                        nc.vector.scalar_tensor_tensor(xt, ps[:, 6, q * P:(q + 1) * P], k.b_hscale[:, q:q + 1], xt,
                                                       ALU.mult, ALU.add).then_inc(k.b_res, 1)
            tile_pipeline(dve, step, 3, count=QUADS)

        @block.tensor
        def _(pe):
            def transposes(t, q):
                pe.wait_ge(k.b_hq_done, 4 * t + q + 1)
                if positive(4 * t + q - 1):
                    pe.wait_ge(k.b_hT, 4 * t + q - 1)
                hT = ps[:, [5, 7][q % 2], 0:INNER // 2].bitcast(BF16)
                for c in range(4):
                    mm = nc.tensor.transpose(hT[:, c * P:(c + 1) * P], k.b_hq[:, q, c * P:(c + 1) * P], k.ident_bf[:, :])
                mm.then_inc(k.b_hT_psum, 1)

            def down(t, q):
                pe.wait_ge(k.b_hT, 4 * t + q + 1)
                if positive(4 * t):
                    pe.wait_ge(k.b_res, 4 * t)
                for c in range(4):
                    mm = nc.tensor.matmul(ps[:, 6, q * P:(q + 1) * P], k.b_hqT[:, q, c * P:(c + 1) * P],
                                          k.bit_w[:, 2, c * P:(c + 1) * P], start=c == 0, stop=c == 3)
                mm.then_inc(k.b_down, 1)

            def step(it, par, ends):
                if active(it, 1, ends):
                    t, b = it - 1, 1 - par
                    pe.wait_ge(k.b_xT, t + 1)
                    for q in range(4):
                        xqT = k.b_xqT[:, b, q * P:(q + 1) * P]
                        if positive(4 * t + q - 1):
                            pe.wait_ge(k.b_silu, 4 * t + q - 1)
                        nc.tensor.matmul(ps[:, q % 2, :], xqT, k.bit_w[:, 0, :], start=True, stop=True).then_inc(k.b_gate, 1)
                        if q >= 2:
                            pe.wait_ge(k.b_hchain, HL * t + q - 1)
                        elif positive(HL * (t - 1) + 4):
                            pe.wait_ge(k.b_hchain, HL * (t - 1) + 4)
                        nc.tensor.matmul(ps[:, 2 + q % 2, :], xqT, k.bit_w[:, 1, :], start=True, stop=True).then_inc(k.b_up, 1)
                if active(it, 2, ends):
                    t = it - 2
                    transposes(t, 0)
                    for q in range(1, 4):
                        transposes(t, q)
                        down(t, q - 1)
                    down(t, 3)
                if active(it, 0, ends):
                    pe.wait_ge(k.b_xq_done, 4 * it + 4)
                    if positive(it):
                        pe.wait_ge(k.b_xT, it)
                    for q in range(4):
                        mm = nc.tensor.transpose(ps[:, 4, 0:QW // 2].bitcast(BF16)[:, q * P:(q + 1) * P],
                                                 k.b_xq[:, par, q * P:(q + 1) * P], k.ident_bf[:, :])
                    mm.then_inc(k.b_xT_psum, 1)
            tile_pipeline(pe, step, 3, count=QUADS)

        @block.scalar
        def _(act):
            def step(it, par, ends):
                if active(it, 1, ends):
                    t, b = it - 1, 1 - par
                    act.wait_ge(k.b_scaled, t + 1)
                    for q in range(4):
                        act.wait_ge(k.b_gate, 4 * t + q + 1)
                        if positive(4 * t + q - 3):
                            act.wait_ge(k.b_hq_done, 4 * t + q - 3)
                        nc.scalar.activation(k.b_h[:, q, :], ps[:, q % 2, :], ACT.Silu,
                                             scale=k.b_scale[:, b, q, 0:1]).then_inc(k.b_silu, 1)
                if active(it, 2, ends):
                    t = it - 2
                    for q in range(4):
                        act.wait_ge(k.b_hT_psum, 4 * t + q + 1)
                        if positive(4 * t + q - 3):
                            act.wait_ge(k.b_down, 4 * t + q - 3)
                        nc.scalar.activation(k.b_hqT[:, q, :], ps[:, [5, 7][q % 2], 0:INNER // 2].bitcast(BF16),
                                             ACT.Copy).then_inc(k.b_hT, 1)
                if active(it, 0, ends):
                    act.wait_ge(k.b_xT_psum, it + 1)
                    if positive(4 * it - 4):
                        act.wait_ge(k.b_up, 4 * it - 4)
                    nc.scalar.activation(k.b_xqT[:, par, :], ps[:, 4, 0:QW // 2].bitcast(BF16), ACT.Copy).then_inc(k.b_xT, 1)
            tile_pipeline(act, step, 3, count=QUADS)


ME = 8
MH = 64


def dense_moe_pass(k, ps, m):
    nc = k.nc
    GL = 15
    front = k.tf(m) * TILES

    def hT_bank(q):
        return ps[:, 4 + q % 2, :]

    with nc.Block() as block:
        @block.gpsimd
        def _(pool):
            def step(it, par, ends):
                if active(it, 0, ends):
                    quad_pool(k, pool, m, it, par)
            tile_pipeline(pool, step, 3, count=QUADS)

        @block.vector
        def _(dve):
            def gate(t, b):
                count = Count(t, GL)
                logit, top, ex, w = k.m_logit[:, b, :], k.m_top[:, b, :], k.m_ex[:, b, :], k.m_w[:, b, :]

                def by_tile(ap):
                    return ap.rearrange("p (q e) -> p q e", q=4)
                dve.wait_ge(k.m_gate, t + 1)
                nc.vector.tensor_copy(logit, ps[:, 7, 0:4 * ME]).then_inc(k.m_chain, 1)
                dve.wait_ge(k.m_chain, count.next())
                nc.vector.memset(k.pause[:, 0:1], 0.0)
                for q in range(4):
                    nc.vector.max(top[:, ME * q:ME * (q + 1)], logit[:, ME * q:ME * (q + 1)]).then_inc(k.m_chain, 1)
                    after = count.next()
                dve.wait_ge(k.m_chain, after)
                nc.vector.tensor_tensor(by_tile(ex), by_tile(logit),
                                        by_tile(top)[:, :, 0:1].broadcast_to([P, 4, ME]),
                                        ALU.subtract).then_inc(k.m_less, 1)
                nc.vector.memset(k.pause[:, 0:1], 0.0)
                for q in range(4):
                    nc.vector.max_index(k.m_place[:, b, q, :], top[:, ME * q:ME * (q + 1)],
                                        logit[:, ME * q:ME * (q + 1)]).then_inc(k.m_chain, 1)
                    after = count.next()
                dve.wait_ge(k.m_chain, after)
                nc.vector.tensor_tensor(
                    k.m_eq[:, b, :, :, :],
                    k.m_place[:, b, :, 0:2].rearrange("p q (o j) -> p q o j", o=1).broadcast_to([P, 4, ME, 2]),
                    k.consts[:, C_EIGHT:C_EIGHT + ME].rearrange("p (u e o) -> p u e o", u=1, o=1)
                     .broadcast_to([P, 4, ME, 2]), ALU.is_equal).then_inc(k.m_chain, 1)
                dve.wait_ge(k.m_chain, count.next())
                nc.vector.tensor_reduce(by_tile(k.m_sel[:, b, :]), k.m_eq[:, b, :, :, :], AX.X,
                                        ALU.add).then_inc(k.m_chain, 1)
                dve.wait_ge(k.m_chain, count.next())
                dve.wait_ge(k.m_exp, t + 1)
                nc.vector.tensor_tensor(w, ex, k.m_sel[:, b, :], ALU.mult).then_inc(k.m_chain, 1)
                dve.wait_ge(k.m_chain, count.next())
                nc.vector.tensor_reduce(k.m_sum[:, b, 0:4], by_tile(w), AX.X, ALU.add).then_inc(k.m_chain, 1)
                dve.wait_ge(k.m_chain, count.next())
                nc.vector.reciprocal(k.m_sum[:, b, 4:8], k.m_sum[:, b, 0:4]).then_inc(k.m_chain, 1)
                dve.wait_ge(k.m_chain, count.next())
                nc.vector.tensor_tensor(by_tile(w), by_tile(w),
                                        k.m_sum[:, b, 4:8].rearrange("p (q o) -> p q o", o=1).broadcast_to([P, 4, ME]),
                                        ALU.mult).then_inc(k.m_chain, 1)
                dve.wait_ge(k.m_chain, count.next())
                assert count.passed == GL

            def step(it, par, ends):
                if active(it, 0, ends):
                    quad_stats(k, dve, m, k.held, it, par)
                if active(it, 0, ends):
                    if positive(front + 4 * it - 4):
                        dve.wait_ge(k.f_xT_psum, front + 4 * it - 4)
                    quad_norm(k, dve, m, k.held, it, par, k.q_xn[:, par, :])
                if active(it, 1, ends):
                    gate(it - 1, 1 - par)
                if active(it, 1, ends):
                    t, b = it - 1, 1 - par
                    for q in range(4):
                        dve.wait_ge(k.m_hidden, 4 * t + q + 1)
                        if positive(4 * t + q - 3):
                            dve.wait_ge(k.m_hT_psum, 4 * t + q - 3)
                        nc.vector.scalar_tensor_tensor(
                            k.m_h[q].rearrange("p (e h) -> p e h", e=ME), ps[:, q, :].rearrange("p (e h) -> p e h", e=ME),
                            0.0, k.m_w[:, b, ME * q:ME * (q + 1)].rearrange("p (e o) -> p e o", o=1)
                                  .broadcast_to([P, ME, MH]), ALU.max, ALU.mult).then_inc(k.m_h_done, 1)
                if active(it, 2, ends):
                    t = it - 2
                    xt = k.x[:, bass.ds(t * QW, QW)]
                    nc.vector.tensor_tensor(xt, xt, k.held[:, bass.ds(t * QW, QW)], ALU.add).then_inc(k.m_held, 1)
                    dve.wait_ge(k.m_down, 4 * t + 4)
                    dve.wait_ge(k.m_held, t + 1)
                    nc.vector.tensor_tensor(xt, xt, ps[:, 6, :], ALU.add).then_inc(k.m_res, 1)
            tile_pipeline(dve, step, 3, count=QUADS)

        @block.tensor
        def _(pe):
            def transposes(t, q):
                pe.wait_ge(k.m_h_done, 4 * t + q + 1)
                if positive(4 * t + q - 1):
                    pe.wait_ge(k.m_hT, 4 * t + q - 1)
                for c in range(4):
                    mm = nc.tensor.transpose(hT_bank(q)[:, c * P:(c + 1) * P], k.m_h[q][:, c * P:(c + 1) * P], k.ident)
                mm.then_inc(k.m_hT_psum, 1)

            def down(t, q):
                pe.wait_ge(k.m_hT, 4 * t + q + 1)
                if positive(t):
                    pe.wait_ge(k.m_res, t)
                for c in range(4):
                    mm = nc.tensor.matmul(ps[:, 6, q * P:(q + 1) * P], k.m_hTs[q][:, c * P:(c + 1) * P], k.moe_w2[:, c, :],
                                          start=c == 0, stop=c == 3)
                mm.then_inc(k.m_down, 1)

            def step(it, par, ends):
                if active(it, 1, ends):
                    t, b = it - 1, 1 - par
                    pe.wait_ge(k.f_xT, front + 4 * t + 4)
                    for q in range(4):
                        mm = nc.tensor.matmul(ps[:, 7, ME * q:ME * (q + 1)], k.q_xnT[:, b, q * P:(q + 1) * P],
                                              k.moe_gate[:, :], start=True, stop=True)
                    mm.then_inc(k.m_gate, 1)
                    for q in range(4):
                        if positive(4 * t + q - 3):
                            pe.wait_ge(k.m_h_done, 4 * t + q - 3)
                        nc.tensor.matmul(ps[:, q, :], k.q_xnT[:, b, q * P:(q + 1) * P], k.moe_w1[:, :], start=True,
                                         stop=True).then_inc(k.m_hidden, 1)
                if active(it, 0, ends):
                    pe.wait_ge(k.f_xn, m * TILES + 4 * it + 4)
                    if positive(front + 4 * it):
                        pe.wait_ge(k.f_xT, front + 4 * it)
                    if positive(GL * (it - 1) + 1):
                        pe.wait_ge(k.m_chain, GL * (it - 1) + 1)
                    for q in range(4):
                        mm = nc.tensor.transpose(ps[:, 7, q * P:(q + 1) * P], k.q_xn[:, par, q * P:(q + 1) * P], k.ident)
                    mm.then_inc(k.f_xT_psum, 4)
                if active(it, 2, ends):
                    t = it - 2
                    transposes(t, 0)
                    for q in range(1, 4):
                        transposes(t, q)
                        down(t, q - 1)
                    down(t, 3)
            tile_pipeline(pe, step, 3, count=QUADS)

        @block.scalar
        def _(act):
            def step(it, par, ends):
                if active(it, 1, ends):
                    t, b = it - 1, 1 - par
                    act.wait_ge(k.m_less, t + 1)
                    nc.scalar.activation(k.m_ex[:, b, :], k.m_ex[:, b, :], ACT.Exp).then_inc(k.m_exp, 1)
                if active(it, 0, ends):
                    act.wait_ge(k.f_xT_psum, front + 4 * it + 4)
                    if positive(4 * (it - 1)):
                        act.wait_ge(k.m_hidden, 4 * (it - 1))
                    nc.scalar.activation(k.q_xnT[:, par, :], ps[:, 7, :], ACT.Identity, scale=k.norm_cols[:, 2:3],
                                         bias=k.norm_cols[:, 3:4]).then_inc(k.f_xT, 4)
                if active(it, 2, ends):
                    t = it - 2
                    for q in range(4):
                        act.wait_ge(k.m_hT_psum, 4 * t + q + 1)
                        if positive(4 * t + q - 3):
                            act.wait_ge(k.m_down, 4 * t + q - 3)
                        nc.scalar.activation(k.m_hTs[q], hT_bank(q), ACT.Copy).then_inc(k.m_hT, 1)
            tile_pipeline(act, step, 3, count=QUADS)



class Routed:

    def __init__(self, name, experts, blocks, shared, scratch):
        self.name = name
        self.E = experts
        self.NB = blocks
        self.FC = shared // P
        self.TW = D + experts
        self.units = experts * blocks
        self.table = scratch["table"]


def quad_stats(k, dve, m, stream, it, par):
    nc, g = k.nc, m * TILES + 4 * it
    if positive(g - 4):
        dve.wait_ge(k.f_xn, g - 4)
    for q in range(4):
        nc.vector.bn_stats(k.q_stats[:, par, q, :], stream[:, bass.ds((4 * it + q) * P, P)]).then_inc(k.f_stats, 1)
    dve.wait_ge(k.f_stats, g + 4)
    nc.vector.memset(k.pause[:, 0:1], 0.0)
    for q in range(4):
        nc.vector.bn_aggr(k.q_meanvar[:, par, q, :], k.q_stats[:, par, q, :]).then_inc(k.f_mv, 1)
    dve.wait_ge(k.f_mv, g + 4)
    nc.vector.tensor_scalar(k.q_vareps[:, par, :], k.q_meanvar[:, par, :, 1:2].rearrange("p q o -> p (q o)"), EPS, None,
                            ALU.add).then_inc(k.f_var, 4)


def quad_pool(k, pool, m, it, par):
    nc, g = k.nc, m * TILES + 4 * it
    pool.wait_ge(k.f_var, g + 4)
    if positive(g - 4):
        pool.wait_ge(k.f_xn, g - 4)
    nc.gpsimd.tensor_tensor(k.q_rstd[:, par, :], k.q_vareps[:, par, :], k.half_power[:, 0:1].broadcast_to([P, 4]),
                            ALU.pow).then_inc(k.f_rstd, 4)


def quad_norm(k, dve, m, stream, it, par, out):
    nc, g = k.nc, m * TILES + 4 * it
    dve.wait_ge(k.f_rstd, g + 4)
    for q in range(4):
        nc.vector.tensor_scalar(out[:, q * P:(q + 1) * P], stream[:, bass.ds((4 * it + q) * P, P)],
                                k.q_meanvar[:, par, q, 0:1], k.q_rstd[:, par, q:q + 1], ALU.subtract,
                                ALU.mult).then_inc(k.f_xn, 1)


def shared_pass(k, ps, m, r):
    nc = k.nc
    E, FC = r.E, r.FC
    choose = r.name == "L0_ffn"
    CL = 59 if choose else 0
    front = k.tf(m) * TILES
    w_quad = k.r_w if choose else k.r_score
    hidden = k.probT if FC > 1 else k.kblock.rearrange("p b c n -> p b (c n)")

    with nc.Block() as block:
        @block.gpsimd
        def _(pool):
            def step(it, par, ends):
                if active(it, 0, ends):
                    quad_pool(k, pool, m, it, par)
            tile_pipeline(pool, step, 3, count=QUADS)

        @block.sync
        def _(sp):
            def step(it, par, ends):
                if active(it, 1, ends):
                    t, b = it - 1, 1 - par
                    rows = r.table[bass.ds(4 * t * P, 4 * P), :].rearrange("(q p) c -> p q c", p=P)
                    sp.wait_ge(k.f_xn, m * TILES + 4 * t + 4)
                    sp.dma_start(rows[:, :, 0:D], k.q_xn[:, b, :].rearrange("p (q c) -> p q c", q=4)
                                 ).then_inc(k.x_out_ready[b], 16)
                    if choose:
                        sp.wait_ge(k.r_chain, CL * (t + 1))
                    else:
                        sp.wait_ge(k.score_ready, t + 1)
                    sp.dma_start(rows[:, :, D:D + E], w_quad[:, b, 0:4 * E].rearrange("p (q e) -> p q e", q=4)
                                 ).then_inc(k.w_out_ready[b], 16)
            tile_pipeline(sp, step, 3, count=QUADS)
            for b in range(2):
                sp.wait_ge(k.x_out_ready[b], 8 * QUADS)
                sp.wait_ge(k.w_out_ready[b], 8 * QUADS)

        @block.vector
        def _(dve):
            if choose:
                nc.vector.memset(k.r_carry[:, :], 0.0).then_inc(k.r_cum, 1)
                dve.wait_ge(k.r_cum, 1)

            def route(t, b):
                count = Count(t, CL)
                score, left, w, sel = k.r_score[:, b, :], k.r_left, k.r_w[:, b, :], k.r_sel[:, b, :]
                sfc = k.r_sfc

                def by_tile(ap):
                    return ap.rearrange("p (q e) -> p q e", q=4)
                dve.wait_ge(k.score_ready, t + 1)
                nc.vector.tensor_tensor(by_tile(sfc[:, :]), by_tile(score),
                                        k.e_bias[:, :].rearrange("p (o e) -> p o e", o=1).broadcast_to([P, 4, E]),
                                        ALU.add).then_inc(k.r_chain, 1)
                dve.wait_ge(k.r_chain, count.next())
                nc.vector.memset(k.pause[:, 0:1], 0.0)
                for g in range(32):
                    nc.vector.max(k.r_gmax[:, g, :], sfc[:, 8 * g:8 * g + 8]).then_inc(k.r_chain, 1)
                    after = count.next()
                dve.wait_ge(k.r_chain, after)
                nc.vector.tensor_tensor(k.r_gs[:, :].rearrange("p (g o) -> p g o", o=1), k.r_gmax[:, :, 0:1],
                                        k.r_gmax[:, :, 1:2], ALU.add).then_inc(k.r_chain, 1)
                dve.wait_ge(k.r_chain, count.next())
                nc.vector.memset(k.pause[:, 0:1], 0.0)
                for q in range(4):
                    nc.vector.max(k.r_gtop[:, 8 * q:8 * q + 8], k.r_gs[:, 8 * q:8 * q + 8]).then_inc(k.r_chain, 1)
                    after = count.next()
                dve.wait_ge(k.r_chain, after)
                nc.vector.memset(k.pause[:, 0:1], 0.0)
                for q in range(4):
                    nc.vector.max_index(k.r_gplace[:, q, :], k.r_gtop[:, 8 * q:8 * q + 8],
                                        k.r_gs[:, 8 * q:8 * q + 8]).then_inc(k.r_chain, 1)
                    after = count.next()
                dve.wait_ge(k.r_chain, after)
                nc.vector.tensor_tensor(
                    k.r_geq[:, :, :, :],
                    k.r_gplace[:, :, 0:4].rearrange("p q (o j) -> p q o j", o=1).broadcast_to([P, 4, 8, 4]),
                    k.consts[:, C_EIGHT:C_EIGHT + 8].rearrange("p (u e o) -> p u e o", u=1, o=1)
                     .broadcast_to([P, 4, 8, 4]), ALU.is_equal).then_inc(k.r_chain, 1)
                dve.wait_ge(k.r_chain, count.next())
                nc.vector.tensor_reduce(k.r_gmask[:, :].rearrange("p (q e) -> p q e", q=4), k.r_geq[:, :, :, :], AX.X,
                                        ALU.add).then_inc(k.r_chain, 1)
                dve.wait_ge(k.r_chain, count.next())
                grouped = sfc[:, :].rearrange("p (g e) -> p g e", e=8)
                nc.vector.tensor_tensor(grouped, grouped,
                                        k.r_gmask[:, :].rearrange("p (g o) -> p g o", o=1).broadcast_to([P, 32, 8]),
                                        ALU.mult).then_inc(k.r_chain, 1)
                dve.wait_ge(k.r_chain, count.next())
                nc.vector.memset(k.pause[:, 0:1], 0.0)
                for q in range(4):
                    nc.vector.max(k.r_top[:, 8 * q:8 * q + 8], sfc[:, E * q:E * (q + 1)]).then_inc(k.r_chain, 1)
                    after = count.next()
                dve.wait_ge(k.r_chain, after)
                nc.vector.memset(k.pause[:, 0:1], 0.0)
                for q in range(4):
                    nc.vector.match_replace(left[:, E * q:E * (q + 1)], k.r_top[:, 8 * q:8 * q + 8],
                                            sfc[:, E * q:E * (q + 1)], LOWEST).then_inc(k.r_chain, 1)
                    after = count.next()
                dve.wait_ge(k.r_chain, after)
                if positive(t - 1):
                    dve.wait_ge(k.r_cum_psum, t - 1)
                nc.vector.tensor_tensor(sel, left[:, :], sfc[:, :], ALU.not_equal).then_inc(k.r_chain, 1)
                dve.wait_ge(k.r_chain, count.next())
                if positive(8 * (t - b)):
                    dve.wait_ge(k.w_out_ready[b], 8 * (t - b))
                nc.vector.tensor_tensor(w, score, sel, ALU.mult).then_inc(k.r_chain, 1)
                dve.wait_ge(k.r_chain, count.next())
                nc.vector.tensor_reduce(k.r_sum[:, 0:4], by_tile(w), AX.X, ALU.add).then_inc(k.r_chain, 1)
                dve.wait_ge(k.r_chain, count.next())
                nc.vector.tensor_scalar(k.r_sum[:, 0:4], k.r_sum[:, 0:4], 1e-20, None, ALU.add).then_inc(k.r_chain, 1)
                dve.wait_ge(k.r_chain, count.next())
                nc.vector.reciprocal(k.r_sum[:, 4:8], k.r_sum[:, 0:4]).then_inc(k.r_chain, 1)
                dve.wait_ge(k.r_chain, count.next())
                nc.vector.scalar_tensor_tensor(by_tile(w), by_tile(w), ROUTE_SCALE,
                                               k.r_sum[:, 4:8].rearrange("p (q o) -> p q o", o=1).broadcast_to([P, 4, E]),
                                               ALU.mult, ALU.mult).then_inc(k.r_chain, 1)
                dve.wait_ge(k.r_chain, count.next())
                assert count.passed == CL

            def norm(it, par):
                if positive(front + 4 * it - 4):
                    dve.wait_ge(k.f_xT_psum, front + 4 * it - 4)
                if positive(8 * (it - par)):
                    dve.wait_ge(k.x_out_ready[par], 8 * (it - par))
                quad_norm(k, dve, m, k.x, it, par, k.q_xn[:, par, :])

            def step(it, par, ends):
                if active(it, 0, ends):
                    quad_stats(k, dve, m, k.x, it, par)
                if active(it, 0, ends) and not choose:
                    norm(it, par)
                if active(it, 1, ends):
                    t, b = it - 1, 1 - par
                    h = hidden[:, b, 0:FC * QW].rearrange("p (c n) -> p c n", c=FC)
                    dve.wait_ge(k.sig_ready, t + 1)
                    nc.vector.tensor_tensor(h, ps[:, 0:FC, :], h, ALU.mult).then_inc(k.gated_ready, 1)
                    dve.wait_ge(k.gated_ready, t + 1)
                    dve.wait_ge(k.up_ready, t + 1)
                    nc.vector.tensor_tensor(h, h, ps[:, 2:2 + FC, :], ALU.mult).then_inc(k.hidden_ready, 1)
                if active(it, 0, ends) and choose:
                    norm(it, par)
                if active(it, 1, ends) and choose:
                    route(t, b)
                if active(it, 2, ends):
                    t = it - 2
                    if choose:
                        dve.wait_ge(k.r_cum_psum, t + 1)
                        nc.vector.tensor_scalar(k.held[0:E, bass.ds(t * QW, QW)], ps[0:E, 5, :], k.r_carry[0:E, 0:1], None,
                                                ALU.add).then_inc(k.r_cum, 1)
                        dve.wait_ge(k.r_cum, 2 * t + 2)
                        nc.vector.tensor_scalar(k.r_carry[0:E, 0:1], ps[0:E, 5, QW - 1:QW], k.r_carry[0:E, 0:1], None,
                                                ALU.add).then_inc(k.r_cum, 1)
                        dve.wait_ge(k.r_cum, 2 * t + 3)
                    dve.wait_ge(k.down_ready, t + 1)
                    xt = k.x[:, bass.ds(t * QW, QW)]
                    nc.vector.tensor_tensor(xt, xt, ps[:, 6, :], ALU.add).then_inc(k.res_ready, 1)
            tile_pipeline(dve, step, 3, count=QUADS)

        @block.tensor
        def _(pe):
            def step(it, par, ends):
                if active(it, 1, ends):
                    t, b = it - 1, 1 - par
                    xT = k.q_xnT[:, b, :]
                    pe.wait_ge(k.f_xT, front + 4 * t + 4)
                    if positive(t):
                        pe.wait_ge(k.gated_ready, t)
                    for c in range(FC):
                        mm = nc.tensor.matmul(ps[:, c, :], k.sh_gate[r.name][:, c * P:(c + 1) * P], xT, start=True, stop=True)
                    mm.then_inc(k.gate_ready, 1)
                    if positive(t):
                        pe.wait_ge(k.score_ready, t)
                    for q in range(4):
                        mm = nc.tensor.matmul(ps[:, 4, E * q:E * (q + 1)], xT[:, q * P:(q + 1) * P], k.router[r.name][:, :],
                                              start=True, stop=True)
                    mm.then_inc(k.logit_ready, 1)
                    if not choose:
                        if positive(t):
                            pe.wait_ge(k.r_scoreT, t)
                        nc.tensor.matmul(ps[0:E, 5, :], k.router[r.name][:, :], xT, start=True,
                                         stop=True).then_inc(k.r_logitT, 1)
                    if positive(t):
                        pe.wait_ge(k.hidden_ready, t)
                    for c in range(FC):
                        mm = nc.tensor.matmul(ps[:, 2 + c, :], k.sh_up[r.name][:, c * P:(c + 1) * P], xT, start=True, stop=True)
                    mm.then_inc(k.up_ready, 1)
                if active(it, 0, ends):
                    pe.wait_ge(k.f_xn, m * TILES + 4 * it + 4)
                    if positive(front + 4 * it):
                        pe.wait_ge(k.f_xT, front + 4 * it)
                    for q in range(4):
                        mm = nc.tensor.transpose(ps[:, 7, q * P:(q + 1) * P], k.q_xn[:, par, q * P:(q + 1) * P], k.ident)
                    mm.then_inc(k.f_xT_psum, 4)
                if active(it, 2, ends):
                    t, b = it - 2, par
                    pe.wait_ge(k.hidden_ready, t + 1)
                    if positive(t):
                        pe.wait_ge(k.res_ready, t)
                    for q in range(4):
                        for c in range(FC):
                            mm = nc.tensor.matmul(ps[:, 6, q * P:(q + 1) * P],
                                                  hidden[:, b, c * QW + q * P:c * QW + (q + 1) * P],
                                                  k.sh_down[r.name][:, c, :], start=c == 0, stop=c == FC - 1)
                    mm.then_inc(k.down_ready, 1)
                    if choose:
                        pe.wait_ge(k.r_chain, CL * (t + 1))
                        pe.wait_ge(k.r_cum, 2 * t + 1)
                        for q in range(4):
                            mm = nc.tensor.matmul(ps[0:E, 5, q * P:QW], k.r_sel[:, b, E * q:E * (q + 1)],
                                                  k.consts[:, C_UPPER:C_UPPER + QW - q * P], start=q == 0, stop=q == 3,
                                                  skip_group_check=True)
                        mm.then_inc(k.r_cum_psum, 1)
            tile_pipeline(pe, step, 3, count=QUADS)

        @block.scalar
        def _(act):
            def step(it, par, ends):
                if active(it, 1, ends):
                    t, b = it - 1, 1 - par
                    act.wait_ge(k.gate_ready, t + 1)
                    if positive(t - 1):
                        act.wait_ge(k.down_ready, t - 1)
                    nc.scalar.activation(hidden[:, b, 0:FC * QW].rearrange("p (c n) -> p c n", c=FC), ps[:, 0:FC, :],
                                         ACT.Sigmoid).then_inc(k.sig_ready, 1)
                    act.wait_ge(k.logit_ready, t + 1)
                    if choose:
                        if positive(CL * (t - 1)):
                            act.wait_ge(k.r_chain, CL * (t - 1))
                    else:
                        if positive(8 * (t - b)):
                            act.wait_ge(k.w_out_ready[b], 8 * (t - b))
                    nc.scalar.activation(k.r_score[:, b, 0:4 * E], ps[:, 4, 0:4 * E], ACT.Sigmoid).then_inc(k.score_ready, 1)
                    if not choose:
                        act.wait_ge(k.r_logitT, t + 1)
                        nc.scalar.activation(k.held[0:E, bass.ds(t * QW, QW)], ps[0:E, 5, :],
                                             ACT.Sigmoid).then_inc(k.r_scoreT, 1)
                if active(it, 0, ends):
                    act.wait_ge(k.f_xT_psum, front + 4 * it + 4)
                    if positive(it - 1):
                        act.wait_ge(k.up_ready, it - 1)
                    nc.scalar.activation(k.q_xnT[:, par, :], ps[:, 7, :], ACT.Copy).then_inc(k.f_xT, 4)
            tile_pipeline(act, step, 3, count=QUADS)


def choose_tokens(k, ps, r):
    nc = k.nc
    W = T // 8
    cap = float(r.NB * P)
    score, work, work2, cum = k.prob[:, 0, :], k.prob[:, 1, :], k.probT[:, 0, :], k.probT[:, 1, :]
    chunk, earlier = k.consts[:, C_CHUNK:C_CHUNK + P], k.consts[:, C_EARLIER:C_EARLIER + P]
    with nc.Block() as block:
        @block.sync
        def _(sp):
            sp.dma_start(k.score_dram, k.held[0:r.E, :]).then_inc(k.c_io, 16)
            sp.wait_ge(k.c_io, 16)
            sp.dma_start(score, k.score_dram.rearrange("e (c n) -> (e c) n", c=8)).then_inc(k.c_io, 16)
            sp.wait_ge(k.c_io, 32)

        @block.gpsimd
        def _(pool):
            nc.gpsimd.memset(k.c_thr[:, 0, :], 0.0).then_inc(k.c_zero, 1)

        @block.vector
        def _(dve):
            dve.wait_ge(k.c_zero, 1)
            dve.wait_ge(k.c_io, 32)
            thr, cand = k.c_thr[:, 0, :], k.c_thr[:, 1, :]
            with dve.Fori(0, 30) as bit:
                count = Count(bit, 4)
                nc.vector.tensor_tensor(cand.bitcast(I32), thr.bitcast(I32), k.bits[:, bass.ds(bit, 1)],
                                        ALU.bitwise_or).then_inc(k.c_chain, 1)
                dve.wait_ge(k.c_chain, count.next())
                nc.vector.tensor_scalar(work, score, cand, None, ALU.is_ge, ALU.add, accum_out=k.c_count[:, 0:1]).then_inc(k.c_chain, 1)
                dve.wait_ge(k.c_chain, count.next())
                dve.wait_ge(k.c_psum, bit + 1)
                nc.vector.tensor_scalar(cand, ps[:, 0, 0:1], cap, cand, ALU.is_ge, ALU.mult).then_inc(k.c_chain, 1)
                dve.wait_ge(k.c_chain, count.next())
                nc.vector.tensor_tensor(thr, thr, cand, ALU.max).then_inc(k.c_chain, 1)
                dve.wait_ge(k.c_chain, count.next())
            count = Count(0, 99)
            nc.vector.tensor_scalar(work, score, thr, None, ALU.is_gt, ALU.add, accum_out=k.c_count[:, 1:2]).then_inc(k.c_chain2, 1)
            dve.wait_ge(k.c_chain2, count.next())
            nc.vector.tensor_scalar(work2, score, thr, None, ALU.is_equal, ALU.add, accum_out=k.c_count[:, 2:3]).then_inc(k.c_chain2, 1)
            dve.wait_ge(k.c_chain2, count.next())
            nc.vector.tensor_tensor_scan(cum, work2, work2, 0.0, ALU.add, ALU.max).then_inc(k.c_chain2, 1)
            dve.wait_ge(k.c_chain2, count.next())
            dve.wait_ge(k.c_psum, 32)
            nc.vector.tensor_scalar(k.c_count[:, 3:4], ps[:, 0, 1:2], -cap, None, ALU.add).then_inc(k.c_chain2, 1)
            dve.wait_ge(k.c_chain2, count.next())
            nc.vector.tensor_tensor(k.c_count[:, 4:5], k.c_count[:, 3:4], ps[:, 0, 2:3], ALU.add).then_inc(k.c_chain2, 1)
            dve.wait_ge(k.c_chain2, count.next())
            nc.vector.tensor_scalar(cum, cum, k.c_count[:, 4:5], 0.0, ALU.add, ALU.is_le).then_inc(k.c_chain2, 1)
            dve.wait_ge(k.c_chain2, count.next())
            nc.vector.tensor_tensor(work2, work2, cum, ALU.mult).then_inc(k.c_chain2, 1)
            dve.wait_ge(k.c_chain2, count.next())
            nc.vector.tensor_tensor(work, work, work2, ALU.add).then_inc(k.c_chain2, 1)
            dve.wait_ge(k.c_chain2, count.next())
            nc.vector.tensor_tensor_scan(cum, work, work, 0.0, ALU.add, ALU.max).then_inc(k.c_chain2, 1)
            dve.wait_ge(k.c_chain2, count.next())
            nc.vector.tensor_copy(k.c_count[:, 5:6], cum[:, W - 1:W]).then_inc(k.c_total, 1)
            dve.wait_ge(k.c_psum, 33)
            nc.vector.tensor_scalar(cum, cum, ps[:, 0, 3:4], None, ALU.add).then_inc(k.c_chain2, 1)
            dve.wait_ge(k.c_chain2, count.next())

        @block.tensor
        def _(pe):
            with pe.Fori(0, 30) as bit:
                pe.wait_ge(k.c_chain, 4 * bit + 2)
                nc.tensor.matmul(ps[:, 0, 0:1], chunk, k.c_count[:, 0:1], start=True, stop=True).then_inc(k.c_psum, 1)
            pe.wait_ge(k.c_chain, 120)
            pe.wait_ge(k.c_chain2, 2)
            nc.tensor.matmul(ps[:, 0, 1:2], chunk, k.c_count[:, 1:2], start=True, stop=True).then_inc(k.c_psum, 1)
            nc.tensor.matmul(ps[:, 0, 2:3], earlier, k.c_count[:, 2:3], start=True, stop=True).then_inc(k.c_psum, 1)
            pe.wait_ge(k.c_total, 1)
            pe.wait_ge(k.c_chain2, 5)
            nc.tensor.matmul(ps[:, 0, 3:4], earlier, k.c_count[:, 5:6], start=True, stop=True).then_inc(k.c_psum, 1)


def find_slots(k, ps, r):
    nc = k.nc
    E, NB = r.E, r.NB
    cend = k.x[:, 0:E * TILES]
    le = k.x[:, TILES * D // 2:TILES * D // 2 + E * TILES]
    parts = E if r.name == "L0_ffn" else P
    per = E * TILES // parts
    counts = (k.held[0:E, :] if r.name == "L0_ffn" else k.probT[:, 1, :])
    LOADS = 8

    with nc.Block() as block:
        @block.sync
        def _(sp):
            xs = k.x_dram[0:T, :].rearrange("(n p) c -> p n c", p=P)
            for c in range(LOADS):
                w = TILES // LOADS
                sp.dma_start(xs[:, c * w:(c + 1) * w, :],
                             k.x[:, c * w * D:(c + 1) * w * D].rearrange("p (n c) -> p n c", c=D)
                             ).then_inc(k.spill_ready, 16)
            sp.dma_start(k.cum_dram[0:E * TILES, :].rearrange("(p n) t -> p (n t)", p=parts), counts).then_inc(k.spill_ready, 16)
            sp.wait_ge(k.zero_ready, 1)
            sp.dma_start(k.x_dram[T:T + P, :], k.zeros[:, 0:D]).then_inc(k.spill_ready, 16)
            sp.dma_start(r.table[T:T + P, :], k.zeros[:, 0:r.TW]).then_inc(k.spill_ready, 16)
            sp.wait_ge(k.ends_ready, 1)
            sp.dma_start(k.cend_dram[0:E * TILES].rearrange("(p n) -> p n", p=parts), k.tile_ends[0:parts, 0:per]).then_inc(k.spill_ready, 16)
            sp.wait_ge(k.spill_ready, 16 * (LOADS + 4))
            sp.dma_start(cend, k.cend_dram[0:E * TILES].partition_broadcast(P)).then_inc(k.spill_ready, 16)
            sp.wait_ge(k.spill_ready, 16 * (LOADS + 5))

        @block.gpsimd
        def _(pool):
            nc.gpsimd.memset(k.zeros[:, :], 0.0).then_inc(k.zero_ready, 1)

        @block.vector
        def _(dve):
            nc.vector.tensor_copy(k.tile_ends[0:parts, 0:per].rearrange("p (n o) -> p n o", o=1),
                                  counts.rearrange("p (n t) -> p n t", t=P)[:, :, P - 1:P]).then_inc(k.ends_ready, 1)
            dve.wait_ge(k.spill_ready, 16 * (LOADS + 5))
            count = Count(0, 99)
            tiles = k.slot_tile[:, 0:r.units].rearrange("p (e b) -> p e b", b=NB)
            rows = k.slot_row[:, 0:r.units].rearrange("p (e b) -> p e b", b=NB)
            for b in range(NB):
                nc.vector.tensor_scalar(le, cend, k.consts[:, C_SLOT + b:C_SLOT + b + 1], None, ALU.is_le).then_inc(k.slotchain_ready, 1)
                dve.wait_ge(k.slotchain_ready, count.next())
                nc.vector.tensor_reduce(tiles[:, :, b:b + 1].rearrange("p e o -> p (e o)"),
                                        le.rearrange("p (e n) -> p e n", n=TILES), AX.X, ALU.add).then_inc(k.slotchain_ready, 1)
                dve.wait_ge(k.slotchain_ready, count.next())
            base = k.consts[:, C_TOKEN0:C_TOKEN0 + E].rearrange("p (e o) -> p e o", o=1).broadcast_to([P, E, NB])
            nc.vector.scalar_tensor_tensor(rows, tiles, float(TILES - 1), base, ALU.min, ALU.add).then_inc(k.slotchain_ready, 1)
            dve.wait_ge(k.slotchain_ready, count.next())

    G = 4
    steps = r.units // G
    with nc.Block() as block:
        @block.gpsimd
        def _(pool):
            def step(it, par, ends):
                if active(it, 0, ends):
                    pool.wait_ge(k.index_ready, it + 1)
                    if positive(G * (it - 1)):
                        pool.wait_ge(k.within_ready, G * (it - 1))
                    pool_pause(k, pool, k.pause_find, 4, it)
                    for q in range(G):
                        nc.gpsimd.indirect_dma_start(
                            out=k.rows[:, par, q, :], out_offset=None, in_=k.cum_dram[0:E * TILES, :],
                            in_offset=bass.IndirectOffsetOnAxis(ap=k.slot_index[:, par, q:q + 1], axis=0),
                            bounds_check=E * TILES - 1, oob_is_err=True).then_inc(k.rows_ready[par], 16)
            tile_pipeline(pool, step, 2, count=steps)

        @block.vector
        def _(dve):
            def step(it, par, ends):
                if active(it, 0, ends):
                    if positive((8 * G) * (it - par)):
                        dve.wait_ge(k.rows_ready[par], (8 * G) * (it - par))
                    nc.vector.tensor_scalar(k.slot_index[:, par, :], k.slot_row[:, bass.ds(G * it, G)], 0.0, None, ALU.add).then_inc(k.index_ready, 1)
                if active(it, 1, ends):
                    t, buf = it - 1, 1 - par
                    dve.wait_ge(k.rows_ready[buf], (8 * G) * (t - buf + 2))
                    for q in range(G):
                        b = (G * buf + q) % NB
                        nc.vector.tensor_scalar(k.row_le[:, q, :], k.rows[:, buf, q, :],
                                                k.consts[:, C_SLOT + b:C_SLOT + b + 1], None, ALU.is_le, ALU.add,
                                                accum_out=k.slot_within[:, bass.ds(G * t + q, 1)]).then_inc(k.within_ready, 1)
                        dve.wait_ge(k.within_ready, G * t + q + 1)
            tile_pipeline(dve, step, 2, count=steps)
            count = Count(0, 99)
            tiles, within = k.slot_tile[:, 0:r.units], k.slot_within[:, 0:r.units]
            nc.vector.scalar_tensor_tensor(within, tiles, float(P), within, ALU.mult, ALU.add).then_inc(k.tokenchain_ready, 1)
            dve.wait_ge(k.tokenchain_ready, count.next())
            nc.vector.tensor_scalar(k.slot_token[:, 0:r.units], within, k.consts[:, C_SLOT + 8:C_SLOT + 9], None, ALU.min).then_inc(k.tokenchain_ready, 1)
            dve.wait_ge(k.tokenchain_ready, count.next())


def small_experts(k, ps, r):
    nc = k.nc
    E, F = r.E, 64
    xe = k.x[:, 0:4 * r.TW].rearrange("p (b n) -> p b n", b=4)
    at = 4 * r.TW
    w13 = k.x[:, at:at + 4 * 2 * F].rearrange("p (b n) -> p b n", b=4)
    at += 8 * F
    w2 = k.x[0:F, at:at + 4 * D].rearrange("p (b n) -> p b n", b=4)
    at += 4 * D
    xeT = k.x[:, at:at + 2 * P].rearrange("p (b n) -> p b n", b=2)
    at += 2 * P
    sig = k.x[0:F, at:at + 2 * P].rearrange("p (b n) -> p b n", b=2)
    at += 2 * P
    eh = k.x[0:F, at:at + 2 * P].rearrange("p (b n) -> p b n", b=2)
    at += 2 * P
    ys = k.x[:, at:at + 2 * D].rearrange("p (b n) -> p b n", b=2)

    with nc.Block() as block:
        @block.sync
        def _(sp):
            def step(it, u, ends):
                par = u % 2
                if active(it, 0, ends):
                    if positive(it - 3):
                        sp.wait_ge(k.e_y, it - 3)
                    sp.dma_start(w13[:, u, :], k.d["e_w13"][bass.ds(it * D, D), :]).then_inc(k.e_w_ready[u], 16)
                    sp.dma_start(w2[:, u, :], k.d["e_w2"][bass.ds(it * F, F), :]).then_inc(k.e_w_ready[u], 16)
            tile_pipeline(sp, step, 5, count=E, unroll=4)

        @block.gpsimd
        def _(pool):
            def step(it, u, ends):
                par = u % 2
                if active(it, 0, ends):
                    pool.wait_ge(k.e_index, it + 1)
                    if positive(it - 3):
                        pool.wait_ge(k.e_xT_psum, it - 3)
                        pool.wait_ge(k.e_col, it - 3)
                    pool_pause(k, pool, k.pause_gather, 5, it)
                    nc.gpsimd.indirect_dma_start(
                        out=xe[:, u, :], out_offset=None, in_=r.table,
                        in_offset=bass.IndirectOffsetOnAxis(ap=k.e_gidx[:, u, 0:1], axis=0),
                        bounds_check=T + P - 1, oob_is_err=True).then_inc(k.e_x_ready[u], 16)
                if active(it, 4, ends):
                    t, b = it - 4, par
                    pool.wait_ge(k.e_scaled, t + 1)
                    if positive(16 * t):
                        pool.wait_ge(k.e_added, 16 * t)
                    pool_pause(k, pool, k.pause_add, 6, t)
                    nc.gpsimd.indirect_dma_start(
                        out=k.x_dram, out_offset=bass.IndirectOffsetOnAxis(ap=k.e_sidx[:, b, 0:1], axis=0),
                        in_=ys[:, b, :], in_offset=None, bounds_check=T + P - 1, oob_is_err=True,
                        compute_op=ALU.add).then_inc(k.e_added, 16)
            tile_pipeline(pool, step, 5, count=E, unroll=4)
            pool.wait_ge(k.e_added, 16 * E)

        @block.vector
        def _(dve):
            def step(it, u, ends):
                par = u % 2
                if active(it, 0, ends):
                    if positive(4 * (it - u)):
                        dve.wait_ge(k.e_x_ready[u], 4 * (it - u))
                    nc.vector.tensor_scalar(k.e_gidx[:, u, 0:1], k.slot_token[:, bass.ds(it, 1)], 0.0, None, ALU.add).then_inc(k.e_index, 1)
                if active(it, 3, ends):
                    t, b, v = it - 3, 1 - par, (u + 1) % 4
                    dve.wait_ge(k.e_x_ready[v], 4 * (t - v + 4))
                    if positive(t - 1):
                        dve.wait_ge(k.e_scaled, t - 1)
                    nc.vector.tensor_scalar(k.e_wcol[:, b, 0:1], xe[:, v, bass.ds(D + t, 1)], 0.0, None, ALU.add).then_inc(k.e_col, 1)
                    dve.wait_ge(k.e_sig, t + 1)
                    if positive(t - 1):
                        dve.wait_ge(k.e_y, t - 1)
                    nc.vector.tensor_tensor(eh[:, b, :], ps[0:F, 0, 0:P], sig[:, b, :], ALU.mult).then_inc(k.e_gated, 1)
                    dve.wait_ge(k.e_gated, t + 1)
                    dve.wait_ge(k.e_h3, t + 1)
                    nc.vector.tensor_tensor(eh[:, b, :], eh[:, b, :], ps[0:F, 1, 0:P], ALU.mult).then_inc(k.e_hid, 1)
                if active(it, 4, ends):
                    t, b = it - 4, par
                    dve.wait_ge(k.e_y, t + 1)
                    dve.wait_ge(k.e_col, t + 1)
                    if positive(16 * (t - 1)):
                        dve.wait_ge(k.e_added, 16 * (t - 1))
                    nc.vector.tensor_scalar(k.e_sidx[:, b, 0:1], k.slot_token[:, bass.ds(t, 1)], 0.0, None, ALU.add).then_inc(k.e_sindex, 1)
                    dve.wait_ge(k.e_sindex, t + 1)
                    nc.vector.tensor_scalar(ys[:, b, :], ps[:, 2, 0:D], k.e_wcol[:, b, 0:1], None,
                                            ALU.mult).then_inc(k.e_scaled, 1)
            tile_pipeline(dve, step, 5, count=E, unroll=4)

        @block.tensor
        def _(pe):
            def step(it, u, ends):
                par = u % 2
                if active(it, 3, ends):
                    t, b, v = it - 3, 1 - par, (u + 1) % 4
                    pe.wait_ge(k.e_x_ready[v], 4 * (t - v + 4))
                    if positive(t):
                        pe.wait_ge(k.e_xT, t)
                    nc.tensor.transpose(ps[:, 4, 0:P], xe[:, v, 0:D], k.ident).then_inc(k.e_xT_psum, 1)
                    pe.wait_ge(k.e_xT, t + 1)
                    pe.wait_ge(k.e_w_ready[v], 8 * (t - v + 4))
                    if positive(t):
                        pe.wait_ge(k.e_gated, t)
                    nc.tensor.matmul(ps[0:F, 0, 0:P], w13[:, v, 0:F], xeT[:, b, :], start=True, stop=True).then_inc(k.e_h1, 1)
                    if positive(t):
                        pe.wait_ge(k.e_hid, t)
                    nc.tensor.matmul(ps[0:F, 1, 0:P], w13[:, v, F:2 * F], xeT[:, b, :], start=True, stop=True).then_inc(k.e_h3, 1)
                if active(it, 4, ends):
                    t, b = it - 4, par
                    pe.wait_ge(k.e_hid, t + 1)
                    if positive(t):
                        pe.wait_ge(k.e_scaled, t)
                    nc.tensor.matmul(ps[:, 2, 0:D], eh[:, b, :], w2[:, u, :], start=True, stop=True).then_inc(k.e_y, 1)
            tile_pipeline(pe, step, 5, count=E, unroll=4)

        @block.scalar
        def _(act):
            def step(it, u, ends):
                par = u % 2
                if active(it, 3, ends):
                    t, b, v = it - 3, 1 - par, (u + 1) % 4
                    act.wait_ge(k.e_xT_psum, t + 1)
                    if positive(t - 1):
                        act.wait_ge(k.e_h3, t - 1)
                    nc.scalar.activation(xeT[:, b, :], ps[:, 4, 0:P], ACT.Copy).then_inc(k.e_xT, 1)
                    act.wait_ge(k.e_h1, t + 1)
                    if positive(t - 1):
                        act.wait_ge(k.e_gated, t - 1)
                    nc.scalar.activation(sig[:, b, :], ps[0:F, 0, 0:P], ACT.Sigmoid).then_inc(k.e_sig, 1)
            tile_pipeline(act, step, 5, count=E, unroll=4)


def large_experts(k, ps, r):
    nc = k.nc
    H = 512
    NC = 4
    WC = 3 * 512 + 2 * NC + D
    steps = r.E * r.NB * P // H
    w = k.held[:, 0:2 * WC].rearrange("p (b n) -> p b n", b=2)
    hid = k.held[:, 2 * WC:2 * WC + 2 * NC * H].rearrange("p (b c n) -> p b c n", b=2, c=NC)
    xg = k.x[:, 0:2 * 4 * r.TW].rearrange("p (b q n) -> p b q n", b=2, q=4)
    at = 2 * 4 * r.TW
    xgT = k.x[:, at:at + 2 * H].rearrange("p (b n) -> p b n", b=2)
    at += 2 * H
    gate = k.x[:, at:at + 2 * H].rearrange("p (b n) -> p b n", b=2)
    at += 2 * H
    ys = k.x[:, at:at + 2 * H].rearrange("p (b n) -> p b n", b=2)

    def expert(it, u):
        return it // 2 if isinstance(it, int) else (it - u % 2) // 2

    with nc.Block() as block:
        @block.sync
        def _(sp):
            def step(it, u, ends):
                if active(it, 0, ends) and u % 2 == 0:
                    if positive(it - 2):
                        sp.wait_ge(k.g_biased, it - 2)
                    sp.dma_start(w[:, u // 2, :], k.d["g_w"][bass.ds(it * (P // 2), P), :]).then_inc(k.g_w_ready[u // 2], 16)
            tile_pipeline(sp, step, 4, count=steps, unroll=4)

        @block.gpsimd
        def _(pool):
            def step(it, u, ends):
                if active(it, 0, ends):
                    pool.wait_ge(k.g_index, it + 1)
                    if positive(it - 1):
                        pool.wait_ge(k.g_xT_psum, it - 1)
                    if positive(it - 1):
                        pool.wait_ge(k.g_col, it - 1)
                    pool_pause(k, pool, k.pause_gather, 5, it)
                    for q in range(4):
                        nc.gpsimd.indirect_dma_start(
                            out=xg[:, u % 2, q, :], out_offset=None, in_=r.table,
                            in_offset=bass.IndirectOffsetOnAxis(ap=k.g_gidx[:, u % 2, q:q + 1], axis=0),
                            bounds_check=T - 1, oob_is_err=True).then_inc(k.g_x_ready[u % 2], 16)
                if active(it, 3, ends):
                    t, b = it - 3, (u + 1) % 2
                    pool.wait_ge(k.g_scaled, t + 1)
                    if u % 2 == 1:
                        if positive(32 * t):
                            pool.wait_ge(k.g_added[0], 32 * t)
                            pool.wait_ge(k.g_added[1], 32 * t)
                    pool_pause(k, pool, k.pause_add, 6, t)
                    for q in range(4):
                        nc.gpsimd.indirect_dma_start(
                            out=k.x_dram, out_offset=bass.IndirectOffsetOnAxis(ap=k.g_sidx[:, b, q:q + 1], axis=0),
                            in_=ys[:, b, q * D:(q + 1) * D], in_offset=None, bounds_check=T - 1, oob_is_err=True,
                            compute_op=ALU.add).then_inc(k.g_added[b], 16)
            tile_pipeline(pool, step, 4, count=steps, unroll=4)
            pool.wait_ge(k.g_added[0], 32 * steps)
            pool.wait_ge(k.g_added[1], 32 * steps)

        @block.vector
        def _(dve):
            def step(it, u, ends):
                par = u % 2
                if active(it, 2, ends):
                    t, b = it - 2, par
                    dve.wait_ge(k.g_x_ready[b], 32 * (t - b + 2))
                    if positive(t - 1):
                        dve.wait_ge(k.g_scaled, t - 1)
                    nc.vector.tensor_scalar(k.g_wcol[:, b, :].rearrange("p (q o) -> p q o", o=1),
                                            xg[:, b, :, bass.ds(D + expert(t, u + 2), 1)], 0.0, None, ALU.add).then_inc(k.g_col, 1)
                if active(it, 0, ends):
                    if positive(32 * (it - par)):
                        dve.wait_ge(k.g_x_ready[par], 32 * (it - par))
                    nc.vector.tensor_scalar(k.g_gidx[:, par, :], k.slot_token[:, bass.ds(4 * it, 4)], 0.0, None, ALU.add).then_inc(k.g_index, 1)
                if active(it, 2, ends):
                    if positive(t - 1):
                        dve.wait_ge(k.g_y, t - 1)
                    wb = (u + 2) % 4 // 2
                    for c in range(NC):
                        dve.wait_ge(k.g_silu, NC * t + c + 1)
                        dve.wait_ge(k.g_up, NC * t + c + 1)
                        nc.vector.scalar_tensor_tensor(hid[:, b, c, :], ps[:, 2 + c % 2, :],
                                                       w[:, wb, 1536 + NC + c:1536 + NC + c + 1], gate[:, c % 2, :],
                                                       ALU.add, ALU.mult).then_inc(k.g_hid, 1)
                if active(it, 3, ends):
                    t, b = it - 3, (u + 1) % 2
                    wb = (u + 1) % 4 // 2
                    dve.wait_ge(k.g_y, t + 1)
                    if positive(32 * (t - b)):
                        dve.wait_ge(k.g_added[b], 32 * (t - b))
                    nc.vector.tensor_scalar(k.g_sidx[:, b, :], k.slot_token[:, bass.ds(4 * t, 4)], 0.0, None, ALU.add).then_inc(k.g_sindex, 1)
                    bias = w[:, wb, 1536 + 2 * NC:WC].rearrange("p (o d) -> p o d", o=1).broadcast_to([P, 4, D])
                    y3 = ys[:, b, :].rearrange("p (q d) -> p q d", d=D)
                    nc.vector.tensor_tensor(y3, ps[:, 5, :].rearrange("p (q d) -> p q d", d=D), bias,
                                            ALU.add).then_inc(k.g_biased, 1)
                    dve.wait_ge(k.g_biased, t + 1)
                    dve.wait_ge(k.g_col, t + 1)
                    dve.wait_ge(k.g_sindex, t + 1)
                    nc.vector.tensor_tensor(
                        y3, y3, k.g_wcol[:, b, :].rearrange("p (q o) -> p q o", o=1).broadcast_to([P, 4, D]),
                        ALU.mult).then_inc(k.g_scaled, 1)
            tile_pipeline(dve, step, 4, count=steps, unroll=4)

        @block.tensor
        def _(pe):
            def step(it, u, ends):
                par = u % 2
                if active(it, 2, ends):
                    t, b = it - 2, par
                    wb = (u + 2) % 4 // 2
                    pe.wait_ge(k.g_x_ready[b], 32 * (t - b + 2))
                    if positive(t):
                        pe.wait_ge(k.g_xT, t)
                    for q in range(4):
                        mm = nc.tensor.transpose(ps[:, 4, q * P:(q + 1) * P], xg[:, b, q, 0:D], k.ident)
                    mm.then_inc(k.g_xT_psum, 1)
                    pe.wait_ge(k.g_xT, t + 1)
                    pe.wait_ge(k.g_w_ready[wb], 4 * (t - (u + 2) % 4 + 4))
                    for c in range(NC):
                        if positive(NC * t + c - 1):
                            pe.wait_ge(k.g_silu, NC * t + c - 1)
                        nc.tensor.matmul(ps[:, c % 2, :], w[:, wb, c * P:(c + 1) * P], xgT[:, b, :], start=True,
                                         stop=True).then_inc(k.g_gate, 1)
                        if positive(NC * t + c - 1):
                            pe.wait_ge(k.g_hid, NC * t + c - 1)
                        nc.tensor.matmul(ps[:, 2 + c % 2, :], w[:, wb, 512 + c * P:512 + (c + 1) * P], xgT[:, b, :],
                                         start=True, stop=True).then_inc(k.g_up, 1)
                if active(it, 3, ends):
                    t, b = it - 3, (u + 1) % 2
                    wb = (u + 1) % 4 // 2
                    pe.wait_ge(k.g_hid, NC * (t + 1))
                    if positive(t):
                        pe.wait_ge(k.g_biased, t)
                    for q in range(4):
                        for c in range(NC):
                            mm = nc.tensor.matmul(ps[:, 5, q * D:(q + 1) * D], hid[:, b, c, q * P:(q + 1) * P],
                                                  w[:, wb, 1024 + c * D:1024 + (c + 1) * D], start=c == 0, stop=c == NC - 1)
                    mm.then_inc(k.g_y, 1)
            tile_pipeline(pe, step, 4, count=steps, unroll=4)

        @block.scalar
        def _(act):
            def step(it, u, ends):
                par = u % 2
                if active(it, 2, ends):
                    t, b = it - 2, par
                    wb = (u + 2) % 4 // 2
                    act.wait_ge(k.g_xT_psum, t + 1)
                    if positive(NC * (t - 1)):
                        act.wait_ge(k.g_up, NC * (t - 1))
                    nc.scalar.activation(xgT[:, b, :], ps[:, 4, :], ACT.Copy).then_inc(k.g_xT, 1)
                    for c in range(NC):
                        act.wait_ge(k.g_gate, NC * t + c + 1)
                        if positive(NC * t + c - 1):
                            act.wait_ge(k.g_hid, NC * t + c - 1)
                        nc.scalar.activation(gate[:, c % 2, :], ps[:, c % 2, :], ACT.Silu,
                                             bias=w[:, wb, 1536 + c:1536 + c + 1]).then_inc(k.g_silu, 1)
            tile_pipeline(act, step, 4, count=steps, unroll=4)


def reload_x(k, r):
    LOADS = 8
    with k.nc.Block() as block:
        @block.sync
        def _(sp):
            xs = k.x_dram[0:T, :].rearrange("(n p) c -> p n c", p=P)
            for c in range(LOADS):
                w = TILES // LOADS
                sp.dma_start(k.x[:, c * w * D:(c + 1) * w * D].rearrange("p (n c) -> p n c", c=D),
                             xs[:, c * w:(c + 1) * w, :]).then_inc(k.reload_ready, 16)
            sp.wait_ge(k.reload_ready, 16 * LOADS)


def background_loads(k, sp, d, routed, stages):
    loads = [(k.attn_w[:, 1:, :, :], d["attn_w"][:, 1:, :, :]),
             (k.bv[:, 1:, :], d["bv"][1:, :].partition_broadcast(P)),
             (k.bo[:, 1:, :], d["bo"][1:, :].partition_broadcast(P)),
             (k.post_gain[:, :, :], d["post_gain"].partition_broadcast(P)),
             (k.norm_cols[:, :], d["norm_cols"]), (k.moe_gate[:, :], d["moe_gate"]), (k.moe_w1[:, :], d["moe_w1"]),
             (k.moe_w2[:, :, :], d["moe_w2"]), (k.bits[:, :], d["bits"]),
             (k.e_bias[:, :], d["e_bias"].partition_broadcast(P)),
             (k.mask_raw[:, :].rearrange("p (n s) -> p n s", s=S // 4), d["mask"].rearrange("(n p) s -> p n s", p=P))]
    for name in routed:
        loads += [(k.sh_gate[name][:, :], d[f"sh_gate_{name}"]), (k.sh_up[name][:, :], d[f"sh_up_{name}"]),
                  (k.sh_down[name][:, :, :], d[f"sh_down_{name}"]), (k.router[name][:, :], d[f"router_{name}"])]
    for dst, src in loads:
        sp.dma_start(dst, src).then_inc(k.loaded_late, 16)
    sp.wait_ge(k.loaded_late, 16 * len(loads))
    if "L1_attn" in stages:
        relative_rows(k, sp)


def build(nc, d, stages):
    k = Kernel()
    k.nc, k.d, k.phases = nc, d, 0
    with ExitStack() as ctx:
        def sb(name, shape, dt=F32):
            return ctx.enter_context(nc.sbuf_tensor(name, shape, dt))

        def sem(name):
            return ctx.enter_context(nc.semaphore(name))

        k.x = sb("x_res", [P, TILES * D])
        k.held = sb("held", [P, TILES * D])
        k.consts = sb("consts", [P, C_END])
        k.attn_w = sb("attn_w", [P, NA, 4, D])
        k.bqk = sb("bqk", [P, NA, 2])
        k.key_scale = sb("key_scale", [P, NA, GH])
        k.key_bias = sb("key_bias", [P, NA, GH])
        k.bv = sb("bv", [P, NA, D])
        k.bo = sb("bo", [P, NA, D])
        k.ctxT = sb("ctxT", [P, 2, P])
        k.stats = sb("stats", [P, 2, 6])
        k.meanvar = sb("meanvar", [P, 2, 2])
        k.vareps = sb("vareps", [P, 2, 2])
        k.rstd = sb("rstd", [P, 2, 2])
        k.half_power = sb("half_power", [P, 1])
        k.pause = sb("pause", [P, 8])
        k.xn = sb("xn", [P, 2, D])
        k.xnT = sb("xnT", [P, 2, P])
        k.srcT = sb("srcT", [P, 2, 2, 2, S])
        k.qT = sb("qT", [P, 2, P])
        k.kblock = sb("kblock", [P, 2, GH, P])
        k.vblock = sb("vblock", [P, 2, HEADS // 2, 2, VW])
        k.rowmax = sb("rowmax", [P, 2, HEADS])
        k.prob = sb("prob", [P, 2, HEADS * S])
        k.probT = sb("probT", [P, 2, HEADS // 2 * P])
        k.rowinv = sb("rowinv", [P, 2, HEADS])
        k.o = sb("o", [P, 2, D])
        k.oT = sb("oT", [P, 2, P])
        k.post = sb("post", [P, 2, D])
        k.z = sb("z", [P, 2, D])
        k.v_low = sb("v_low", [P, 2, D])
        k.v_high = sb("v_high", [P, 2, D])
        k.z_dram = nc.dram_tensor("z_dram", (T, D), F32, kind="Internal").ap()
        k.post_stats = sb("post_stats", [P, 2, 6])
        k.post_meanvar = sb("post_meanvar", [P, 2, 2])
        k.post_gain = sb("post_gain", [P, 4, D])
        k.norm_cols = sb("norm_cols", [P, 4])
        k.mask_raw = sb("mask_raw", [P, TILES * S // 4], U32)
        k.maskadd = sb("maskadd", [P, 2, S])
        k.relpos = sb("relpos", [P, HEADS * S])
        k.ones = sb("ones", [P, P])
        k.ident_bf = sb("ident_bf", [P, P], BF16)
        k.bit_raw = k.held[:, 0:3 * INNER].rearrange("p (w n) -> p w n", w=3)
        k.bit_w = sb("bit_w", [P, 3, INNER], BF16)
        k.bit_sum = sb("bit_sum", [P, 4])
        k.bit_mean = sb("bit_mean", [P, 4])
        k.bit_inv = sb("bit_inv", [P, 4])
        k.moe_gate = sb("moe_gate", [P, ME])
        k.moe_w1 = sb("moe_w1", [P, ME * MH])
        k.moe_w2 = sb("moe_w2", [P, 4, D])
        k.b_xmax = sb("b_xmax", [P, 2, 4])
        k.b_xinv = sb("b_xinv", [P, 4])
        k.b_scale = sb("b_scale", [P, 2, 4, 2])
        k.b_hmax = sb("b_hmax", [P, 2, 4])
        k.b_hinv = sb("b_hinv", [P, 4])
        k.b_hscale = sb("b_hscale", [P, 4])
        k.b_h = k.prob[:, :, :].rearrange("p b (q n) -> p (b q) n", q=2)
        k.b_xn = k.probT[:, :, 0:QW]
        k.b_xq = k.probT[:, :, QW:QW + QW // 2].bitcast(BF16)
        k.b_xqT = k.probT[:, :, QW + QW // 2:2 * QW].bitcast(BF16)
        k.b_hq = k.relpos[:, :].bitcast(BF16).rearrange("p (q n) -> p q n", q=4)
        k.b_hqT = k.kblock[:, :, :, :].rearrange("p b c n -> p (b c n)").bitcast(BF16).rearrange("p (q n) -> p q n", q=4)
        k.m_logit = sb("m_logit", [P, 2, 4 * ME])
        k.m_top = sb("m_top", [P, 2, 4 * ME])
        k.m_place = sb("m_place", [P, 2, 4, ME], U32)
        k.m_eq = sb("m_eq", [P, 2, 4, ME, 2])
        k.m_sel = sb("m_sel", [P, 2, 4 * ME])
        k.m_ex = sb("m_ex", [P, 2, 4 * ME])
        k.m_w = sb("m_w", [P, 2, 4 * ME])
        k.m_sum = sb("m_sum", [P, 2, 8])
        kb = k.kblock[:, :, :, :].rearrange("p b c n -> p b (c n)")
        k.m_h = [k.relpos[:, 0:QW], k.relpos[:, QW:2 * QW], kb[:, 0, :], kb[:, 1, :]]
        k.m_hTs = [k.probT[:, b, h * QW:(h + 1) * QW] for b in range(2) for h in range(2)]
        k.e_bias = sb("e_bias", [P, 64])
        k.sh_gate = {"L0_ffn": sb("sh_gate0", [P, P]), "L2_ffn": sb("sh_gate2", [P, 2 * P])}
        k.sh_up = {"L0_ffn": sb("sh_up0", [P, P]), "L2_ffn": sb("sh_up2", [P, 2 * P])}
        k.sh_down = {"L0_ffn": sb("sh_down0", [P, 1, D]), "L2_ffn": sb("sh_down2", [P, 2, D])}
        k.router = {"L0_ffn": sb("router0", [P, 64]), "L2_ffn": sb("router2", [P, 16])}
        k.bits = sb("bits", [P, 30], I32)
        k.r_score = sb("r_score", [P, 2, 256])
        k.r_w = sb("r_w", [P, 2, 256])
        k.r_sel = sb("r_sel", [P, 2, 256])
        k.r_sfc = sb("r_sfc", [P, 256])
        k.r_left = sb("r_left", [P, 256])
        k.r_gmax = sb("r_gmax", [P, 32, 8])
        k.r_gs = sb("r_gs", [P, 32])
        k.r_gtop = sb("r_gtop", [P, 32])
        k.r_gplace = sb("r_gplace", [P, 4, 8], U32)
        k.r_geq = sb("r_geq", [P, 4, 8, 4])
        k.r_gmask = sb("r_gmask", [P, 32])
        k.r_top = sb("r_top", [P, 32])
        k.r_sum = sb("r_sum", [P, 8])
        k.q_stats = sb("q_stats", [P, 2, 4, 6])
        k.q_meanvar = sb("q_meanvar", [P, 2, 4, 2])
        k.q_vareps = sb("q_vareps", [P, 2, 4])
        k.q_rstd = sb("q_rstd", [P, 2, 4])
        k.q_xn = k.prob[:, :, 0:QW]
        k.q_xnT = k.prob[:, :, QW:2 * QW]
        k.r_carry = sb("r_carry", [P, 1])
        k.tile_ends = sb("tile_ends", [P, TILES])
        k.zeros = sb("zeros", [P, 192])
        k.slot_tile = sb("slot_tile", [P, 128])
        k.slot_row = sb("slot_row", [P, 128], U32)
        k.slot_index = sb("slot_index", [P, 2, 4], U32)
        k.slot_within = sb("slot_within", [P, 128])
        k.slot_token = sb("slot_token", [P, 128], U32)
        k.rows = k.prob[:, :, 0:4 * P].rearrange("p b (q n) -> p b q n", q=4)
        k.row_le = sb("row_le", [P, 4, P], BF16)
        k.c_thr = sb("c_thr", [P, 2, 1])
        k.c_count = sb("c_count", [P, 8])
        k.e_gidx = sb("e_gidx", [P, 4, 1], U32)
        k.e_sidx = sb("e_sidx", [P, 2, 1], U32)
        k.e_wcol = sb("e_wcol", [P, 2, 1])
        k.g_gidx = sb("g_gidx", [P, 2, 4], U32)
        k.g_sidx = sb("g_sidx", [P, 2, 4], U32)
        k.g_wcol = sb("g_wcol", [P, 2, 4])

        def dram(name, shape):
            return nc.dram_tensor(name, shape, F32, kind="Internal").ap()
        k.x_dram = dram("x_dram", (T + P, D))
        k.cum_dram = dram("cum_dram", (64 * TILES, P))
        k.cend_dram = dram("cend_dram", (64 * TILES,))
        k.score_dram = dram("score_dram", (16, T))
        routed = {"L0_ffn": Routed("L0_ffn", 64, 1, 128, {"table": dram("table0", (T + P, D + 64))}),
                  "L2_ffn": Routed("L2_ffn", 16, 8, 256, {"table": dram("table2", (T + P, D + 16))})}
        k.rel_emb = sb("rel_emb", [P, 2, D])
        k.rel_table = sb("rel_table", [P, 2, HEADS])
        k.rel_tableT = sb("rel_tableT", [HEADS, 2 * P])
        k.rel_dram = nc.dram_tensor("rel_dram", (HEADS, 2 * P), F32, kind="Internal").ap()
        lora = sb("lora", [16, 8, D])
        ps = ctx.enter_context(nc.psum_tensor("ps", [P, 8, 512], F32))
        k.ident = k.consts[:, C_ID:C_ID + P]
        k.scores = ps[:, 0:4, :]
        k.ps_o = ps[:, 4, 0:2 * 8 * VW]
        k.ps_pT = ps[:, 4:6, :]
        k.ps_q = ps[:, 6, 0:128]
        k.ps_k = ps[:, 6, 128:256]
        k.ps_v = ps[:, 7, 256:512].rearrange("p (b d) -> p b d", b=2)
        k.ps_y = ps[:, 7, 0:128]
        k.ps_xT = ps[:, 7, 0:128]
        k.ps_oT = ps[:, 7, 128:256]

        lasting_semaphores(k, sem)
        relative_bias_semaphores(k, sem)
        run = [s for s in stages if s in ATTENTIONS]
        kinds = {"cross": CROSS, "out": OUT_BIAS - set(POST_NORM), "post": set(POST_NORM), "biased": BIASED}

        def before(kind, name):
            return sum(r in kinds[kind] for r in run[:run.index(name)])
        k.before = before

        LOADS = 8
        fronts = [s for s in stages if s in FFNS or s == "L3_ffn"]
        k.tf = lambda m: sum(s in WITH_TRANSPOSE for s in fronts[:m])

        with nc.Block() as block:
            @block.sync
            def _(sp):
                for dst, src in [(k.consts[:, :], d["consts"]), (lora[:, :, :], d["lora"]), (k.bqk[:, :, :], d["bqk"]),
                                 (k.attn_w[:, 0, :, :], d["attn_w"][:, 0, :, :]),
                                 (k.bv[:, 0, :], d["bv"][0, :].partition_broadcast(P)),
                                 (k.bo[:, 0, :], d["bo"][0, :].partition_broadcast(P))]:
                    sp.dma_start(dst, src).then_inc(k.loaded, 16)
                xs = d["x"].rearrange("(n p) c -> p n c", p=P)
                for c in range(LOADS):
                    w = TILES // LOADS
                    sp.dma_start(k.x[:, c * w * D:(c + 1) * w * D].rearrange("p (n c) -> p n c", c=D),
                                 xs[:, c * w:(c + 1) * w, :]).then_inc(k.loaded, 16)
                sp.wait_ge(k.loaded, 16 * (6 + LOADS))

            @block.gpsimd
            def _(pool):
                nc.gpsimd.memset(k.half_power[:, :], -0.5).then_inc(k.made, 1)
                nc.gpsimd.memset(k.ones[:, :], 1.0).then_inc(k.made, 1)
                nc.gpsimd.memset(k.vblock[:, :, :, :, :], 0.0).then_inc(k.made, 1)
                pool.wait_ge(k.made, 3)
                nc.gpsimd.memset(k.vblock[0:S, :, :, :, HD:HD + 1], 1.0).then_inc(k.made, 1)
                nc.gpsimd.memset(k.vblock[S:P, :, :, :, VW - 1:VW], 1.0).then_inc(k.made, 1)
                pool.wait_ge(k.made, 5)

            @block.tensor
            def _(pe):
                pe.wait_ge(k.loaded, 16 * (6 + LOADS))
                for m in range(4):
                    nc.tensor.matmul(ps[:, 0, m * P:(m + 1) * P], lora[:, m, :], lora[:, 4 + m, :], start=True,
                                     stop=True).then_inc(k.lora_psum, 1)

            @block.vector
            def _(dve):
                dve.wait_ge(k.lora_psum, 4)
                for m in range(4):
                    nc.vector.scalar_tensor_tensor(k.attn_w[:, 0, m, :], ps[:, 0, m * P:(m + 1) * P], 1.0 / 16,
                                                   k.attn_w[:, 0, m, :], ALU.mult, ALU.add).then_inc(k.lora_done, 1)
                dve.wait_ge(k.lora_done, 4)
                for a, name in enumerate(ATTENTIONS):
                    heads = k.consts[:, C_HEAD:C_HEAD + GH]
                    nc.vector.tensor_scalar(k.key_scale[:, a, :], heads, SCALES[name], None, ALU.mult).then_inc(k.lora_done, 1)
                    nc.vector.tensor_scalar(k.key_bias[:, a, :], heads, k.bqk[:, a, 1:2], SCALES[name], ALU.mult,
                                            ALU.mult).then_inc(k.lora_done, 1)
                dve.wait_ge(k.lora_done, 4 + 2 * NA)

        if "L1_attn" in stages:
            relative_bias(k, ps)
        if "L0_attn" not in stages:
            with nc.Block() as block:
                @block.sync
                def _(sp):
                    background_loads(k, sp, d, routed, stages)
        n = 0
        for stage in stages:
            m = sum(s in FFNS or s == "L3_ffn" for s in stages[:stages.index(stage)])
            if stage == "L1_ffn":
                with phase(k, bitlinear_semaphores):
                    bitlinear_weights(k, ps)
                    bitlinear_pass(k, ps, m)
            if stage in routed:
                r = routed[stage]
                with phase(k, routed_semaphores, small_experts_semaphores if stage == "L0_ffn" else large_experts_semaphores):
                    shared_pass(k, ps, m, r)
                    if stage == "L2_ffn":
                        choose_tokens(k, ps, r)
                    find_slots(k, ps, r)
                    (small_experts if stage == "L0_ffn" else large_experts)(k, ps, r)
                    reload_x(k, r)
            if stage == "L3_moe":
                with phase(k, dense_moe_semaphores):
                    dense_moe_pass(k, ps, m)
            if stage == "L3_ffn":
                prenorm_pass(k, m)
            if stage == "L1_attn":
                relative_mask(k)
            if stage in ATTENTIONS:
                with nc.Block() as block:
                    @block.sync
                    def _(sp):
                        if stage == "L0_attn":
                            background_loads(k, sp, d, routed, stages)
                        attention_loads(k, sp, stage, n)

                    @block.gpsimd
                    def _(pool):
                        attention_pool(k, pool, stage, n)

                    @block.tensor
                    def _(pe):
                        attention_pe(k, pe, stage, n)

                    @block.scalar
                    def _(act):
                        attention_act(k, act, stage, n)

                    @block.vector
                    def _(dve):
                        attention_dve(k, dve, stage, n)
                n += 1

        with nc.Block() as block:
            @block.sync
            def _(sp):
                out = d["out"].rearrange("(n p) c -> p n c", p=P)
                for c in range(LOADS):
                    w = TILES // LOADS
                    sp.dma_start(out[:, c * w:(c + 1) * w, :],
                                 k.x[:, c * w * D:(c + 1) * w * D].rearrange("p (n c) -> p n c", c=D)
                                 ).then_inc(k.stored, 16)
                sp.wait_ge(k.stored, 16 * LOADS)


def constants():
    c = np.zeros((P, C_END), np.float32)
    c[:, C_ID:C_ID + P] = np.eye(P)
    p = np.arange(P)
    for h in range(GH):
        c[:, C_HEAD + h] = (p // HD) % GH == h
    c[:, C_CAUSAL:C_CAUSAL + S] = MASKED * (np.arange(S)[None, :] > (p % S)[:, None])
    c[:, C_FUTURE:C_FUTURE + S] = LOWEST * (np.arange(S)[None, :] > (p % S)[:, None])
    c[:, C_SLOT:C_SLOT + 8] = p[:, None] + P * np.arange(8)[None, :]
    c[:, C_SLOT + 8] = T + p
    c[:, C_EIGHT:C_EIGHT + 8] = np.arange(8)
    c[:, C_CHUNK:C_CHUNK + P] = p[:, None] // 8 == p[None, :] // 8
    c[:, C_EARLIER:C_EARLIER + P] = (p[:, None] // 8 == p[None, :] // 8) & (p[:, None] < p[None, :])
    c[:, C_TOKEN0:C_TOKEN0 + 64] = TILES * np.arange(64)
    c[:, C_UPPER:C_UPPER + P] = p[:, None] <= p[None, :]
    c[:, C_UPPER + P:C_UPPER + QW] = 1.0
    return c


def lay_out(i):
    z = np.zeros((D,), np.float32)
    zz = np.zeros((D, D), np.float32)
    qkv, b3 = i["L1_attn_qkv_w"], i["L1_attn_qkv_b"]

    def rep(w, times):
        return np.repeat(w.reshape(-1, HD, *w.shape[1:]), times, axis=0).reshape(-1, *w.shape[1:])
    weights = [
        [i["L0_attn_Wq"].T, i["L0_attn_Wk"].T, i["L0_attn_Wv"].T, i["L0_attn_Wo"].T],
        [i["L0_xattn_w_q"], i["L0_xattn_w_k"], i["L0_xattn_w_v"], i["L0_xattn_w_o"]],
        [qkv[0:D].T, qkv[D:2 * D].T, qkv[2 * D:].T, i["L1_attn_proj_w"].T],
        [i["L1_xattn_Wq"].T, i["L1_xattn_Wk"].T, i["L1_xattn_Wv"].T, zz],
        [i["L2_attn_wq"].T, rep(i["L2_attn_wk"], 4).T, rep(i["L2_attn_wv"], 4).T, i["L2_attn_wo"].T],
        [i["L2_xattn_wq"].T, i["L2_xattn_wk"].T, i["L2_xattn_wv"].T, i["L2_xattn_wo"].T],
        [i["L3_attn_Wq"].T, rep(i["L3_attn_Wk"], 16).T, rep(i["L3_attn_Wv"], 16).T, i["L3_attn_Wo"].T],
        [i["L3_xattn_wq_w"].T, i["L3_xattn_wk_w"].T, i["L3_xattn_wv_w"].T, i["L3_xattn_wo_w"].T],
        [i["L3_ffn_Wq"], i["L3_ffn_Wk"], i["L3_ffn_Wv"], i["L3_ffn_Wo"]],
    ]
    bq = [z, i["L0_xattn_b_q"], b3[0:D], i["L1_xattn_bq"], z, z, i["L3_attn_bq"], i["L3_xattn_wq_b"], z]
    bk = [z, i["L0_xattn_b_k"], b3[D:2 * D], i["L1_xattn_bk"], z, z, z, i["L3_xattn_wk_b"], z]
    bv = [z, i["L0_xattn_b_v"], b3[2 * D:], i["L1_xattn_bv"], z, z, rep(i["L3_attn_bv"], 16), i["L3_xattn_wv_b"], z]
    bo = [i["L0_attn_bo"], i["L0_xattn_b_o"], i["L1_attn_proj_b"], z, z, i["L2_xattn_bo"], i["L3_attn_bo"],
          i["L3_xattn_wo_b"], z]
    return {
        "rel_rev": np.concatenate([i["L1_attn_rel_pos_emb"][::-1], np.zeros((1, D), np.float32)]),
        "bit_w": np.stack([i["L1_ffn_w_gate"].T, i["L1_ffn_w_up"].T,
                           i["L1_ffn_w_down"].T.reshape(4, P, D).transpose(1, 0, 2).reshape(P, 4 * D)]).transpose(1, 0, 2),
        "bits": np.broadcast_to((1 << np.arange(29, -1, -1)).astype(np.int32), (P, 30)),
        "e_bias": i["L0_ffn_e_bias"],
        "sh_gate_L0_ffn": i["L0_ffn_shared_gate"].T,
        "sh_up_L0_ffn": i["L0_ffn_shared_up"].T,
        "sh_down_L0_ffn": i["L0_ffn_shared_down"].T.reshape(1, P, D).transpose(1, 0, 2),
        "router_L0_ffn": i["L0_ffn_gate_weight"].T,
        "e_w13": np.concatenate([i["L0_ffn_w1"], i["L0_ffn_w3"]], axis=1).transpose(0, 2, 1).reshape(64 * D, 128),
        "e_w2": i["L0_ffn_w2"].transpose(0, 2, 1).reshape(64 * 64, D),
        "sh_gate_L2_ffn": i["L2_ffn_sh_gate_w"].T,
        "sh_up_L2_ffn": i["L2_ffn_sh_up_w"].T,
        "sh_down_L2_ffn": i["L2_ffn_sh_down_w"].T.reshape(2, P, D).transpose(1, 0, 2),
        "router_L2_ffn": i["L2_ffn_gate_w"].T,
        "g_w": np.concatenate([
            i["L2_ffn_gw"].transpose(0, 2, 1), i["L2_ffn_up_w"].transpose(0, 2, 1),
            i["L2_ffn_down_w"].transpose(0, 2, 1).reshape(16, 4, P, D).transpose(0, 2, 1, 3).reshape(16, P, 4 * D),
            i["L2_ffn_gb"].reshape(16, 4, P).transpose(0, 2, 1), i["L2_ffn_up_b"].reshape(16, 4, P).transpose(0, 2, 1),
            np.broadcast_to(i["L2_ffn_down_b"][:, None, :], (16, P, D))], axis=2).reshape(16 * P, -1),
        "moe_gate": i["L3_ffn_Wg"],
        "moe_w1": i["L3_ffn_W1"].transpose(1, 0, 2).reshape(D, ME * MH),
        "moe_w2": i["L3_ffn_W2"].reshape(4, P, D).transpose(1, 0, 2),
        "x": i["x"].reshape(T, D),
        "ctxT": i["ctx_1024"].reshape(T, D).T,
        "consts": constants(),
        "attn_w": np.stack([np.stack(w) for w in weights]).transpose(2, 0, 1, 3),
        "bqk": np.stack([np.stack(bq), np.stack(bk)]).transpose(2, 1, 0),
        "post_gain": np.stack([i["L1_xattn_gamma"], i["L1_xattn_beta"], i["L3_xattn_ln_g"], i["L3_xattn_ln_b"]]),
        "norm_cols": np.stack([i["L3_ffn_g1"], i["L3_ffn_b1"], i["L3_ffn_g2"], i["L3_ffn_b2"]]).T,
        "mask": i["mask_Bx1xSxS2_bf0"].reshape(T, S).view(np.uint32),
        "bv": np.stack(bv),
        "bo": np.stack(bo),
        "lora": np.stack([i[f"L0_attn_A{m}"] for m in "qkvo"] + [i[f"L0_attn_B{m}"].T for m in "qkvo"]).transpose(1, 0, 2),
    }


FFNS = ["L0_ffn", "L1_ffn", "L2_ffn", "L3_moe"]
WITH_TRANSPOSE = {"L0_ffn", "L2_ffn", "L3_moe"}
STAGES = ["L0_attn", "L0_xattn", "L0_ffn", "L1_attn", "L1_xattn", "L1_ffn", "L2_attn", "L2_xattn", "L2_ffn",
          "L3_attn", "L3_xattn", "L3_ffn", "L3_moe"]


def kernel(**inputs):
    import concourse.bacc as bacc
    from concourse.bass_utils import run_bass_kernel_spmd

    nc = bacc.Bacc("TRN2", target_bir_lowering=False, num_devices=1)
    given = {n: np.ascontiguousarray(a) for n, a in lay_out({n: np.asarray(a) for n, a in inputs.items()}).items()}
    d = {n: nc.dram_tensor(f"in_{n}", a.shape, mybir.dt.from_np(a.dtype), kind="ExternalInput").ap()
         for n, a in given.items()}
    d["out"] = nc.dram_tensor("out_x", (T, D), F32, kind="ExternalOutput").ap()
    build(nc, d, STAGES)
    got = run_bass_kernel_spmd(nc, [{f"in_{n}": a for n, a in given.items()}], core_ids=[0])
    return got.results[0]["out_x"].reshape(B, S, D)
```
